# Optimizing a Trainium2 kernel written in Bass

```python
import numpy as np
import jax
import jax.numpy as jnp

def _softmax(x, axis=-1):
    return jax.nn.softmax(x, axis=axis)

def _gelu(x):
    return jax.nn.gelu(x, approximate=True)

def _silu(x):
    return jax.nn.silu(x)

def _sigmoid(x):
    return jax.nn.sigmoid(x)

def _layernorm(x, axis=-1, eps=1e-05):
    m = jnp.mean(x, axis=axis, keepdims=True)
    v = jnp.var(x, axis=axis, keepdims=True)
    return (x - m) / jnp.sqrt(v + eps)

def _scatter_add(tgt, idx, src, axis=0):
    return tgt.at[idx].add(src)

def _segment_sum(src, seg, n):
    return jax.ops.segment_sum(src, seg, n)
kernel_name = 'mk_macaron_d2_jaxref_r8_5e8ad3'

def setup_inputs(seed: int=0):
    np.random.seed(seed)
    _w = jnp.asarray

    def _L0_attn_setup():
        import jax, jax.numpy as jnp
        import numpy as np
        B, T, D = (2, 256, 256)
        H, LAT, RD = (16, 64, 64)
        HD = D // H

        def _rope_tables(rd, max_t, theta=10000.0):
            freqs = 1.0 / theta ** (np.arange(0, rd, 2, dtype=np.float32) / rd)
            t = np.arange(max_t, dtype=np.float32)
            ang = np.outer(t, freqs)
            cos = np.tile(np.cos(ang), (1, 2))
            sin = np.tile(np.sin(ang), (1, 2))
            return (jnp.asarray(cos), jnp.asarray(sin))

        def _rotate_half(x):
            d = x.shape[-1] // 2
            return jnp.concatenate([-x[..., d:], x[..., :d]], axis=-1)

        def _apply_rope(x, cos, sin):
            t = x.shape[2]
            return x * cos[:t][None, None] + _rotate_half(x) * sin[:t][None, None]
        key = jax.random.key(seed)
        ks = jax.random.split(key, 9)
        s = 0.02
        return {'x': jax.random.normal(ks[0], (B, T, D), jnp.float32), 'Wqd': jax.random.normal(ks[1], (D, LAT), jnp.float32) * s, 'Wqu': jax.random.normal(ks[2], (LAT, D), jnp.float32) * s, 'Wqr': jax.random.normal(ks[3], (LAT, H * RD), jnp.float32) * s, 'Wkvd': jax.random.normal(ks[4], (D, LAT), jnp.float32) * s, 'Wku': jax.random.normal(ks[5], (LAT, D), jnp.float32) * s, 'Wvu': jax.random.normal(ks[6], (LAT, D), jnp.float32) * s, 'Wkr': jax.random.normal(ks[7], (D, RD), jnp.float32) * s, 'Wo': jax.random.normal(ks[8], (D, D), jnp.float32) * s}
    _L0_attn_in = _L0_attn_setup()

    def _L0_ffn_setup():
        import jax, jax.numpy as jnp
        import numpy as np
        NUM_EXPERTS = 8
        TOP_K = 2
        key = jax.random.key(seed)
        ks = jax.random.split(key, 7)
        B, S, H, I, E = (4, 256, 256, 256, NUM_EXPERTS)
        sc = 0.02
        return {'hidden_states': jax.random.normal(ks[0], (B, S, H), dtype=jnp.float32), 'gate_w': jax.random.normal(ks[1], (E, H), dtype=jnp.float32) * sc, 'gate_b': jax.random.normal(ks[2], (E,), dtype=jnp.float32) * sc, 'w1': jax.random.normal(ks[3], (E, 2 * I, H), dtype=jnp.float32) * sc, 'b1': jax.random.normal(ks[4], (E, 2 * I), dtype=jnp.float32) * sc, 'w2': jax.random.normal(ks[5], (E, H, I), dtype=jnp.float32) * sc, 'b2': jax.random.normal(ks[6], (E, H), dtype=jnp.float32) * sc}
    _L0_ffn_in = _L0_ffn_setup()

    def _L1_attn_setup():
        import jax, jax.numpy as jnp
        import numpy as np
        TOPK = 32
        NEG = -1e+30

        def hadamard(x):
            d = x.shape[-1]
            shape = x.shape
            x = x.reshape(-1, d)
            h = 1
            while h < d:
                x = x.reshape(-1, d // (2 * h), 2, h)
                a, b = (x[:, :, 0, :], x[:, :, 1, :])
                x = jnp.stack([a + b, a - b], axis=2).reshape(-1, d)
                h *= 2
            return (x * d ** (-0.5)).reshape(shape)
        key = jax.random.key(seed)
        ks = jax.random.split(key, 8)
        D, S, B = (256, 256, 1)
        Hi, Di, H, hd = (16, 128, 16, 128)
        w = 0.02
        return {'x': jax.random.normal(ks[0], (B, S, D), jnp.float32), 'wq_idx': jax.random.normal(ks[1], (D, Hi * Di), jnp.float32) * w, 'wk_idx': jax.random.normal(ks[2], (D, Di), jnp.float32) * w, 'w_iw': jax.random.normal(ks[3], (D, Hi), jnp.float32) * w, 'wq': jax.random.normal(ks[4], (D, H * hd), jnp.float32) * w, 'wk': jax.random.normal(ks[5], (D, hd), jnp.float32) * w, 'wv': jax.random.normal(ks[6], (D, hd), jnp.float32) * w, 'wo': jax.random.normal(ks[7], (H * hd, D), jnp.float32) * w}
    _L1_attn_in = _L1_attn_setup()

    def _L1_ffn_setup():
        import jax, jax.numpy as jnp
        import numpy as np
        B, S, D, H = (4, 256, 256, 1024)

        def fwht(x):
            orig_shape = x.shape
            n = orig_shape[-1]
            x = x.reshape(-1, n)
            h = 1
            while h < n:
                xb = x.reshape(-1, n // (2 * h), 2, h)
                a = xb[:, :, 0, :]
                b = xb[:, :, 1, :]
                x = jnp.stack([a + b, a - b], axis=2).reshape(-1, n)
                h *= 2
            scale = jnp.asarray(1.0 / np.sqrt(n), dtype=x.dtype)
            return (x * scale).reshape(orig_shape)
        key = jax.random.key(seed)
        kx, k1, k2, k3 = jax.random.split(key, 4)
        x = jax.random.normal(kx, (B, S, D), dtype=jnp.float32)
        W1 = jax.random.normal(k1, (H, D), dtype=jnp.float32) * (1.0 / np.sqrt(D))
        W2 = jax.random.normal(k2, (D, H), dtype=jnp.float32) * (1.0 / np.sqrt(H))
        W3 = jax.random.normal(k3, (H, D), dtype=jnp.float32) * (1.0 / np.sqrt(D))
        return {'x': x, 'W1': W1, 'W2': W2, 'W3': W3}
    _L1_ffn_in = _L1_ffn_setup()
    _d = {'L0_attn_x': _L0_attn_in['x'], 'L0_attn_Wqd': _L0_attn_in['Wqd'], 'L0_attn_Wqu': _L0_attn_in['Wqu'], 'L0_attn_Wqr': _L0_attn_in['Wqr'], 'L0_attn_Wkvd': _L0_attn_in['Wkvd'], 'L0_attn_Wku': _L0_attn_in['Wku'], 'L0_attn_Wvu': _L0_attn_in['Wvu'], 'L0_attn_Wkr': _L0_attn_in['Wkr'], 'L0_attn_Wo': _L0_attn_in['Wo'], 'L0_ffn_gate_w': _L0_ffn_in['gate_w'], 'L0_ffn_gate_b': _L0_ffn_in['gate_b'], 'L0_ffn_w1': _L0_ffn_in['w1'], 'L0_ffn_b1': _L0_ffn_in['b1'], 'L0_ffn_w2': _L0_ffn_in['w2'], 'L0_ffn_b2': _L0_ffn_in['b2'], 'L1_attn_wq_idx': _L1_attn_in['wq_idx'], 'L1_attn_wk_idx': _L1_attn_in['wk_idx'], 'L1_attn_w_iw': _L1_attn_in['w_iw'], 'L1_attn_wq': _L1_attn_in['wq'], 'L1_attn_wk': _L1_attn_in['wk'], 'L1_attn_wv': _L1_attn_in['wv'], 'L1_attn_wo': _L1_attn_in['wo'], 'L1_ffn_W1': _L1_ffn_in['W1'], 'L1_ffn_W2': _L1_ffn_in['W2'], 'L1_ffn_W3': _L1_ffn_in['W3']}
    _x0 = _d['L0_attn_x']
    _d['L0_attn_x'] = jax.random.normal(jax.random.fold_in(jax.random.key(seed), 1), (1, 2048, 256), dtype=_x0.dtype)
    del _x0
    return _d

def reference(L0_attn_x, L0_attn_Wqd, L0_attn_Wqu, L0_attn_Wqr, L0_attn_Wkvd, L0_attn_Wku, L0_attn_Wvu, L0_attn_Wkr, L0_attn_Wo, L0_ffn_gate_w, L0_ffn_gate_b, L0_ffn_w1, L0_ffn_b1, L0_ffn_w2, L0_ffn_b2, L1_attn_wq_idx, L1_attn_wk_idx, L1_attn_w_iw, L1_attn_wq, L1_attn_wk, L1_attn_wv, L1_attn_wo, L1_ffn_W1, L1_ffn_W2, L1_ffn_W3):

    def _L0_attn_ref(x, Wqd, Wqu, Wqr, Wkvd, Wku, Wvu, Wkr, Wo):
        import jax, jax.numpy as jnp
        import numpy as np
        B, T, D = (2, 256, 256)
        H, LAT, RD = (16, 64, 64)
        HD = D // H

        def _rope_tables(rd, max_t, theta=10000.0):
            freqs = 1.0 / theta ** (np.arange(0, rd, 2, dtype=np.float32) / rd)
            t = np.arange(max_t, dtype=np.float32)
            ang = np.outer(t, freqs)
            cos = np.tile(np.cos(ang), (1, 2))
            sin = np.tile(np.sin(ang), (1, 2))
            return (jnp.asarray(cos), jnp.asarray(sin))

        def _rotate_half(x):
            d = x.shape[-1] // 2
            return jnp.concatenate([-x[..., d:], x[..., :d]], axis=-1)

        def _apply_rope(x, cos, sin):
            t = x.shape[2]
            return x * cos[:t][None, None] + _rotate_half(x) * sin[:t][None, None]
        b, t, d = x.shape
        cos, sin = _rope_tables(RD, t)
        ql = x @ Wqd
        q = (ql @ Wqu).reshape(b, t, H, HD).transpose(0, 2, 1, 3)
        qr = (ql @ Wqr).reshape(b, t, H, RD).transpose(0, 2, 1, 3)
        qr = _apply_rope(qr, cos, sin)
        ckv = x @ Wkvd
        k = (ckv @ Wku).reshape(b, t, H, HD).transpose(0, 2, 1, 3)
        v = (ckv @ Wvu).reshape(b, t, H, HD).transpose(0, 2, 1, 3)
        kr = _apply_rope((x @ Wkr)[:, None], cos, sin)[:, 0]
        scale = 1.0 / jnp.sqrt(jnp.float32(HD + RD))
        scores = (jnp.einsum('bhtd,bhsd->bhts', q, k) + jnp.einsum('bhtd,bsd->bhts', qr, kr)) * scale
        causal = jnp.tril(jnp.ones((t, t), dtype=bool))
        scores = jnp.where(causal[None, None], scores, jnp.float32(-jnp.inf))
        attn = jax.nn.softmax(scores, axis=-1)
        out = jnp.einsum('bhts,bhsd->bhtd', attn, v)
        out = out.transpose(0, 2, 1, 3).reshape(b, t, d)
        return out @ Wo

    def _L0_ffn_ref(hidden_states, gate_w, gate_b, w1, b1, w2, b2):
        import jax, jax.numpy as jnp
        import numpy as np
        NUM_EXPERTS = 8
        TOP_K = 2
        B, S, H = hidden_states.shape
        x = hidden_states.reshape(-1, H)
        logits = x @ gate_w.T + gate_b
        top_vals, top_idx = jax.lax.top_k(logits, TOP_K)
        routing = jax.nn.softmax(top_vals.astype(jnp.float32), axis=-1).astype(x.dtype)
        out = jnp.zeros_like(x)
        E = w1.shape[0]
        for e in range(E):
            h = x @ w1[e].T + b1[e]
            x_glu = h[:, 0::2]
            x_lin = h[:, 1::2]
            y = x_glu * jax.nn.sigmoid(1.702 * x_glu) * (x_lin + 1.0)
            ye = y @ w2[e].T + b2[e]
            we = jnp.sum(routing * (top_idx == e), axis=-1)
            out = out + ye * we[:, None]
        return out.reshape(B, S, H)

    def _L1_attn_ref(x, wq_idx, wk_idx, w_iw, wq, wk, wv, wo):
        import jax, jax.numpy as jnp
        import numpy as np
        TOPK = 32
        NEG = -1e+30

        def hadamard(x):
            d = x.shape[-1]
            shape = x.shape
            x = x.reshape(-1, d)
            h = 1
            while h < d:
                x = x.reshape(-1, d // (2 * h), 2, h)
                a, b = (x[:, :, 0, :], x[:, :, 1, :])
                x = jnp.stack([a + b, a - b], axis=2).reshape(-1, d)
                h *= 2
            return (x * d ** (-0.5)).reshape(shape)
        B, S, D = x.shape
        Di = wk_idx.shape[-1]
        Hi = w_iw.shape[-1]
        hd = wk.shape[-1]
        H = wq.shape[-1] // hd
        qi = hadamard((x @ wq_idx).reshape(B, S, Hi, Di))
        ki = hadamard(x @ wk_idx)
        iw = x @ w_iw
        logits = jax.nn.relu(jnp.einsum('bthd,bsd->bhts', qi, ki))
        I = jnp.einsum('bth,bhts->bts', iw, logits)
        t = jnp.arange(S)
        causal = t[None, :, None] >= t[None, None, :]
        I = jnp.where(causal, I, NEG)
        vals, idx = jax.lax.top_k(I, TOPK)
        valid = vals > NEG / 2
        q = (x @ wq).reshape(B, S, H, hd)
        k = x @ wk
        v = x @ wv
        gather = jax.vmap(lambda kk, ii: kk[ii])
        k_sel, v_sel = (gather(k, idx), gather(v, idx))
        scores = jnp.einsum('bthd,btkd->bhtk', q, k_sel) * hd ** (-0.5)
        scores = jnp.where(valid[:, None], scores, NEG)
        p = jax.nn.softmax(scores, axis=-1)
        o = jnp.einsum('bhtk,btkd->bthd', p, v_sel)
        return o.reshape(B, S, H * hd) @ wo

    def _L1_ffn_ref(x, W1, W2, W3):
        import jax, jax.numpy as jnp
        import numpy as np
        B, S, D, H = (4, 256, 256, 1024)

        def fwht(x):
            orig_shape = x.shape
            n = orig_shape[-1]
            x = x.reshape(-1, n)
            h = 1
            while h < n:
                xb = x.reshape(-1, n // (2 * h), 2, h)
                a = xb[:, :, 0, :]
                b = xb[:, :, 1, :]
                x = jnp.stack([a + b, a - b], axis=2).reshape(-1, n)
                h *= 2
            scale = jnp.asarray(1.0 / np.sqrt(n), dtype=x.dtype)
            return (x * scale).reshape(orig_shape)
        up_gate = jnp.einsum('bsd,hd->bsh', x, W1)
        up_lin = jnp.einsum('bsd,hd->bsh', x, W3)
        hidden = jax.nn.silu(up_gate) * up_lin
        hidden = fwht(hidden)
        out = jnp.einsum('bsh,dh->bsd', hidden, W2)
        return out
    x = L0_attn_x
    x = x + 0.5 * _L0_ffn_ref(_layernorm(x, axis=-1), L0_ffn_gate_w, L0_ffn_gate_b, L0_ffn_w1, L0_ffn_b1, L0_ffn_w2, L0_ffn_b2)
    x = x + _L0_attn_ref(_layernorm(x, axis=-1), L0_attn_Wqd, L0_attn_Wqu, L0_attn_Wqr, L0_attn_Wkvd, L0_attn_Wku, L0_attn_Wvu, L0_attn_Wkr, L0_attn_Wo)
    x = x + 0.5 * _L0_ffn_ref(_layernorm(x, axis=-1), L0_ffn_gate_w, L0_ffn_gate_b, L0_ffn_w1, L0_ffn_b1, L0_ffn_w2, L0_ffn_b2)
    x = x + 0.5 * _L1_ffn_ref(_layernorm(x, axis=-1), L1_ffn_W1, L1_ffn_W2, L1_ffn_W3)
    x = x + _L1_attn_ref(_layernorm(x, axis=-1), L1_attn_wq_idx, L1_attn_wk_idx, L1_attn_w_iw, L1_attn_wq, L1_attn_wk, L1_attn_wv, L1_attn_wo)
    x = x + 0.5 * _L1_ffn_ref(_layernorm(x, axis=-1), L1_ffn_W1, L1_ffn_W2, L1_ffn_W3)
    return x

_drawn_inputs = setup_inputs


def setup_inputs(seed=0):
    import zlib

    import numpy as np

    out = dict(_drawn_inputs(seed))
    spreads = {}
    factors = {'L0_attn_Wqd': 8.0,
     'L0_attn_Wqu': 8.0,
     'L0_attn_Wqr': 8.0,
     'L0_attn_Wkvd': 8.0,
     'L0_attn_Wku': 8.0,
     'L0_attn_Wvu': 8.0,
     'L0_attn_Wkr': 8.0,
     'L0_attn_Wo': 8.0,
     'L0_ffn_gate_b': 5.381,
     'L0_ffn_b1': 8.0,
     'L0_ffn_b2': 3.011,
     'L1_attn_wq': 8.0,
     'L1_attn_wk': 8.0}
    for name, (base, spread) in spreads.items():
        noise = np.random.default_rng([zlib.crc32(name.encode()), seed]).standard_normal(out[name].shape)
        drawn = base * np.exp(spread * noise) if base else spread * noise
        out[name] = jnp.asarray(drawn.astype(out[name].dtype))
    for name, factor in factors.items():
        out[name] = (out[name] * factor).astype(out[name].dtype)
    return out
```

```python
from contextlib import ExitStack

import concourse.bass as bass
from concourse import mybir
import numpy as np

F32 = mybir.dt.float32
F32R = mybir.dt.float32r
U32 = mybir.dt.uint32
ALU = mybir.AluOpType
ACT = mybir.ActivationFunctionType
AX_X = mybir.AxisListType.X

P = 128
EPS = 1e-5



def met(value):
    return max(value, 0) if isinstance(value, int) else value


def ds(start, size):
    if isinstance(start, int):
        return slice(start, start + size)
    return bass.ds(start, size)


def product(pe, out, lhs, rhs, start, stop):
    pe.matmul(out, lhs[0], rhs[0], start=start, stop=False)
    pe.matmul(out, lhs[0], rhs[1], start=False, stop=False)
    return pe.matmul(out, lhs[1], rhs[0], start=False, stop=stop)


def build(nc, a, out, stages=("moe0", "attn0", "moe1", "ffn0", "index1", "select1", "ffn1")):
    T, D = a["x"].shape
    TILES = T // P
    KD = D // P
    CH = 512
    NCH = T // CH
    CT = CH // P

    LNC, LNF, LNA = {}, {}, {}

    x_dram = a["x"].rearrange("(i p) d -> p i d", p=P)
    out_dram = out.rearrange("(i p) d -> p i d", p=P)

    ctx = ExitStack()
    with ctx:
        sem_names = {}

        def sem(name):
            if name not in sem_names:
                sem_names[name] = ctx.enter_context(nc.semaphore(name))
            return sem_names[name]

        def sb(name, shape, dt, c=None):
            return (c or ctx).enter_context(nc.sbuf_tensor(name, shape, dt))

        ps = ctx.enter_context(nc.psum_tensor("ps", [P, 8, CH], F32))

        X = sb("X", [P, TILES, D], F32)
        XTh = sb("XTh", [P, KD, T], F32R)
        XTl = sb("XTl", [P, KD, T], F32R)
        ident = sb("ident", [P, P], F32)
        xn = sb("xn", [P, CT, D], F32)
        stats = sb("stats", [P, CT, 6], F32)
        mv = sb("mv", [P, CT, 2], F32)
        rstd = sb("rstd", [P, CT], F32)
        veps = sb("veps", [P, CT], F32)
        mhalf = sb("mhalf", [P, CT], F32)
        ln_ve = sem("ln_ve")
        TOPK_STEPS = 11
        idxT = xn[:, 0:2, :].rearrange("p a d -> p (a d)").bitcast(U32).rearrange("p (t g) -> p t g", g=P // 4)
        ln_stats, ln_mv, ln_rs, ln_xn = sem("ln_stats"), sem("ln_mv"), sem("ln_rs"), sem("ln_xn")
        ln_tr, ln_hi, ln_lo = sem("ln_tr"), sem("ln_hi"), sem("ln_lo")
        x_in, x_out = sem("x_in"), sem("x_out")
        stage_done = sem("stage_done")
        LN_BANK = 0

        def ln_vector(v, n, c):
            q = NCH * n + c
            for r in range(CT):
                i = v.bn_stats(stats[:, r, :], X[:, ds(CT * c + r, 1), :])
            i.then_inc(ln_stats, 1)
            v.wait_ge(ln_stats, q + 1)
            v.nop(nofuse=True)
            for r in range(CT):
                i = v.bn_aggr(mv[:, r, :], stats[:, r, :])
            i.then_inc(ln_mv, 1)
            v.wait_ge(ln_rs, q + 1)
            v.wait_ge(ln_tr, met(KD * q))
            for r in range(CT):
                i = v.tensor_scalar(xn[:, r, :], X[:, ds(CT * c + r, 1), :].rearrange("p a d -> p (a d)"),
                                    mv[:, r, 0:1], rstd[:, r:r + 1], ALU.subtract, ALU.mult)
            i.then_inc(ln_xn, 1)

        def ln_gpsimd(g, n, c):
            q = NCH * n + c
            g.wait_ge(ln_mv, q + 1)
            g.nop(nofuse=True)
            g.tensor_scalar(veps[:], mv[:, :, 1], EPS, None, ALU.add).then_inc(ln_ve, 1)
            g.wait_ge(ln_ve, q + 1)
            g.tensor_tensor(rstd[:], veps[:], mhalf[:], ALU.pow).then_inc(ln_rs, 1)

        def ln_split(v, n, c):
            q = NCH * n + c
            for k in range(KD):
                v.wait_ge(ln_hi, KD * q + k + 1)
                dst = XTl[:, k, ds(CH * c, CH)]
                v.tensor_tensor(dst, ps[:, LN_BANK + k, :], XTh[:, k, ds(CH * c, CH)].bitcast(F32),
                                ALU.subtract).then_inc(ln_lo, 1)

        def ln_tensor(pe, n, c):
            q = NCH * n + c
            pe.wait_ge(ln_xn, q + 1)
            pe.wait_ge(ln_lo, met(KD * q))
            for k in range(KD):
                for r in range(CT):
                    i = pe.transpose(ps[:, LN_BANK + k, r * P:(r + 1) * P], xn[:, r, k * P:(k + 1) * P], ident[:])
                i.then_inc(ln_tr, 1)

        def ln_scalar(s, n, c):
            q = NCH * n + c
            for k in range(KD):
                s.wait_ge(ln_tr, KD * q + k + 1)
                s.copy(XTh[:, k, ds(CH * c, CH)], ps[:, LN_BANK + k, :]).then_inc(ln_hi, 1)

        def xt(k, c):
            return XTh[:, k, ds(CH * c, CH)], XTl[:, k, ds(CH * c, CH)]

        E = a["b2"].shape[0]
        I = a["w2"].shape[2] * 0 + 256
        JI = I // P
        UNITS = E * JI
        moe_ctx = ExitStack()
        w1raw = sb("w1raw", [P, 2, KD, 2 * I], F32, moe_ctx)
        w2raw = sb("w2raw", [P, 2, JI, D], F32, moe_ctx)
        w1h = sb("w1h", [P, E, KD, 2 * I], F32R, moe_ctx)
        w1l = sb("w1l", [P, E, KD, 2 * I], F32R, moe_ctx)
        w2h = sb("w2h", [P, E, JI, D], F32R, moe_ctx)
        w2l = sb("w2l", [P, E, JI, D], F32R, moe_ctx)
        b1 = sb("b1", [P, E, 2 * JI], F32, moe_ctx)
        b1s = sb("b1s", [P, E, 2 * JI], F32, moe_ctx)
        b1p = sb("b1p", [P, E, 2 * JI], F32, moe_ctx)
        b2 = sb("b2", [E, D], F32, moe_ctx)
        gwraw = sb("gwraw", [P, KD, E], F32, moe_ctx)
        gwh = sb("gwh", [P, KD, E], F32R, moe_ctx)
        gwl = sb("gwl", [P, KD, E], F32R, moe_ctx)
        gb = sb("gb", [E, 1], F32, moe_ctx)
        lgT = sb("lgT", [E, CH], F32, moe_ctx)
        top = sb("top", [P, CT, 8], F32, moe_ctx)
        topi = sb("topi", [P, CT, 8], U32, moe_ctx)
        topf = sb("topf", [P, CT, 8], F32, moe_ctx)
        gap = sb("gap", [P, CT, 2], F32, moe_ctx)
        gate = sb("gate", [P, CT, 2], F32, moe_ctx)
        pick = sb("pick", [P, CT, 2, E], F32, moe_ctx)
        we = sb("we", [P, CT, E], F32, moe_ctx)
        weT = sb("weT", [E, CH], F32, moe_ctx)
        weTc = sb("weTc", [E, CH], F32, moe_ctx)
        iota_e = sb("iota_e", [P, E], F32, moe_ctx)
        WR = 4
        web = sb("web", [P, WR, CH], F32, moe_ctx)
        sig = sb("sig", [P, 2, CH], F32, moe_ctx)
        gt = sb("gt", [P, 2, CH], F32, moe_ctx)
        lt = sb("lt", [P, 2, CH], F32, moe_ctx)
        y = sb("y", [P, 2, CH], F32, moe_ctx)
        yh = sb("yh", [P, 3, CH], F32R, moe_ctx)
        yl = sb("yl", [P, 3, CH], F32R, moe_ctx)
        moe_ctx.close()
        w1_dram, w2_dram = a["w1"], a["w2"]
        we_scratch = [a["we_scratch0"], a["we_scratch1"]]
        m_w, m_wh, m_wl, m_b, m_bs = [sem("m_w0"), sem("m_w1")], sem("m_wh"), sem("m_wl"), sem("m_b"), sem("m_bs")
        g_lg, g_lgs, g_tr, g_top, g_topi, g_gap, g_sig, g_pk, g_pg, g_we, g_weT, g_weTs, g_st = (
            sem(n) for n in "g_lg g_lgs g_tr g_top g_topi g_gap g_sig g_pk g_pg g_we g_weT g_weTs g_st".split())
        m_wtc, m_g, m_l, m_sig, m_gt, m_lt, m_y, m_yh, m_yl, m_dn, m_x = (
            sem(n) for n in "m_wtc m_g m_l m_sig m_gt m_lt m_y m_yh m_yl m_dn m_x".split())
        m_web = [sem(f"m_web{k}") for k in range(WR)]
        O_BANK, GL_BANK = 2, 4

        def o_tile(r):
            return ps[:, O_BANK + r // 2, (r % 2) * D:(r % 2 + 1) * D]

        def moe_sync(sp, n):
            sp.dma_start(b1[:], a["b1"]).then_inc(m_b, 16)
            sp.dma_start(b2[:], a["b2"]).then_inc(m_b, 16)
            sp.dma_start(gwraw[:], a["gate_w"]).then_inc(m_b, 16)
            sp.dma_start(gb[:], a["gate_b"]).then_inc(m_b, 16)
            sp.dma_start(iota_e[:], a["iota_e"]).then_inc(m_b, 16)
            for e in range(E):
                if e >= 2:
                    sp.wait_ge(m_wl, met(E * n + e - 1))
                sp.dma_start(w1raw[:, e % 2], w1_dram[:, e]).then_inc(m_w[e % 2], 16)
                sp.dma_start(w2raw[:, e % 2], w2_dram[:, e]).then_inc(m_w[e % 2], 16)
                if e == 1:
                    with sp.Fori(0, NCH) as c:
                        sp.wait_ge(g_weTs, NCH * n + c + 1)
                        sp.dma_start(we_scratch[n][:, ds(CH * c, CH)], weT[:]).then_inc(g_st, 16)

            def chunk(c):
                q = NCH * n + c
                for e in range(E):
                    sp.wait_ge(m_y, met(UNITS * q + JI * (e - WR + 1)))
                    sp.dma_start(web[:, e % WR, :], we_scratch[n][e, ds(CH * c, CH)].partition_broadcast(P)).then_inc(m_web[e % WR], 16)
                sp.wait_ge(m_dn, met(UNITS * q))
                sp.dma_start(weTc[:], we_scratch[n][:, ds(CH * c, CH)]).then_inc(m_wtc, 16)

            sp.wait_ge(g_st, 16 * NCH * (n + 1))
            chunk(0)
            with sp.Fori(1, NCH) as c:
                chunk(c)

        def moe_scalar(s, n):
            s.wait_ge(m_b, 80 * (n + 1))
            s.copy(gwh[:], gwraw[:]).then_inc(m_bs, 1)
            s.wait_ge(m_b, 80 * (n + 1))
            s.mul(b1s[:], b1[:], 1.702).then_inc(m_bs, 1)
            with s.Fori(0, NCH) as c:
                ln_scalar(s, LNC[n], c)
                gate_scalar(s, n, c)
            for e in range(E):
                s.wait_ge(m_w[e % 2], 32 * (E // 2 * n + e // 2 + 1))
                s.copy(w1h[:, e], w1raw[:, e % 2])
                s.copy(w2h[:, e], w2raw[:, e % 2]).then_inc(m_wh, 1)

            def sigmoid(q, u):
                U = UNITS * q + u
                e, j = u // JI, u % JI
                s.wait_ge(m_g, U + 1)
                s.wait_ge(m_gt, met(U - 1))
                s.activation(sig[:, u % 2, :], ps[:, GL_BANK + 2 * (u % 2), :], ACT.Sigmoid,
                             bias=b1s[:, e, j:j + 1], scale=1.702).then_inc(m_sig, 1)

            def high(q, u, b):
                U = UNITS * q + u
                s.wait_ge(m_y, U + 1)
                s.wait_ge(m_dn, met(U - 2))
                s.copy(yh[:, b, :], y[:, u % 2, :]).then_inc(m_yh, 1)

            def chunk(c):
                q = NCH * n + c
                for u in range(UNITS):
                    sigmoid(q, u)
                    if u >= 1:
                        high(q, u - 1, (u - 1) % 3)
                high(q, UNITS - 1, (UNITS - 1) % 3)

            chunk(0)
            with s.Fori(1, NCH) as c:
                chunk(c)

        def gate_tensor(pe, n, c):
            q = NCH * n + c
            if isinstance(c, int) is False or True:
                pe.wait_ge(m_bs, 3 * (n + 1))
            pe.wait_ge(ln_lo, KD * (NCH * LNC[n] + c + 1))
            pe.wait_ge(g_weTs, met(q))
            for k in range(KD):
                i = product(pe, ps[0:E, 2, :], (gwh[:, k, :], gwl[:, k, :]), xt(k, c), k == 0, k == KD - 1)
            i.then_inc(g_lg, 1)
            pe.wait_ge(g_lgs, q + 1)
            pe.nop(nofuse=True)
            for r in range(CT):
                i = pe.transpose(ps[:, 3, r * E:(r + 1) * E], lgT[:, r * P:(r + 1) * P], ident[0:E, 0:E])
            i.then_inc(g_tr, 1)
            pe.wait_ge(g_we, q + 1)
            for r in range(CT):
                i = pe.transpose(ps[0:E, 4, r * P:(r + 1) * P], we[:, r, :], ident[:])
            i.then_inc(g_weT, 1)

        def gate_scalar(s, n, c):
            q = NCH * n + c
            s.wait_ge(g_lg, q + 1)
            s.activation(lgT[:], ps[0:E, 2, :], ACT.Identity, bias=gb[:]).then_inc(g_lgs, 1)
            s.wait_ge(g_gap, q + 1)
            s.activation(gate[:], gap[:], ACT.Sigmoid).then_inc(g_sig, 1)
            s.wait_ge(g_weT, q + 1)
            if True:
                s.wait_ge(g_st, met(16 * q))
            s.copy(weT[:], ps[0:E, 4, :]).then_inc(g_weTs, 1)

        def gate_vector(v, n, c):
            q = NCH * n + c
            lg = ps[:, 3, 0:CT * E].rearrange("p (r e) -> p r e", e=E)
            v.wait_ge(g_tr, q + 1)
            v.nop(nofuse=True)
            for r in range(CT):
                i = v.max(top[:, r, :], lg[:, r, :])
            i.then_inc(g_top, 1)
            v.wait_ge(g_top, q + 1)
            v.nop(nofuse=True)
            for r in range(CT):
                i = v.max_index(topi[:, r, :], top[:, r, :], lg[:, r, :])
            v.tensor_tensor(gap[:, :, 0], top[:, :, 0], top[:, :, 1], ALU.subtract)
            v.tensor_tensor(gap[:, :, 1], top[:, :, 1], top[:, :, 0], ALU.subtract).then_inc(g_gap, 1)
            v.wait_ge(g_gap, q + 1)
            v.tensor_copy(topf[:], topi[:]).then_inc(g_topi, 1)
            v.wait_ge(g_topi, q + 1)
            for r in range(CT):
                for m in range(2):
                    i = v.tensor_scalar(pick[:, r, m, :], iota_e[:], topf[:, r, m:m + 1], None, ALU.is_equal)
            i.then_inc(g_pk, 1)
            v.wait_ge(g_sig, q + 1)
            v.wait_ge(g_pk, q + 1)
            for r in range(CT):
                i = v.tensor_scalar(we[:, r, :], pick[:, r, 0, :], gate[:, r, 0:1], None, ALU.mult)
            i.then_inc(g_pg, 1)
            v.wait_ge(g_pg, q + 1)
            for r in range(CT):
                i = v.scalar_tensor_tensor(out=we[:, r, :], in0=pick[:, r, 1, :], scalar=gate[:, r, 1:2],
                                           in1=we[:, r, :], op0=ALU.mult, op1=ALU.add)
            i.then_inc(g_we, 1)

        def moe_vector(v, n):
            v.wait_ge(m_bs, 3 * n + 2)
            v.tensor_tensor(gwl[:], gwraw[:], gwh[:].bitcast(F32), ALU.subtract).then_inc(m_bs, 1)
            v.tensor_scalar(b1p[:], b1[:], 1.0, None, ALU.add)
            with v.Fori(0, NCH) as c:
                ln_vector(v, LNC[n], c)
                ln_split(v, LNC[n], c)
                gate_vector(v, n, c)
            for e in range(E):
                v.wait_ge(m_wh, E * n + e + 1)
                v.tensor_tensor(w1l[:, e], w1raw[:, e % 2], w1h[:, e].bitcast(F32), ALU.subtract)
                v.tensor_tensor(w2l[:, e], w2raw[:, e % 2], w2h[:, e].bitcast(F32), ALU.subtract).then_inc(m_wl, 1)

            def glu(q, u):
                U = UNITS * q + u
                e, j = u // JI, u % JI
                v.wait_ge(m_sig, U + 1)
                v.scalar_tensor_tensor(out=gt[:, u % 2, :], in0=ps[:, GL_BANK + 2 * (u % 2), :],
                                       scalar=b1[:, e, j:j + 1], in1=sig[:, u % 2, :],
                                       op0=ALU.add, op1=ALU.mult).then_inc(m_gt, 1)
                v.wait_ge(m_l, U + 1)
                v.wait_ge(m_gt, U + 1)
                v.wait_ge(m_y, met(U - 1))
                v.scalar_tensor_tensor(out=lt[:, u % 2, :], in0=ps[:, GL_BANK + 2 * (u % 2) + 1, :],
                                       scalar=b1p[:, e, JI + j:JI + j + 1], in1=gt[:, u % 2, :],
                                       op0=ALU.add, op1=ALU.mult).then_inc(m_lt, 1)

            def low(q, u):
                U = UNITS * q + u
                v.wait_ge(m_yh, U + 1)
                v.tensor_tensor(yl[:, u % 3, :], y[:, u % 2, :], yh[:, u % 3, :].bitcast(F32),
                                ALU.subtract).then_inc(m_yl, 1)

            def residual(q, c):
                v.wait_ge(m_dn, UNITS * (q + 1))
                for r in range(CT):
                    xr = X[:, ds(CT * c + r, 1), :].rearrange("p a d -> p (a d)")
                    i = v.scalar_tensor_tensor(out=xr, in0=o_tile(r), scalar=0.5, in1=xr, op0=ALU.mult, op1=ALU.add)
                i.then_inc(m_x, 1)

            def chunk(c):
                q = NCH * n + c
                for u in range(UNITS):
                    glu(q, u)
                    if u >= 1:
                        low(q, u - 1)
                low(q, UNITS - 1)
                residual(q, c)

            chunk(0)
            with v.Fori(1, NCH) as c:
                chunk(c)

        def moe_gpsimd(g, n):
            with g.Fori(0, NCH) as c:
                ln_gpsimd(g, LNC[n], c)

            def chunk(c):
                q = NCH * n + c
                for u in range(UNITS):
                    U = UNITS * q + u
                    if u % JI == 0:
                        g.wait_ge(m_web[u // JI % WR], 16 * (E // WR * q + u // JI // WR + 1))
                    g.wait_ge(m_lt, U + 1)
                    g.wait_ge(m_yl, met(U - 1))
                    g.tensor_tensor(y[:, u % 2, :], lt[:, u % 2, :], web[:, u // JI % WR, :], ALU.mult).then_inc(m_y, 1)
            chunk(0)
            with g.Fori(1, NCH) as c:
                chunk(c)

        def moe_tensor(pe, n):
            with pe.Fori(0, NCH) as c:
                ln_tensor(pe, LNC[n], c)
                gate_tensor(pe, n, c)
            pe.wait_ge(ln_lo, KD * NCH * (LNC[n] + 1))
            pe.wait_ge(g_weTs, NCH * (n + 1))

            def up(q, c, u):
                U = UNITS * q + u
                e, j = u // JI, u % JI
                pe.wait_ge(m_lt, met(U - 1))
                if j == 0:
                    pe.wait_ge(m_wl, E * n + e + 1)
                for half, signal in ((0, m_g), (1, m_l)):
                    f = half * I + j * P
                    for k in range(KD):
                        i = product(pe, ps[:, GL_BANK + 2 * (u % 2) + half, :],
                                    (w1h[:, e, k, f:f + P], w1l[:, e, k, f:f + P]), xt(k, c), k == 0, k == KD - 1)
                    i.then_inc(signal, 1)

            def down(q, u):
                U = UNITS * q + u
                e, j = u // JI, u % JI
                pe.wait_ge(m_yl, U + 1)
                if u == 0:
                    pe.wait_ge(m_x, met(q))
                for r in range(CT):
                    i = product(pe, o_tile(r), (yh[:, u % 3, r * P:(r + 1) * P], yl[:, u % 3, r * P:(r + 1) * P]),
                                (w2h[:, e, j, :], w2l[:, e, j, :]), u == 0 and r % 2 == 0, False)
                if u < UNITS - 1:
                    i.then_inc(m_dn, 1)
                else:
                    pe.wait_ge(m_wtc, 16 * (q + 1))
                    for r in range(CT):
                        i = pe.matmul(o_tile(r), weTc[:, r * P:(r + 1) * P], b2[:], start=False, stop=r % 2 == 1)
                    i.then_inc(m_dn, 1)

            def chunk(c):
                q = NCH * n + c
                for u in range(UNITS):
                    up(q, c, u)
                    if u >= 2:
                        down(q, u - 2)
                down(q, UNITS - 2)
                down(q, UNITS - 1)

            chunk(0)
            with pe.Fori(1, NCH) as c:
                chunk(c)

        F = a["W1"].shape[2]
        FB = F // P
        f_ctx = ExitStack()
        fraw = [sb(f"f{w}raw", [P, KD, F], F32, f_ctx) for w in "13"]
        fh = [sb(f"f{w}h", [P, KD, F], F32R, f_ctx) for w in "13"]
        fl = [sb(f"f{w}l", [P, KD, F], F32R, f_ctx) for w in "13"]
        f2raw = sb("f2raw", [P, FB, D], F32, f_ctx)
        f2rh = sb("f2rh", [P, FB, D], F32R, f_ctx)
        f2rl = sb("f2rl", [P, FB, D], F32R, f_ctx)
        f2a = sb("f2a", [P, FB, D], F32, f_ctx)
        f2b = sb("f2b", [P, FB, D], F32, f_ctx)
        f2h = sb("f2h", [P, FB, D], F32R, f_ctx)
        f2l = sb("f2l", [P, FB, D], F32R, f_ctx)
        hadr = sb("hadr", [P, P], F32, f_ctx)
        had = sb("had", [P, P], F32R, f_ctx)
        fsig = sb("fsig", [P, 2, CH], F32, f_ctx)
        fg = sb("fg", [P, 2, CH], F32, f_ctx)
        fy = sb("fy", [P, 2, CH], F32, f_ctx)
        fyh = sb("fyh", [P, 3, CH], F32R, f_ctx)
        fyl = sb("fyl", [P, 3, CH], F32R, f_ctx)
        f_ctx.close()
        f_w2, f_w13, f_h2, f_l2, f_h13, f_l13, f_had, f_hev, f_bf, f_2h, f_2l = (
            sem(n) for n in "f_w2 f_w13 f_h2 f_l2 f_h13 f_l13 f_had f_hev f_bf f_2h f_2l".split())
        f_g, f_l, f_sig, f_gt, f_y, f_yh, f_yl, f_dn, f_x = (
            sem(n) for n in "f_g f_l f_sig f_gt f_y f_yh f_yl f_dn f_x".split())
        HB = FB * D // CH
        BF = FB.bit_length() - 1

        def ffn_sync(sp, n):
            sp.dma_start(fraw[0][:], a["W1"]).then_inc(f_w13, 16)
            sp.dma_start(fraw[1][:], a["W3"]).then_inc(f_w13, 16)
            sp.dma_start(hadr[:], a["hadamard"]).then_inc(f_w2, 16)
            sp.dma_start(f2raw[:], a["W2"]).then_inc(f_w2, 16)

        def ffn_scalar(s, n):
            s.wait_ge(f_w2, 32 * (n + 1))
            s.copy(had[:], hadr[:])
            s.copy(f2rh[:], f2raw[:]).then_inc(f_h2, 1)
            s.wait_ge(f_w13, 32 * (n + 1))
            for w in range(2):
                s.copy(fh[w][:], fraw[w][:]).then_inc(f_h13, 1)
            with s.Fori(0, NCH) as c:
                ln_scalar(s, LNF[n], c)
            for b in range(HB):
                s.wait_ge(f_had, n + 1)
                s.mul(f2a[:, 2 * b:2 * b + 2, :], ps[:, 4 + b, :], float(F) ** -0.5).then_inc(f_hev, 1)
            s.wait_ge(f_bf, (BF) * (n + 1))
            s.copy(f2h[:], f2b[:]).then_inc(f_2h, 1)

            def sigmoid(q, u):
                U = FB * q + u
                s.wait_ge(f_g, U + 1)
                s.wait_ge(f_gt, met(U - 1))
                s.activation(fsig[:, u % 2, :], ps[:, GL_BANK + 2 * (u % 2), :], ACT.Sigmoid).then_inc(f_sig, 1)

            def high(q, u):
                U = FB * q + u
                s.wait_ge(f_y, U + 1)
                s.wait_ge(f_dn, met(U - 2))
                s.copy(fyh[:, u % 3, :], fy[:, u % 2, :]).then_inc(f_yh, 1)

            def chunk(c):
                q = NCH * n + c
                for u in range(FB):
                    sigmoid(q, u)
                    if u >= 1:
                        high(q, u - 1)
                high(q, FB - 1)

            chunk(0)
            with s.Fori(1, NCH) as c:
                chunk(c)

        def ffn_vector(v, n):
            v.wait_ge(f_h2, n + 1)
            v.tensor_tensor(f2rl[:], f2raw[:], f2rh[:].bitcast(F32), ALU.subtract).then_inc(f_l2, 1)
            for w in range(2):
                v.wait_ge(f_h13, 2 * n + w + 1)
                v.tensor_tensor(fl[w][:], fraw[w][:], fh[w][:].bitcast(F32), ALU.subtract).then_inc(f_l13, 1)
            with v.Fori(0, NCH) as c:
                ln_vector(v, LNF[n], c)
                ln_split(v, LNF[n], c)
            v.wait_ge(f_hev, HB * (n + 1))
            bufs = [f2a, f2b]
            for k in range(BF):
                src, dst = (t[:].rearrange("p (a two h) d -> p a two (h d)", two=2, h=1 << k)
                            for t in (bufs[k % 2], bufs[(k + 1) % 2]))
                if k >= 1:
                    v.wait_ge(f_bf, met(BF * n + k))
                v.tensor_tensor(dst[:, :, 0], src[:, :, 0], src[:, :, 1], ALU.add)
                v.tensor_tensor(dst[:, :, 1], src[:, :, 0], src[:, :, 1], ALU.subtract).then_inc(f_bf, 1)
            assert BF % 2 == 1
            v.wait_ge(f_2h, n + 1)
            v.tensor_tensor(f2l[:], f2b[:], f2h[:].bitcast(F32), ALU.subtract).then_inc(f_2l, 1)

            def glu(q, u):
                U = FB * q + u
                v.wait_ge(f_sig, U + 1)
                v.tensor_tensor(fg[:, u % 2, :], ps[:, GL_BANK + 2 * (u % 2), :], fsig[:, u % 2, :],
                                ALU.mult).then_inc(f_gt, 1)
                v.wait_ge(f_l, U + 1)
                v.wait_ge(f_gt, U + 1)
                v.wait_ge(f_yl, met(U - 1))
                v.tensor_tensor(fy[:, u % 2, :], ps[:, GL_BANK + 2 * (u % 2) + 1, :], fg[:, u % 2, :],
                                ALU.mult).then_inc(f_y, 1)

            def residual(q, c):
                v.wait_ge(f_dn, FB * (q + 1))
                for r in range(CT):
                    xr = X[:, ds(CT * c + r, 1), :].rearrange("p a d -> p (a d)")
                    i = v.scalar_tensor_tensor(out=xr, in0=o_tile(r), scalar=0.5, in1=xr, op0=ALU.mult, op1=ALU.add)
                i.then_inc(f_x, 1)

            def chunk(c):
                q = NCH * n + c
                for u in range(FB):
                    glu(q, u)
                residual(q, c)

            chunk(0)
            with v.Fori(1, NCH) as c:
                chunk(c)

        def ffn_gpsimd(g, n):
            with g.Fori(0, NCH) as c:
                ln_gpsimd(g, LNF[n], c)

            def chunk(c):
                q = NCH * n + c
                for u in range(FB):
                    U = FB * q + u
                    g.wait_ge(f_yh, U + 1)
                    g.tensor_tensor(fyl[:, u % 3, :], fy[:, u % 2, :], fyh[:, u % 3, :].bitcast(F32),
                                    ALU.subtract).then_inc(f_yl, 1)
            chunk(0)
            with g.Fori(1, NCH) as c:
                chunk(c)

        def ffn_tensor(pe, n):
            pe.wait_ge(f_l2, n + 1)
            for b in range(HB):
                pe.matmul(ps[:, 4 + b, :], had[:], f2rh[:, 2 * b:2 * b + 2, :], start=True, stop=False)
                i = pe.matmul(ps[:, 4 + b, :], had[:], f2rl[:, 2 * b:2 * b + 2, :], start=False, stop=True)
            i.then_inc(f_had, 1)
            with pe.Fori(0, NCH) as c:
                ln_tensor(pe, LNF[n], c)
            pe.wait_ge(ln_lo, KD * NCH * (LNF[n] + 1))
            pe.wait_ge(f_l13, 2 * (n + 1))
            pe.wait_ge(f_hev, HB * (n + 1))

            def up(q, c, u):
                U = FB * q + u
                pe.wait_ge(f_y, met(U - 1))
                for half, signal in ((0, f_g), (1, f_l)):
                    for k in range(KD):
                        i = product(pe, ps[:, GL_BANK + 2 * (u % 2) + half, :],
                                    (fh[half][:, k, u * P:(u + 1) * P], fl[half][:, k, u * P:(u + 1) * P]),
                                    xt(k, c), k == 0, k == KD - 1)
                    i.then_inc(signal, 1)

            def down(q, u):
                U = FB * q + u
                pe.wait_ge(f_yl, U + 1)
                if u == 0:
                    pe.wait_ge(f_2l, n + 1)
                    pe.wait_ge(f_x, met(q))
                for r in range(CT):
                    i = product(pe, o_tile(r), (fyh[:, u % 3, r * P:(r + 1) * P], fyl[:, u % 3, r * P:(r + 1) * P]),
                                (f2h[:, u, :], f2l[:, u, :]), u == 0 and r % 2 == 0, u == FB - 1 and r % 2 == 1)
                i.then_inc(f_dn, 1)

            def chunk(c):
                q = NCH * n + c
                for u in range(FB):
                    up(q, c, u)
                    if u >= 2:
                        down(q, u - 2)
                down(q, FB - 2)
                down(q, FB - 1)

            chunk(0)
            with pe.Fori(1, NCH) as c:
                chunk(c)

        NHEAD, HD, RD, LAT = 16, 16, 64, 64
        GH = 4
        NG = NHEAD // GH
        SCALE = float(1.0 / np.sqrt(np.float32(HD + RD)))
        BF16 = mybir.dt.bfloat16
        a_ctx = ExitStack()
        QL = sb("QL", [P, T], F32R, a_ctx)
        CK = sb("CK", [P, T], F32R, a_ctx)
        KB = sb("KB", [P, T], F32R, a_ctx)
        V = sb("V", [P, TILES, D], F32, a_ctx)
        rb = sb("rb", [P, 2, CH], F32, a_ctx)
        rr = sb("rr", [P, 2, CH], F32, a_ctx)
        cs = sb("cs", [P, 2, 2, CH], F32, a_ctx)
        tmpq = sb("tmpq", [P, 2, CH], F32R, a_ctx)
        tmpk = sb("tmpk", [P, 2, CH], F32R, a_ctx)
        cm_raw = sb("cm_raw", [P, 2, P], F32, a_ctx)
        cm_bf = sb("cm_bf", [P, 3, P], BF16, a_ctx)
        rowm = sb("rowm", [P, 1], F32, a_ctx)
        mp = sb("mp", [P, GH * CT, 2], F32, a_ctx)
        mcol = sb("mcol", [P, GH * CT], F32, a_ctx)
        mrow = sb("mrow", [GH * CT, P], F32R, a_ctx)
        whr = sb("whr", [P, 2, CH], F32, a_ctx)
        whh = sb("whh", [P, GH, CH], F32R, a_ctx)
        whl = sb("whl", [P, GH, CH], F32R, a_ctx)
        wor = sb("wor", [P, D], F32, a_ctx)
        woh = sb("woh", [P, D], F32R, a_ctx)
        wol = sb("wol", [P, D], F32R, a_ctx)
        VG = sb("VG", [P, TILES, GH, 2 * HD], F32, a_ctx)
        qA = sb("qA", [P, 2, GH, CH], F32R, a_ctx)
        qB = sb("qB", [P, 2, GH, CH], F32R, a_ctx)
        pre_ctx = ExitStack()
        wp_raw = sb("wp_raw", [P, KD, 4, P], F32, pre_ctx)
        wp_h = sb("wp_h", [P, KD, 4, P], F32R, pre_ctx)
        wp_l = sb("wp_l", [P, KD, 4, P], F32R, pre_ctx)
        wv_raw = sb("wv_raw", [P, D], F32, pre_ctx)
        wv_h = sb("wv_h", [P, D], F32R, pre_ctx)
        wv_l = sb("wv_l", [P, D], F32R, pre_ctx)
        tmpl = sb("tmpl", [P, 2, CH], F32R, pre_ctx)
        pre_ctx.close()
        PT = sb("PT", [P, 2, GH, CH], F32, a_ctx)
        Osb = sb("Osb", [P, CH], F32, a_ctx)
        rec = sb("rec", [P, CH], F32, a_ctx)
        onh = sb("onh", [P, CH], F32R, a_ctx)
        onl = sb("onl", [P, CH], F32R, a_ctx)
        spread = sb("spread", [P, P], F32, a_ctx)
        a_ctx.close()
        KA = [XTh[:, 0, :], XTh[:, 1, :], XTl[:, 0, :], XTl[:, 1, :]]
        (a_c, a_wph, a_wpl, a_ms, a_cs, a_pq, a_pt, a_pd, a_rr, a_rh, a_kb, a_v, a_ve, a_kr) = (
            sem(x) for x in ("a_c a_wph a_wpl a_ms a_cs a_pq a_pt a_pd a_rr a_rh a_kb a_v a_ve a_kr").split())
        a_w = [sem("a_w0"), sem("a_w1")]
        (a_wh, a_wl, a_wo, a_woh, a_wol, a_full, a_free, a_tk, a_tq, a_qhi, a_qb, a_mc, a_mt, a_mr, a_md, a_st, a_exp,
         a_av, a_vg, a_oe, a_den, a_rc, a_on, a_oh, a_ol) = (
            sem(x) for x in ("a_wh a_wl a_wo a_woh a_wol a_full a_free a_tk a_tq a_qhi a_qb a_mc a_mt a_mr a_md a_st a_exp "
                             "a_av a_vg a_oe a_den a_rc a_on a_oh a_ol").split())
        a_csl = [sem("a_cs0"), sem("a_cs1")]
        ST_BANK, AV_BANK, MISC_BANK = 4, 6, 7

        def first_part(c):
            yield "P", c, 0, 0
            yield "P", c, 1, 0
            for h in range(GH):
                yield "H", c, h, 0
                for r in range(CT):
                    yield "M", c, h, r
                if h + 2 < GH:
                    yield "P", c, h + 2, 0
            yield "R", c, 0, 0

        def second_part(c):
            for j in range(CT * (c + 1)):
                yield "S", c, j, 0
                if c >= 1 and j == 1:
                    yield "F", c - 1, 0, 0
                if c >= 1 and j == 3:
                    yield "G", c - 1, 0, 0
            yield "L", c, 0, 0

        def steps():
            for h in range(GH):
                for c in range(NCH):
                    yield "K", c, h, 0
            yield from first_part(0)
            for c in range(NCH):
                one = list(first_part(c + 1)) if c + 1 < NCH else []
                two = list(second_part(c))
                done = 0
                for k, step in enumerate(two):
                    yield step
                    want = (k + 1) * len(one) // len(two)
                    yield from one[done:want]
                    done = want
            yield "F", NCH - 1, 0, 0
            yield "G", NCH - 1, 0, 0

        STEPS = list(steps())
        piece, PIECES = {}, 0
        for s_, c_, h_, r_ in STEPS:
            for k in range({"K": 1, "P": 2, "M": (c_ + 2) // 2, "G": 1}.get(s_, 0)):
                piece[s_, c_, h_, r_, k] = PIECES
                PIECES += 1
        if PIECES % 2:
            raise ValueError("a group takes an even number of pieces")
        SROUND = [CT * c * (c + 1) // 2 for c in range(NCH + 1)]

        def slot(n):
            return 2 * (n % 2)

        def st_start(c, j):
            return max(0, j - CT * c) * P

        def attn_tensor(pe, n):
            k0 = LNA[n]
            with pe.Fori(0, NCH) as c:
                ln_tensor(pe, k0, c)
            pe.wait_ge(ln_lo, KD * NCH * (k0 + 1))
            pe.wait_ge(a_wpl, 1)

            def latents(c):
                pe.wait_ge(a_pd, met(4 * c))
                for w in range(4):
                    for k in range(KD):
                        i = product(pe, ps[:, w, :], (wp_h[:, k, w, :], wp_l[:, k, w, :]), xt(k, c), k == 0, k == KD - 1)
                    i.then_inc(a_pq, 1)
            with pe.Fori(0, NCH) as c:
                latents(c)
            pe.wait_ge(a_pd, met(4 * NCH))
            for t in range(TILES):
                pe.wait_ge(a_ve, met(t - 3))
                tok = slice(t * P, (t + 1) * P)
                pe.matmul(ps[:, 4 + t % 4, 0:D], CK[:, tok], wv_h[:], start=True, stop=False)
                pe.matmul(ps[:, 4 + t % 4, 0:D], CK[0:LAT, tok], wv_l[0:LAT, :], start=False, stop=True).then_inc(a_v, 1)
            pe.wait_ge(a_ve, TILES)
            pe.wait_ge(a_kb, NCH)
            pe.wait_ge(a_kr, 1)

            def project(out, h, w, lat, cols):
                pe.matmul(out, whh[:, h, w * P:(w + 1) * P], lat[:, cols], start=True, stop=False)
                return pe.matmul(out, whl[0:LAT, h, w * P:(w + 1) * P], lat[0:LAT, cols], start=False, stop=True)

            def group(g):
                def take(key, after=0):
                    pe.wait_ge(a_free, met(PIECES * g + max(piece[key] - 1, after)))
                    return slot(piece[key])

                def products(c, j):
                    pe.wait_ge(a_exp, met(GH * (SROUND[-1] * g + SROUND[c] + j + 1)))
                    if j == 0:
                        pe.wait_ge(a_vg, g + 1)
                        pe.wait_ge(a_oe, met(NCH * g + c))
                    lo = st_start(c, j)
                    for h in range(GH):
                        i = pe.matmul(ps[2 * HD * h:2 * HD * (h + 1), AV_BANK, lo:CH], VG[:, j, h, :], PT[:, j % 2, h, lo:CH],
                                      start=(j == 0), stop=(j == CT * (c + 1) - 1))
                    i.then_inc(a_av, 1)

                for kind, c, h, r in STEPS:
                    u = NCH * g + c
                    par = c % 2
                    if kind == "K":
                        b = take((kind, c, h, r, 0))
                        pe.wait_ge(a_wl, GH * g + h + 1)
                        project(ps[:, b, :], h, 3, CK, slice(CH * c, CH * (c + 1))).then_inc(a_full, 1)
                    elif kind == "P":
                        b = take((kind, c, h, r, 0))
                        project(ps[:, b, :], h, 0, QL, slice(CH * c, CH * (c + 1)))
                        project(ps[:, b + 1, :], h, 1, QL, slice(CH * c, CH * (c + 1))).then_inc(a_full, 1)
                        b = take((kind, c, h, r, 1))
                        project(ps[:, b, :], h, 2, QL, slice(CH * c, CH * (c + 1))).then_inc(a_full, 1)
                    elif kind == "M":
                        pe.wait_ge(a_qhi, GH * u + h + 1)
                        q = qA[:, par, h, r * P:(r + 1) * P]
                        for k in range((c + 2) // 2):
                            b = take((kind, c, h, r, k), piece["P", c, h, 0, 1] + 1)
                            for s in range(2 * k, min(2 * k + 2, c + 1)):
                                wide = CH if s < c else max(2 * P, (r + 1) * P)
                                i = pe.matmul(ps[:, b + s % 2, 0:wide], q, KA[h][:, CH * s:CH * s + wide],
                                              start=True, stop=s < c)
                                if s == c:
                                    i = pe.matmul(ps[:, b + s % 2, r * P:(r + 1) * P], cm_bf[:, 2, :], cm_bf[:, 0, :],
                                                  start=False, stop=True)
                            i.then_inc(a_full, 1)
                    elif kind == "R":
                        pe.wait_ge(a_mc, u + 1)
                        pe.wait_ge(a_mr, met(u))
                        pe.wait_ge(a_rc, met(u - 1 if c >= 1 else u))
                        pe.transpose(ps[0:GH * CT, MISC_BANK, 0:P], mcol[:], ident[:]).then_inc(a_mt, 1)
                    elif kind == "S":
                        if h == 0:
                            pe.wait_ge(a_md, 16 * (u + 1))
                            pe.wait_ge(a_qb, GH * (u + 1))
                        j = h
                        lo = st_start(c, j)
                        mm_lo = min(lo, CH - 2 * P)
                        for hh in range(GH):
                            e = GH * (SROUND[-1] * g + SROUND[c] + j) + hh
                            pe.wait_ge(a_exp, met(e - 1))
                            o = ps[:, ST_BANK + hh % 2, :]
                            pe.matmul(o[:, mm_lo:CH], KA[hh][:, j * P:(j + 1) * P], qA[:, par, hh, mm_lo:CH], start=True, stop=False)
                            i = pe.matmul(o[:, mm_lo:CH], KB[:, j * P:(j + 1) * P], qB[:, par, hh, mm_lo:CH],
                                          start=False, stop=j < CT * c)
                            if j >= CT * c:
                                i = pe.matmul(o[:, lo:lo + P], cm_bf[:, 2, :], cm_bf[:, 1, :], start=False, stop=True)
                            i.then_inc(a_st, 1)
                        if j >= 1:
                            products(c, j - 1)
                    elif kind == "L":
                        products(c, CT * (c + 1) - 1)
                    elif kind == "F":
                        pe.wait_ge(a_oe, u + 1)
                        pe.wait_ge(a_mr, met(u + 2 if c + 1 < NCH and False else 0))
                        pe.matmul(ps[:, MISC_BANK, :], spread[:], Osb[:], start=True, stop=True).then_inc(a_den, 1)
                    elif kind == "G":
                        pe.wait_ge(a_ol, u + 1)
                        pe.wait_ge(a_wol, g + 1)
                        b = take((kind, c, h, r, 0))
                        for t in range(CT):
                            tok = slice(t * P, (t + 1) * P)
                            i = product(pe, ps[:, b + t // 2, (t % 2) * D:(t % 2 + 1) * D], (onh[:, tok], onl[:, tok]),
                                        (woh[:], wol[:]), t % 2 == 0, t % 2 == 1)
                        i.then_inc(a_full, 1)

            group(0)
            with pe.Fori(1, NG) as g:
                group(g)

        def attn_vector(v, n):
            k0 = LNA[n]
            v.wait_ge(a_ms, 1)
            v.memset(tmpk[96:97].bitcast(F32), 1.0).then_inc(a_ms, 1)
            v.wait_ge(a_wph, 1)
            v.tensor_tensor(wp_l[:], wp_raw[:], wp_h[:].bitcast(F32), ALU.subtract)
            v.tensor_tensor(wv_l[:], wv_raw[:], wv_h[:].bitcast(F32), ALU.subtract).then_inc(a_wpl, 1)
            with v.Fori(0, NCH) as c:
                ln_vector(v, k0, c)
                ln_split(v, k0, c)

            def latents(c):
                cols = ds(CH * c, CH)
                for w, dst in ((0, QL), (1, CK)):
                    v.wait_ge(a_pt, 2 * c + w + 1)
                    v.tensor_tensor(dst[:, cols], ps[:, w, :], tmpl[:, w, :].bitcast(F32), ALU.add).then_inc(a_pd, 1)
                v.wait_ge(a_cs, 16 * (c + 1))
                v.wait_ge(a_rr, met(c))
                for w in range(2):
                    v.wait_ge(a_pq, met(4 * c + 3 + w))
                    v.tensor_tensor(rb[:, w, :], ps[:, 2 + w, :], cs[:, 0, w, :], ALU.mult).then_inc(a_pd, 1)
                v.wait_ge(a_rh, c + 1)
                v.tensor_tensor(KB[:, cols], rr[:, 0, :], tmpl[:, 0, :].bitcast(F32), ALU.add).then_inc(a_kb, 1)
            v.wait_ge(a_ms, 2)
            with v.Fori(0, NCH) as c:
                latents(c)

            def group(g):
                def full(key):
                    v.wait_ge(a_full, PIECES * g + piece[key] + 1)
                    return slot(piece[key])

                for h in range(GH):
                    v.wait_ge(a_wh, GH * g + h + 1)
                    v.tensor_tensor(whl[:, h, :], whr[:, h % 2, :], whh[:, h, :].bitcast(F32), ALU.subtract).then_inc(a_wl, 1)
                v.wait_ge(a_woh, g + 1)
                v.tensor_tensor(wol[:], wor[:], woh[:].bitcast(F32), ALU.subtract).then_inc(a_wol, 1)
                for kind, c, h, r in STEPS:
                    u = NCH * g + c
                    par = c % 2
                    pj = GH * u + h
                    if kind == "K":
                        b = full((kind, c, h, r, 0))
                        v.wait_ge(a_tk, NCH * (GH * g + h) + c + 1)
                        v.tensor_tensor(KA[h][RD:P, CH * c:CH * (c + 1)], ps[RD:P, b, :],
                                        tmpk[RD:P, c % 2, :].bitcast(F32), ALU.add).then_inc(a_free, 1)
                    elif kind == "P":
                        b = full((kind, c, h, r, 0))
                        if h == 0:
                            v.wait_ge(a_csl[par], 16 * (NCH // 2 * g + c // 2 + 1))
                        v.wait_ge(a_rr, met(NCH + pj))
                        v.tensor_tensor(rb[:, 0, :], ps[:, b, :], cs[:, par, 0, :], ALU.mult)
                        v.tensor_tensor(rb[:, 1, :], ps[:, b + 1, :], cs[:, par, 1, :], ALU.mult).then_inc(a_free, 1)
                        b = full((kind, c, h, r, 1))
                        v.wait_ge(a_tq, pj + 1)
                        v.tensor_tensor(qA[RD:P, par, h, :], ps[RD:P, b, :], tmpq[RD:P, h % 2, :].bitcast(F32),
                                        ALU.add).then_inc(a_free, 1)
                    elif kind == "M":
                        for k in range((c + 2) // 2):
                            b = full((kind, c, h, r, k))
                            end = min(2 * CH, (CT * c + r + 1) * P - 2 * CH * k)
                            v.tensor_reduce(mp[:, CT * h + r, k:k + 1],
                                            ps[:, b:b + 2, :].rearrange("p b s -> p (b s)")[:, 0:end], AX_X,
                                            ALU.max).then_inc(a_free, 1)
                    elif kind == "R":
                        v.wait_ge(a_free, met(PIECES * g + piece["M", c, GH - 1, CT - 1, (c + 2) // 2 - 1] + 1))
                        v.wait_ge(a_mt, met(u))
                        v.tensor_reduce(mcol[:], mp[:, :, 0:(c + 2) // 2], AX_X, ALU.max).then_inc(a_mc, 1)
                    elif kind == "F":
                        v.wait_ge(a_den, u + 1)
                        v.reciprocal(rec[:], ps[:, MISC_BANK, :]).then_inc(a_rc, 1)
                        v.wait_ge(a_rc, u + 1)
                        v.tensor_tensor(rec[:], Osb[:], rec[:], ALU.mult).then_inc(a_on, 1)
                        v.wait_ge(a_oh, u + 1)
                        v.tensor_tensor(onl[:], rec[:], onh[:].bitcast(F32), ALU.subtract).then_inc(a_ol, 1)
                    elif kind == "G":
                        b = full((kind, c, h, r, 0))
                        for t in range(CT):
                            xr = X[:, CT * c + t, :]
                            i = v.tensor_tensor(xr, ps[:, b + t // 2, (t % 2) * D:(t % 2 + 1) * D], xr, ALU.add)
                        i.then_inc(a_free, 1)

            group(0)
            with v.Fori(1, NG) as g:
                group(g)

        def attn_scalar(s, n):
            k0 = LNA[n]
            s.wait_ge(a_c, 96)
            s.copy(cm_bf[:, 0:2, :], cm_raw[:])
            s.copy(cm_bf[:, 2, :], ident[:])
            s.copy(wp_h[:], wp_raw[:])
            s.copy(wv_h[:], wv_raw[:]).then_inc(a_wph, 1)
            with s.Fori(0, NCH) as c:
                ln_scalar(s, k0, c)
            s.wait_ge(a_ms, 2)

            def latents(c):
                for w in range(2):
                    s.wait_ge(a_pq, 4 * c + w + 1)
                    if w == 0:
                        s.wait_ge(a_kb, met(c))
                    else:
                        s.wait_ge(a_pd, met(4 * c))
                    s.mul(tmpl[LAT:P, w, :], ps[LAT:P, w, :], -1.0).then_inc(a_pt, 1)
                s.wait_ge(a_rr, c + 1)
                s.wait_ge(a_pd, 4 * c + 1)
                s.mul(tmpl[LAT:P, 0, :], rr[LAT:P, 0, :], -1.0).then_inc(a_rh, 1)
            with s.Fori(0, NCH) as c:
                latents(c)
            for t in range(TILES):
                s.wait_ge(a_v, t + 1)
                s.copy(V[:, t, :], ps[:, 4 + t % 4, 0:D]).then_inc(a_ve, 1)
            s.wait_ge(a_kb, NCH)
            for h in range(GH):
                i = s.copy(KA[h][0:RD, :], KB[0:RD, :].bitcast(F32))
            i.then_inc(a_kr, 1)

            def group(g):
                for h in range(GH):
                    s.wait_ge(a_w[h % 2], 16 * (GH // 2 * g + h // 2 + 1))
                    if h == 0:
                        s.wait_ge(a_full, met(PIECES * g))
                    s.copy(whh[:, h, :], whr[:, h % 2, :]).then_inc(a_wh, 1)
                s.wait_ge(a_wo, 16 * (g + 1))
                s.copy(woh[:], wor[:]).then_inc(a_woh, 1)
                s.wait_ge(a_av, met(SROUND[-1] * g))
                s.wait_ge(a_ve, TILES)
                s.copy(VG[:, :, :, 0:HD], V[:, :, ds(GH * HD * g, GH * HD)].rearrange("p t (h d) -> p t h d", d=HD)).then_inc(a_vg, 1)
                for kind, c, h, r in STEPS:
                    u = NCH * g + c
                    par = c % 2
                    pj = GH * u + h
                    if kind == "K":
                        s.wait_ge(a_full, PIECES * g + piece[kind, c, h, r, 0] + 1)
                        if h > 0 or c > 1:
                            s.wait_ge(a_free, met(PIECES * g + piece[kind, c, h, r, 0] - 1))
                        s.activation(tmpk[RD:RD + 32, c % 2, :], ps[RD:RD + 32, slot(piece[kind, c, h, r, 0]), :],
                                     ACT.Copy, scale=rowm[RD:RD + 32, :]).then_inc(a_tk, 1)
                    elif kind == "P":
                        s.wait_ge(a_full, PIECES * g + piece[kind, c, h, r, 1] + 1)
                        if True:
                            last = ("P", c, h - 2, 0, 1) if h >= 2 else None
                            if last:
                                s.wait_ge(a_free, PIECES * g + piece[last] + 1)
                            elif c >= 1:
                                s.wait_ge(a_free, met(PIECES * g + piece["P", c - 1, h + 2, 0, 1] + 1))
                            else:
                                s.wait_ge(a_free, met(PIECES * g))
                        s.activation(tmpq[96:P, h % 2, :], ps[96:P, slot(piece[kind, c, h, r, 1]), :],
                                     ACT.Copy, scale=rowm[96:P, :]).then_inc(a_tq, 1)
                    elif kind == "H":
                        s.wait_ge(a_rr, NCH + pj + 1)
                        s.copy(qA[0:RD, par, h, :], rr[0:RD, h % 2, :])
                        s.copy(qB[RD:P, par, h, :], rr[RD:P, h % 2, :]).then_inc(a_qhi, 1)
                    elif kind == "R":
                        s.wait_ge(a_mt, u + 1)
                        s.wait_ge(a_md, met(16 * u))
                        s.mul(mrow[:], ps[0:GH * CT, MISC_BANK, 0:P], -1.0).then_inc(a_mr, 1)
                    elif kind == "S":
                        j = h
                        lo = st_start(c, j)
                        for hh in range(GH):
                            rnd = SROUND[-1] * g + SROUND[c] + j
                            s.wait_ge(a_st, GH * rnd + hh + 1)
                            if hh == 0:
                                s.wait_ge(a_av, met(rnd - 1))
                            s.activation(PT[:, j % 2, hh, lo:CH], ps[:, ST_BANK + hh % 2, lo:CH], ACT.Exp,
                                         scale=SCALE).then_inc(a_exp, 1)
                    elif kind == "L":
                        s.wait_ge(a_av, met(SROUND[-1] * g + SROUND[c + 1]))
                        s.wait_ge(a_ol, met(u))
                        s.copy(Osb[:], ps[:, AV_BANK, :]).then_inc(a_oe, 1)
                    elif kind == "F":
                        s.wait_ge(a_on, u + 1)
                        s.wait_ge(a_full, met(PIECES * g + piece["G", c - 1, 0, 0, 0] + 1 if c >= 1 else PIECES * g))
                        s.copy(onh[:], rec[:]).then_inc(a_oh, 1)

            group(0)
            with s.Fori(1, NG) as g:
                group(g)

        def attn_gpsimd(p, n):
            k0 = LNA[n]
            p.memset(VG[:], 1.0)
            for t in (tmpl, tmpq, tmpk):
                i = p.memset(t[:].bitcast(F32), 0.0)
            i.then_inc(a_ms, 1)
            with p.Fori(0, NCH) as c:
                ln_gpsimd(p, k0, c)
            with p.Fori(0, NCH) as c:
                p.wait_ge(a_pd, 4 * (c + 1))
                p.wait_ge(a_kb, met(c))
                p.tensor_tensor(rr[:, 0, :], rb[:, 0, :], rb[:, 1, :], ALU.add).then_inc(a_rr, 1)

            def group(g):
                for kind, c, h, r in STEPS:
                    u = NCH * g + c
                    par = c % 2
                    pj = GH * u + h
                    if kind == "P":
                        p.wait_ge(a_free, PIECES * g + piece[kind, c, h, r, 0] + 1)
                        p.wait_ge(a_kb, NCH)
                        p.wait_ge(a_qb, met(pj - 1))
                        p.tensor_tensor(rr[:, h % 2, :], rb[:, 0, :], rb[:, 1, :], ALU.add).then_inc(a_rr, 1)
                    elif kind == "H":
                        p.wait_ge(a_qhi, pj + 1)
                        p.tensor_tensor(qB[0:RD, par, h, :], rr[0:RD, h % 2, :], qA[0:RD, par, h, :].bitcast(F32),
                                        ALU.subtract).then_inc(a_qb, 1)

            group(0)
            with p.Fori(1, NG) as g:
                group(g)

        def attn_sync(sp, n):
            sp.dma_start(wp_raw[:], a["wp"]).then_inc(a_c, 16)
            sp.dma_start(wv_raw[:], a["wv"]).then_inc(a_c, 16)
            sp.dma_start(cm_raw[:], a["cmask"]).then_inc(a_c, 16)
            sp.dma_start(rowm[:], a["rowm"]).then_inc(a_c, 16)
            sp.dma_start(spread[:], a["spread"]).then_inc(a_c, 32)
            with sp.Fori(0, NCH) as c:
                sp.wait_ge(a_pd, met(4 * c))
                sp.dma_start(cs[:, 0], a["rope"][:, :, ds(CH * c, CH)]).then_inc(a_cs, 16)
            sp.wait_ge(a_pd, met(4 * NCH))

            def group(g):
                for h in range(GH):
                    sp.wait_ge(a_wl, met(GH * g + h - 1))
                    sp.dma_start(whr[:, h % 2, :], a["whead"][:, ds(GH * g + h, 1), :]).then_inc(a_w[h % 2], 16)
                sp.wait_ge(a_wol, met(g))
                sp.dma_start(wor[:], a["wog"][ds(g, 1)]).then_inc(a_wo, 16)
                for kind, c, h, r in STEPS:
                    u = NCH * g + c
                    if kind == "P" and h == 0:
                        if c >= 2:
                            sp.wait_ge(a_rr, met(NCH + GH * (u - 1)))
                        else:
                            sp.wait_ge(a_rr, met(NCH + GH * NCH * g))
                        sp.dma_start(cs[:, c % 2], a["rope"][:, :, CH * c:CH * (c + 1)]).then_inc(a_csl[c % 2], 16)
                    if kind == "R":
                        sp.wait_ge(a_mr, u + 1)
                        sp.dma_start(qA[96:97, c % 2].rearrange("a h (r t) -> a (h r) t", t=P).bitcast(F32), mrow[:].bitcast(F32)).then_inc(a_md, 16)

            group(0)
            with sp.Fori(1, NG) as g:
                group(g)

        NHI, DI = 16, 128
        TOPK = 32
        NEG = -1e30
        TAKEN = -3e38
        KVI = 2 * P + NHI
        i_ctx = ExitStack()
        ikv_h = sb("ikv_h", [P, KD, KVI], F32R, i_ctx)
        ikv_l = sb("ikv_l", [P, KD, KVI], F32R, i_ctx)
        wih = sb("wih", [P, NHI + 1, KD, DI], F32R, i_ctx)
        wil = sb("wil", [P, NHI + 1, KD, DI], F32R, i_ctx)
        KIh = sb("KIh", [P, T], F32R, i_ctx)
        KIl = sb("KIl", [P, T], F32R, i_ctx)
        imask = sb("imask", [P, CH], F32, i_ctx)
        iw = sb("iw", [P, TILES, NHI], F32, i_ctx)
        iwa = sb("iwa", [P, TILES, NHI], F32, i_ctx)
        iws = sb("iws", [P, TILES, NHI], F32, i_ctx)
        kvs = sb("kvs", [P, 2, 2 * P], F32, i_ctx)
        Isc = sb("Isc", [P, 2, T], F32, i_ctx)
        RL = 4
        rl = sb("rl", [P, RL, CH], F32, i_ctx)
        v8 = sb("v8", [P, 2, 8], F32, i_ctx)
        idx = sb("idx", [P, TILES, TOPK], U32, i_ctx)
        idxf = sb("idxf", [P, TILES, TOPK], F32, i_ctx)
        selt = sb("selt", [P, 4, P // 4], F32, i_ctx)
        raw_ctx = ExitStack()
        wir = sb("wir", [P, NHI + 1, D], F32, raw_ctx)
        wirh = sb("wirh", [P, NHI + 1, D], F32R, raw_ctx)
        wirl = sb("wirl", [P, NHI + 1, D], F32R, raw_ctx)
        ikv_raw = sb("ikv_raw", [P, KD, KVI], F32, raw_ctx)
        ihadr = sb("ihadr", [P, P], F32, raw_ctx)
        ihad = sb("ihad", [P, P], F32R, raw_ctx)
        raw_ctx.close()
        qih = sb("qih", [P, NHI, CH], F32R, i_ctx)
        qil = sb("qil", [P, NHI, CH], F32R, i_ctx)
        i_ctx.close()
        (i_c, i_rh, i_rl, i_t, i_th, i_tl, i_ki, i_kh, i_kl, i_kv, i_kve, i_iw, i_q, i_qh, i_ql, i_L, i_R,
         i_A, i_k, i_xf, i_xt) = (
            sem(x) for x in ("i_c i_rh i_rl i_t i_th i_tl i_ki i_kh i_kl i_kv i_kve i_iw i_q i_qh i_ql i_L i_R "
                             "i_A i_k i_xf i_xt").split())
        i_kvd = [sem("i_kvd0"), sem("i_kvd1")]
        HSC = float(DI) ** -0.5
        NTB = (NHI + 1 + 1) // 2

        def blocks(t):
            return [(h, b) for h in range(NHI) for b in range(t // CT + 1)]

        LB = [0]
        for t in range(TILES):
            LB.append(LB[-1] + len(blocks(t)))

        def width(t, b):
            return CH if b < t // CT else (t % CT + 1) * P

        def index_sync(sp, n):
            sp.dma_start(wir[:], a["wi"]).then_inc(i_c, 16)
            sp.dma_start(ihadr[:], a["hadamard"]).then_inc(i_c, 16)
            sp.dma_start(ikv_raw[:], a["wkvi"]).then_inc(i_c, 16)
            sp.dma_start(imask[:], a["imask"]).then_inc(i_c, 16)
            sp.dma_start(selt[:], a["selt"]).then_inc(i_c, 16)
            for t in range(TILES):
                sp.wait_ge(i_kve, t + 1)
                sp.dma_start(a["kv_scratch"][t * P:(t + 1) * P, :], kvs[:, t % 2, :]).then_inc(i_kvd[t % 2], 16)
            sp.wait_ge(i_kvd[0], met(16 * TILES // 2))
            sp.wait_ge(i_kvd[1], met(16 * TILES // 2))

        def index_tensor(pe, n):
            k0 = LNA[n]
            pe.wait_ge(i_rl, 1)
            for m in range(NTB):
                pe.wait_ge(i_tl, met(m - 3))
                for hh in range(min(2, NHI + 1 - 2 * m)):
                    for k in range(KD):
                        at = (hh * KD + k) * DI
                        o = ps[:, 4 + m % 4, at:at + DI]
                        first = at == 0
                        last = hh == min(2, NHI + 1 - 2 * m) - 1 and k == KD - 1
                        pe.matmul(o, wirh[:, 2 * m + hh, k * P:(k + 1) * P], ihad[:], start=first, stop=False)
                        i = pe.matmul(o, wirl[:, 2 * m + hh, k * P:(k + 1) * P], ihad[:], start=False, stop=last)
                i.then_inc(i_t, 1)
            with pe.Fori(0, NCH) as c:
                ln_tensor(pe, k0, c)
            pe.wait_ge(ln_lo, KD * NCH * (k0 + 1))
            pe.wait_ge(i_tl, NTB)

            def keys(c):
                pe.wait_ge(i_kl, met(c))
                for k in range(KD):
                    i = product(pe, ps[:, 2, :], (wih[:, NHI, k, :], wil[:, NHI, k, :]), xt(k, c), k == 0, k == KD - 1)
                i.then_inc(i_ki, 1)
            with pe.Fori(0, NCH) as c:
                keys(c)
            for t in range(TILES):
                pe.wait_ge(i_kve, met(t - 1))
                tok = slice(t * P, (t + 1) * P)
                for k in range(KD):
                    i = product(pe, ps[:, 4 + t % 2, 0:KVI], (XTh[:, k, tok], XTl[:, k, tok]),
                                (ikv_h[:, k, :], ikv_l[:, k, :]), k == 0, k == KD - 1)
                i.then_inc(i_kv, 1)
            pe.wait_ge(i_kl, NCH)
            pe.wait_ge(i_kve, TILES)
            n_l = 0
            for c in range(NCH):
                for h in range(NHI):
                    pe.wait_ge(i_ql, met(NHI * c + h - 1))
                    for k in range(KD):
                        i = product(pe, ps[:, h % 2, :], (wih[:, h, k, :], wil[:, h, k, :]), xt(k, c), k == 0, k == KD - 1)
                    i.then_inc(i_q, 1)
                for t in range(CT * c, CT * (c + 1)):
                    tok = slice((t - CT * c) * P, (t - CT * c + 1) * P)
                    for h, b in blocks(t):
                        pe.wait_ge(i_ql, NHI * c + h + 1)
                        pe.wait_ge(i_R, met(n_l - 3))
                        w = max(width(t, b), 2 * P)
                        product(pe, ps[:, 2 + n_l % 4, 0:w], (qih[:, h, tok], qil[:, h, tok]),
                                (KIh[:, CH * b:CH * b + w], KIl[:, CH * b:CH * b + w]), True, True).then_inc(i_L, 1)
                        n_l += 1
            pe.wait_ge(i_xf, 1)
            for t in range(TILES):
                for j in range(4):
                    i = pe.matmul(ps[TOPK * j:TOPK * (j + 1), 6, TOPK * t:TOPK * (t + 1)], idxf[:, t, :], selt[:, j, :],
                                  start=t == 0, stop=t == TILES - 1)
            i.then_inc(i_xt, 1)

        def index_scalar(s, n):
            k0 = LNA[n]
            s.wait_ge(i_c, 80)
            s.copy(wirh[:], wir[:])
            s.copy(ihad[:], ihadr[:])
            s.copy(ikv_h[:], ikv_raw[:]).then_inc(i_rh, 1)
            for m in range(NTB):
                hs = slice(2 * m, min(2 * m + 2, NHI + 1))
                size = (hs.stop - hs.start) * KD * DI
                s.wait_ge(i_t, m + 1)
                s.mul(wih[:, hs], ps[:, 4 + m % 4, 0:size], HSC).then_inc(i_th, 1)
            with s.Fori(0, NCH) as c:
                ln_scalar(s, k0, c)
            with s.Fori(0, NCH) as c:
                s.wait_ge(i_ki, c + 1)
                s.copy(KIh[:, ds(CH * c, CH)], ps[:, 2, :]).then_inc(i_kh, 1)
            for t in range(TILES):
                s.wait_ge(i_kv, t + 1)
                if t >= 2:
                    s.wait_ge(i_kvd[t % 2], met(16 * (t // 2)))
                s.copy(iw[:, t, :], ps[:, 4 + t % 2, 2 * P:KVI])
                s.copy(kvs[:, t % 2, :], ps[:, 4 + t % 2, 0:2 * P]).then_inc(i_kve, 1)
            n_l = 0
            for c in range(NCH):
                for h in range(NHI):
                    s.wait_ge(i_q, NHI * c + h + 1)
                    s.wait_ge(i_L, met(LB[CT * c]))
                    s.copy(qih[:, h, :], ps[:, h % 2, :]).then_inc(i_qh, 1)
                if c == 0:
                    s.wait_ge(i_iw, 3)
                for t in range(CT * c, CT * (c + 1)):
                    for h, b in blocks(t):
                        s.wait_ge(i_L, n_l + 1)
                        s.wait_ge(i_A, met(n_l - RL + 1))
                        w = width(t, b)
                        s.activation(rl[:, n_l % RL, 0:w], ps[:, 2 + n_l % 4, 0:w], ACT.Relu,
                                     scale=iwa[:, t, h:h + 1]).then_inc(i_R, 1)
                        n_l += 1

        def index_vector(v, n):
            k0 = LNA[n]
            v.wait_ge(i_rh, 1)
            v.tensor_tensor(wirl[:], wir[:], wirh[:].bitcast(F32), ALU.subtract)
            v.tensor_tensor(ikv_l[:], ikv_raw[:], ikv_h[:].bitcast(F32), ALU.subtract).then_inc(i_rl, 1)
            for m in range(NTB):
                hs = slice(2 * m, min(2 * m + 2, NHI + 1))
                size = (hs.stop - hs.start) * KD * DI
                v.wait_ge(i_th, m + 1)
                v.scalar_tensor_tensor(out=wil[:, hs], in0=ps[:, 4 + m % 4, 0:size], scalar=HSC,
                                       in1=wih[:, hs].bitcast(F32), op0=ALU.mult, op1=ALU.subtract).then_inc(i_tl, 1)
            with v.Fori(0, NCH) as c:
                ln_vector(v, k0, c)
                ln_split(v, k0, c)
            with v.Fori(0, NCH) as c:
                v.wait_ge(i_kh, c + 1)
                v.tensor_tensor(KIl[:, ds(CH * c, CH)], ps[:, 2, :], KIh[:, ds(CH * c, CH)].bitcast(F32), ALU.subtract).then_inc(i_kl, 1)
            v.wait_ge(i_kve, TILES)
            v.tensor_scalar(iwa[:], iw[:], -1.0, None, ALU.mult).then_inc(i_iw, 1)
            v.tensor_scalar(iws[:], iw[:], 0.0, 2.0, ALU.is_ge, ALU.mult).then_inc(i_iw, 1)
            v.wait_ge(i_iw, 2)
            v.tensor_tensor(iwa[:], iwa[:], iw[:], ALU.max)
            v.tensor_scalar(iws[:], iws[:], 1.0, None, ALU.subtract).then_inc(i_iw, 1)
            v.wait_ge(i_iw, 3)

            def topk_step(t, k):
                W = (t + 1) * P
                scores = Isc[:, t % 2, 0:W]
                rnd = k // 3
                v.wait_ge(i_k, met(TOPK_STEPS * t + k))
                if k == 0:
                    v.wait_ge(i_A, met(LB[t + 1]))
                if k % 3 == 0:
                    i = v.max(v8[:, rnd % 2, :], scores)
                elif k % 3 == 1:
                    i = v.max_index(idx[:, t, 8 * rnd:8 * rnd + 8], v8[:, rnd % 2, :], scores)
                else:
                    i = v.match_replace(scores, v8[:, rnd % 2, :], scores, TAKEN)
                i.then_inc(i_k, 1)

            n_l = 0
            for c in range(NCH):
                for h in range(NHI):
                    v.wait_ge(i_qh, NHI * c + h + 1)
                    v.tensor_tensor(qil[:, h, :], ps[:, h % 2, :], qih[:, h, :].bitcast(F32), ALU.subtract).then_inc(i_ql, 1)
                for t in range(CT * c, CT * (c + 1)):
                    if t >= 2:
                        v.wait_ge(i_k, met(TOPK_STEPS * (t - 1)))
                    steps_done = 0
                    todo = blocks(t)
                    for at, (h, b) in enumerate(todo):
                        w = width(t, b)
                        acc = Isc[:, t % 2, CH * b:CH * b + w]
                        v.wait_ge(i_R, n_l + 1)
                        if h > 0:
                            v.wait_ge(i_A, met(n_l - c))
                        if h == 0 and b < c:
                            i = v.tensor_scalar(acc, rl[:, n_l % RL, 0:w], iws[:, t, h:h + 1], None, ALU.mult)
                        else:
                            i = v.scalar_tensor_tensor(out=acc, in0=rl[:, n_l % RL, 0:w], scalar=iws[:, t, h:h + 1],
                                                       in1=imask[:, CH - w:CH] if h == 0 else acc,
                                                       op0=ALU.mult, op1=ALU.add)
                        i.then_inc(i_A, 1)
                        n_l += 1
                        while t >= 1 and steps_done < (at + 1) * TOPK_STEPS // len(todo):
                            topk_step(t - 1, steps_done)
                            steps_done += 1
            for k in range(TOPK_STEPS):
                topk_step(TILES - 1, k)
            v.wait_ge(i_k, met(TOPK_STEPS * TILES))
            v.tensor_copy(idxf[:], idx[:]).then_inc(i_xf, 1)
            v.wait_ge(i_xt, 1)
            v.tensor_copy(idxT, ps[:, 6, :].rearrange("p (t g) -> p t g", g=TOPK))

        def index_gpsimd(g, n):
            with g.Fori(0, NCH) as c:
                ln_gpsimd(g, LNA[n], c)

        NHQ, HQ = 16, 128
        GT = 4
        GR = GT * NHQ
        BG = 8
        NB = CH // (GT * BG)
        TB = P // (GT * BG)
        SSC = float(HQ) ** -0.5
        s_ctx = ExitStack()
        swqh = sb("swqh", [P, NHQ, KD, HQ], F32R, s_ctx)
        swql = sb("swql", [P, NHQ, KD, HQ], F32R, s_ctx)
        swo = sb("swo", [P, NHQ, D], F32, s_ctx)
        smk = sb("smk", [8, P + 2 * CH], BF16, s_ctx)
        sidx = sb("sidx", [P, 2, P // GT], U32, s_ctx)
        RB = 4
        KV = sb("KV", [P, RB * BG, 2 * P], F32, s_ctx)
        KT = sb("KT", [P, BG, P], F32, s_ctx)
        smx = sb("smx", [P, 2, BG // 2], F32, s_ctx)
        snm = sb("snm", [P, 2, BG // 2], F32, s_ctx)
        ssum = sb("ssum", [P, 2, BG // 2], F32, s_ctx)
        srs = sb("srs", [P, 2, BG // 2], F32, s_ctx)
        sP = sb("sP", [P, 2, BG // 2, P], F32, s_ctx)
        sPT = sb("sPT", [P, BG // 2, P], F32, s_ctx)
        raw2_ctx = ExitStack()
        swr = sb("swr", [P, 2, NHQ // 2 * D], F32, raw2_ctx)
        smk_raw = sb("smk_raw", [8, P + 2 * CH], F32, raw2_ctx)
        raw2_ctx.close()
        qT = sb("qT", [P, CH, NHQ], F32, s_ctx)
        oT = sb("oT", [P, 2, P, NHQ], F32, s_ctx)
        s_ctx.close()
        s_w = [sem("s_w0"), sem("s_w1")]
        s_g = [sem(f"s_g{k}") for k in range(RB)]
        (s_c, s_wh, s_wl, s_q, s_qe, s_ix, s_kt, s_kte, s_s, s_nm, s_ex, s_rs, s_p, s_pt, s_pte, s_o, s_oe,
         s_y, s_x) = (
            sem(x) for x in ("s_c s_wh s_wl s_q s_qe s_ix s_kt s_kte s_s s_nm s_ex s_rs s_p s_pt s_pte s_o s_oe "
                             "s_y s_x").split())
        NW = 2

        def w_piece(m):
            return slice(NHQ // 2 * m, NHQ // 2 * (m + 1))

        def select_sync(sp, n):
            sp.dma_start(smk_raw[:], a["smask"]).then_inc(s_c, 16)
            for m in range(NW):
                sp.dma_start(swr[:, m, :], a["swq"][:, m]).then_inc(s_w[m], 16)
            sp.dma_start(swo[:], a["swo"]).then_inc(s_c, 16)

        def batches():
            for b in range(NB + 3):
                if b < NB:
                    yield "T", b
                if 1 <= b <= NB:
                    yield "Q", b - 1
                if 2 <= b <= NB + 1:
                    yield "W", b - 2
                if 3 <= b:
                    yield "O", b - 3
                    if (b - 3) % TB == TB - 1:
                        yield "Y", (b - 3) // TB

        def select_tensor(pe, n):
            pe.wait_ge(s_wl, NW)

            def chunk(c):
                for h in range(NHQ):
                    pe.wait_ge(s_qe, met(NHQ * c + h - 1))
                    pe.wait_ge(s_x, met(CT * c))
                    for k in range(KD):
                        i = product(pe, ps[:, 6 + h % 2, :], (swqh[:, h, k, :], swql[:, h, k, :]), xt(k, c), k == 0, k == KD - 1)
                    i.then_inc(s_q, 1)
                for kind, b in batches():
                    B = NB * c + b
                    if kind == "T":
                        pe.wait_ge(s_g[b % RB], 16 * BG * (NB // RB * c + b // RB + 1))
                        pe.wait_ge(s_kte, met(2 * B))
                        for g in range(BG):
                            i = pe.transpose(ps[:, g // 4, (g % 4) * P:(g % 4 + 1) * P], KV[:, BG * (b % RB) + g, 0:P], ident[:])
                            if g % 4 == 3:
                                i.then_inc(s_kt, 1)
                    elif kind == "Q":
                        pe.wait_ge(s_kte, 2 * B + 2)
                        pe.wait_ge(s_qe, NHQ * (c + 1))
                        pe.wait_ge(s_ex, met(B - 1))
                        rhs = smk[:, P:P + CH] if isinstance(c, int) and b == 0 else smk[:, P + CH:P + 2 * CH]
                        for g in range(BG):
                            pe.matmul(ps[GR * (g % 2):GR * (g % 2 + 1), 2 + b % 2, g // 2 * P:(g // 2 + 1) * P],
                                          qT[:, (b * BG + g) * GT:(b * BG + g + 1) * GT, :].rearrange("p t h -> p (t h)"),
                                          KT[:, g, :], start=g < 2, stop=False)
                        pe.matmul(ps[:, 2 + b % 2, :], smk[:, 0:P], rhs, start=False, stop=True).then_inc(s_s, 1)
                    elif kind == "W":
                        pe.wait_ge(s_p, B + 1)
                        pe.wait_ge(s_pte, B)
                        for m in range(BG // 2):
                            i = pe.transpose(ps[:, 4, m * P:(m + 1) * P], sP[:, b % 2, m, :], ident[:])
                        i.then_inc(s_pt, 1)
                    elif kind == "O":
                        pe.wait_ge(s_pte, B + 1)
                        pe.wait_ge(s_oe, B)
                        for g in range(BG):
                            i = pe.matmul(ps[:, 5, g * GR:(g + 1) * GR], KV[:, BG * (b % RB) + g, P:2 * P],
                                          sPT[:, g // 2, GR * (g % 2):GR * (g % 2 + 1)], start=True, stop=True)
                        i.then_inc(s_o, 1)
                    else:
                        pe.wait_ge(s_oe, NB * c + TB * (b + 1))
                        pe.wait_ge(s_x, met(CT * c + b - 1))
                        for h in range(NHQ):
                            i = pe.matmul(ps[:, 6 + b % 2, 0:D], oT[:, b % 2, :, h], swo[:, h, :], start=h == 0, stop=h == NHQ - 1)
                        i.then_inc(s_y, 1)
            chunk(0)
            with pe.Fori(1, NCH) as c:
                chunk(c)

        def select_scalar(s, n):
            s.wait_ge(s_c, 32)
            s.copy(smk[:], smk_raw[:])
            for m in range(NW):
                s.wait_ge(s_w[m], 16)
                s.copy(swqh[:, w_piece(m)], swr[:, m, :]).then_inc(s_wh, 1)
            s.wait_ge(s_wl, NW)

            def chunk(c):
                for h in range(NHQ):
                    s.wait_ge(s_q, NHQ * c + h + 1)
                    s.copy(qT[:, :, h], ps[:, 6 + h % 2, :]).then_inc(s_qe, 1)
                for kind, b in batches():
                    B = NB * c + b
                    if kind == "T":
                        for k in range(2):
                            s.wait_ge(s_kt, 2 * B + k + 1)
                            s.wait_ge(s_s, B)
                            s.copy(KT[:, 4 * k:4 * k + 4, :], ps[:, k, :]).then_inc(s_kte, 1)
                    elif kind == "Q":
                        s.wait_ge(s_nm, 2 * B + 2)
                        s.wait_ge(s_pt, met(B - 1))
                        for m in range(BG // 2):
                            i = s.activation(sP[:, b % 2, m, :], ps[:, 2 + b % 2, m * P:(m + 1) * P], ACT.Exp,
                                             bias=snm[:, b % 2, m:m + 1], scale=SSC, accum_out=ssum[:, b % 2, m:m + 1])
                        i.then_inc(s_ex, 1)
                    elif kind == "O":
                        s.wait_ge(s_o, B + 1)
                        s.wait_ge(s_y, met(CT * c + b // TB - 1))
                        s.copy(oT[:, b // TB % 2, (b % TB) * GT * BG:(b % TB + 1) * GT * BG, :], ps[:, 5, :]).then_inc(s_oe, 1)
            chunk(0)
            with s.Fori(1, NCH) as c:
                chunk(c)

        def select_vector(v, n):
            for m in range(NW):
                v.wait_ge(s_wh, m + 1)
                v.tensor_tensor(swql[:, w_piece(m)], swr[:, m, :], swqh[:, w_piece(m)].bitcast(F32), ALU.subtract).then_inc(s_wl, 1)

            def indices(c, r):
                v.wait_ge(s_kt, met(2 * (NB * c + TB * (r - 1)) if isinstance(c, int) and c == 0 and r < 1 else 2 * (NB * c + TB * (r - 1))))
                v.tensor_copy(sidx[:, r % 2, :], idxT[:, ds(CT * c + r, 1), :].rearrange("p a g -> p (a g)")).then_inc(s_ix, 1)

            def chunk(c):
                indices(c, 0)
                for kind, b in batches():
                    B = NB * c + b
                    if kind == "T" and b % TB == 0 and b // TB + 1 < CT:
                        indices(c, b // TB + 1)
                    if kind == "Q":
                        v.wait_ge(s_s, B + 1)
                        v.tensor_reduce(smx[:, b % 2, :], ps[:, 2 + b % 2, :].rearrange("p (m k) -> p m k", k=P), AX_X,
                                        ALU.max).then_inc(s_nm, 1)
                        v.wait_ge(s_nm, 2 * B + 1)
                        v.tensor_scalar(snm[:, b % 2, :], smx[:, b % 2, :], -SSC, None, ALU.mult).then_inc(s_nm, 1)
                        v.wait_ge(s_ex, B + 1)
                        v.reciprocal(srs[:, b % 2, :], ssum[:, b % 2, :]).then_inc(s_rs, 1)
                        v.wait_ge(s_rs, B + 1)
                        for m in range(BG // 2):
                            i = v.tensor_scalar(sP[:, b % 2, m, :], sP[:, b % 2, m, :], srs[:, b % 2, m:m + 1], None, ALU.mult)
                        i.then_inc(s_p, 1)
                    elif kind == "W":
                        v.wait_ge(s_pt, B + 1)
                        v.wait_ge(s_o, B)
                        v.tensor_copy(sPT[:], ps[:, 4, :].rearrange("p (m k) -> p m k", k=P)).then_inc(s_pte, 1)
                    elif kind == "Y":
                        v.wait_ge(s_y, CT * c + b + 1)
                        xr = X[:, ds(CT * c + b, 1), :].rearrange("p a d -> p (a d)")
                        v.tensor_tensor(xr, ps[:, 6 + b % 2, 0:D], xr, ALU.add).then_inc(s_x, 1)
            chunk(0)
            with v.Fori(1, NCH) as c:
                chunk(c)

        def select_gpsimd(g, n):
            def chunk(c):
                for b in range(NB):
                    B = NB * c + b
                    if b % TB == 0:
                        g.wait_ge(s_ix, CT * c + b // TB + 1)
                    g.wait_ge(s_o, met(B - RB + 1))
                    g.nop(nofuse=True)
                    for k in range(BG):
                        at = (b % TB) * BG + k
                        g.indirect_dma_start(KV[:, BG * (b % RB) + k, :], None, a["kv_scratch"],
                                             bass.IndirectOffsetOnAxis(sidx[:, b // TB % 2, at:at + 1], 0)).then_inc(s_g[b % RB], 16)
            chunk(0)
            with g.Fori(1, NCH) as c:
                chunk(c)

        plan, norms = [], 0
        for k, name in enumerate(stages):
            plan.append((name[:-1], int(name[-1]), k))
            if name[:-1] != "select":
                {"moe": LNC, "ffn": LNF}.get(name[:-1], LNA)[int(name[-1])] = norms
                norms += 1

        def run(eng, which):
            table = {
                "moe": {"sync": moe_sync, "scalar": moe_scalar, "vector": moe_vector, "gpsimd": moe_gpsimd, "tensor": moe_tensor},
                "ffn": {"sync": ffn_sync, "scalar": ffn_scalar, "vector": ffn_vector, "gpsimd": ffn_gpsimd, "tensor": ffn_tensor},
                "attn": {"sync": attn_sync, "scalar": attn_scalar, "vector": attn_vector, "gpsimd": attn_gpsimd, "tensor": attn_tensor},
                "index": {"sync": index_sync, "scalar": index_scalar, "vector": index_vector, "gpsimd": index_gpsimd, "tensor": index_tensor},
                "select": {"sync": select_sync, "scalar": select_scalar, "vector": select_vector, "gpsimd": select_gpsimd, "tensor": select_tensor},
            }
            for kind, n, k in plan:
                if k > 0:
                    eng.wait_ge(stage_done, 5 * k)
                table[kind][which](eng, n)
                eng.drain().then_inc(stage_done, 1)

        block = ctx.enter_context(nc.Block())

        @block.sync
        def _(sp):
            sp.dma_start(X[:], x_dram).then_inc(x_in, 16)
            sp.dma_start(ident[:], a["ident"]).then_inc(x_in, 16)
            run(sp, "sync")
            sp.wait_ge(stage_done, 5 * len(stages))
            sp.dma_start(out_dram, X[:]).then_inc(x_out, 16)
            sp.wait_ge(x_out, 16)

        @block.scalar
        def _(s):
            run(s, "scalar")

        @block.vector
        def _(v):
            v.memset(mhalf[:], -0.5)
            v.wait_ge(x_in, 32)
            run(v, "vector")

        @block.gpsimd
        def _(g):
            run(g, "gpsimd")

        @block.tensor
        def _(pe):
            pe.wait_ge(x_in, 32)
            run(pe, "tensor")


def lay_out(i):
    P_ = 128
    c = np.ascontiguousarray
    a = {k: np.asarray(v) for k, v in i.items()}
    E, F2, D = a["L0_ffn_w1"].shape
    I = F2 // 2
    g = {}
    g["x"] = c(a["L0_attn_x"][0])
    w1 = np.concatenate([a["L0_ffn_w1"][:, 0::2], a["L0_ffn_w1"][:, 1::2]], axis=1)
    g["w1"] = c(w1.reshape(E, F2, D // P_, P_).transpose(3, 0, 2, 1))
    g["w2"] = c(a["L0_ffn_w2"].reshape(E, D, I // P_, P_).transpose(3, 0, 2, 1))
    b1 = np.concatenate([a["L0_ffn_b1"][:, 0::2], a["L0_ffn_b1"][:, 1::2]], axis=1)
    g["b1"] = c(b1.reshape(E, F2 // P_, P_).transpose(2, 0, 1))
    g["b2"] = c(a["L0_ffn_b2"])
    g["gate_w"] = c(a["L0_ffn_gate_w"].reshape(E, D // P_, P_).transpose(2, 1, 0))
    g["gate_b"] = c(a["L0_ffn_gate_b"].reshape(E, 1))
    for w in ("W1", "W3"):
        t = a[f"L1_ffn_{w}"]
        g[w] = c(t.T.reshape(D // P_, P_, t.shape[0]).transpose(1, 0, 2))
    t = a["L1_ffn_W2"]
    g["W2"] = c(t.T.reshape(t.shape[1] // P_, P_, D).transpose(1, 0, 2))
    T = g["x"].shape[0]
    NHEAD, HD, RD, LAT = 16, 16, 64, 64
    wqd, wkvd, wkr = a["L0_attn_Wqd"], a["L0_attn_Wkvd"], a["L0_attn_Wkr"]
    swap = np.r_[RD // 2:RD, 0:RD // 2]
    wp = np.stack([np.tile(w, (1, 2)) for w in (wqd, wkvd, wkr, wkr[:, swap])], axis=1)
    g["wp"] = c(wp.reshape(D // P_, P_, 4, P_).transpose(1, 0, 2, 3))
    g["wv"] = c(np.tile(a["L0_attn_Wvu"], (2, 1)))
    wqr = a["L0_attn_Wqr"].reshape(LAT, NHEAD, RD)
    wqu, wku = (a[f"L0_attn_{n}"].reshape(LAT, NHEAD, HD) for n in ("Wqu", "Wku"))
    wh = np.zeros((LAT, NHEAD, 4, P_), np.float32)
    wh[:, :, 0] = np.tile(wqr, (1, 1, 2))
    wh[:, :, 1] = np.tile(wqr[:, :, swap], (1, 1, 2))
    for k, w in ((2, wqu), (3, wku)):
        for at in (RD, RD + HD, RD + 3 * HD):
            wh[:, :, k, at:at + HD] = w
    g["whead"] = c(np.tile(wh.reshape(LAT, NHEAD, 4 * P_), (2, 1, 1)))
    wog = np.zeros((NHEAD // 4, 4, 2 * HD, D), np.float32)
    wog[:, :, 0:HD] = a["L0_attn_Wo"].reshape(NHEAD // 4, 4, HD, D)
    g["wog"] = c(wog.reshape(NHEAD // 4, P_, D))
    freqs = 1.0 / 10000.0 ** (np.arange(0, RD, 2, dtype=np.float32) / RD)
    ang = np.outer(np.arange(T, dtype=np.float32), freqs).T
    cos, sin = np.cos(ang), np.sin(ang)
    g["rope"] = c(np.stack([np.tile(cos, (4, 1)), np.tile(np.concatenate([-sin, sin]), (2, 1))], axis=1).astype(np.float32))
    upper = np.triu(np.full((P_, P_), -1e30, np.float32), 1)
    g["cmask"] = c(np.stack([upper, upper.T], axis=1))
    rowm = np.zeros((P_, 1), np.float32)
    rowm[RD + HD:RD + 2 * HD] = rowm[RD + 3 * HD:] = -1.0
    g["rowm"] = rowm
    k = np.arange(P_)
    g["spread"] = c((k[:, None] == (k[None, :] // (2 * HD)) * 2 * HD + HD).astype(np.float32))
    h = np.ones((1, 1), np.float32)
    while h.shape[0] < P_:
        h = np.block([[h, h], [h, -h]])
    g["hadamard"] = c(h)
    wi = np.concatenate([a["L1_attn_wq_idx"], a["L1_attn_wk_idx"]], axis=1)
    g["wi"] = c(wi.T.reshape(-1, P_, D).transpose(1, 0, 2))
    wkvi = np.concatenate([a["L1_attn_wk"], a["L1_attn_wv"], a["L1_attn_w_iw"]], axis=1)
    g["wkvi"] = c(wkvi.reshape(D // P_, P_, -1).transpose(1, 0, 2))
    g["imask"] = c(np.concatenate([np.zeros((P_, 3 * P_), np.float32), upper], axis=1))
    t = np.arange(P_)
    g["selt"] = c((t[:, None, None] == 4 * np.arange(P_ // 4)[None, None, :] + np.arange(4)[None, :, None]).astype(np.float32))
    wq = a["L1_attn_wq"].reshape(D // P_, P_, 16, P_).transpose(1, 2, 0, 3)
    g["swq"] = c(wq.reshape(P_, 2, -1))
    wo = a["L1_attn_wo"].reshape(16, P_, D).transpose(1, 0, 2)
    g["swo"] = c(wo)
    row = np.arange(8)
    m = np.zeros((8, P_ + 2 * 512), np.float32)
    m[:, 0:P_] = row[:, None] == np.arange(P_)[None, :] // 16
    pair, tok, rank = np.meshgrid(np.arange(4), np.arange(4), np.arange(32), indexing="ij")
    for r_ in row:
        own = tok == r_ % 4
        m[r_, P_:P_ + 512] = np.where(own & (rank <= 8 * pair + r_), 0, -1e30).reshape(-1)
        m[r_, P_ + 512:] = np.where(own, 0, -1e30).reshape(-1)
    g["smask"] = m
    g["ident"] = np.eye(P_, dtype=np.float32)
    g["iota_e"] = np.tile(np.arange(E, dtype=np.float32), (P_, 1))
    return g


def scratch(laid):
    T, E = laid["x"].shape[0], laid["b2"].shape[0]
    return {"we_scratch0": ((E, T), F32), "we_scratch1": ((E, T), F32), "kv_scratch": ((T, 256), F32)}


def kernel(**inputs):
    import concourse.bacc as bacc
    from concourse.bass_utils import run_bass_kernel_spmd

    nc = bacc.Bacc("TRN2", target_bir_lowering=False, num_devices=1)
    laid = lay_out(inputs)
    T, D = laid["x"].shape
    args = {n: nc.dram_tensor(f"in_{n}", v.shape, mybir.dt.from_np(v.dtype), kind="ExternalInput").ap()
            for n, v in laid.items()}
    for n, (shape, dt) in scratch(laid).items():
        args[n] = nc.dram_tensor(n, shape, dt, kind="Internal").ap()
    out = nc.dram_tensor("out", (T, D), F32, kind="ExternalOutput").ap()
    build(nc, args, out)
    r = run_bass_kernel_spmd(nc, [{f"in_{n}": v for n, v in laid.items()}], core_ids=[0])
    return r.results[0]["out"].reshape(1, T, D)
```

```python
from contextlib import ExitStack

import concourse.bass as bass
from concourse import mybir
import numpy as np

F32 = mybir.dt.float32
F32R = mybir.dt.float32r
U32 = mybir.dt.uint32
ALU = mybir.AluOpType
ACT = mybir.ActivationFunctionType
AX_X = mybir.AxisListType.X

P = 128
EPS = 1e-5



def met(value):
    return max(value, 0) if isinstance(value, int) else value


def ds(start, size):
    if isinstance(start, int):
        return slice(start, start + size)
    return bass.ds(start, size)


def product(pe, out, lhs, rhs, start, stop):
    pe.matmul(out, lhs[0], rhs[0], start=start, stop=False)
    pe.matmul(out, lhs[0], rhs[1], start=False, stop=False)
    return pe.matmul(out, lhs[1], rhs[0], start=False, stop=stop)


def build(nc, a, out, stages=("moe0", "attn0", "moe1", "ffn0", "index1", "select1", "ffn1")):
    T, D = a["x"].shape
    TILES = T // P
    KD = D // P
    CH = 512
    NCH = T // CH
    CT = CH // P

    LNC, LNF, LNA = {}, {}, {}

    x_dram = a["x"].rearrange("(i p) d -> p i d", p=P)
    out_dram = out.rearrange("(i p) d -> p i d", p=P)

    ctx = ExitStack()
    with ctx:
        sem_names = {}

        def sem(name):
            if name not in sem_names:
                sem_names[name] = ctx.enter_context(nc.semaphore(name))
            return sem_names[name]

        def sb(name, shape, dt, c=None):
            return (c or ctx).enter_context(nc.sbuf_tensor(name, shape, dt))

        ps = ctx.enter_context(nc.psum_tensor("ps", [P, 8, CH], F32))

        X = sb("X", [P, TILES, D], F32)
        XTh = sb("XTh", [P, KD, T], F32R)
        XTl = sb("XTl", [P, KD, T], F32R)
        ident = sb("ident", [P, P], F32)
        xn = sb("xn", [P, CT, D], F32)
        stats = xn[:, CT - 1, 0:6 * TILES].rearrange("p (t s) -> p t s", s=6)
        mv = sb("mv", [P, TILES, 2], F32)
        rstd = sb("rstd", [P, TILES], F32)
        veps = sb("veps", [P, TILES], F32)
        mhalf = sb("mhalf", [P, TILES], F32)
        ln_ve = sem("ln_ve")
        TOPK_STEPS = 11
        idxT = xn[:, 0:2, :].rearrange("p a d -> p (a d)").bitcast(U32).rearrange("p (t g) -> p t g", g=P // 4)
        ln_stats, ln_mv, ln_rs, ln_xn = sem("ln_stats"), sem("ln_mv"), sem("ln_rs"), sem("ln_xn")
        ln_tr, ln_hi, ln_lo = sem("ln_tr"), sem("ln_hi"), sem("ln_lo")
        x_in, x_out = sem("x_in"), sem("x_out")
        stage_done = sem("stage_done")
        LN_BANK = 0

        def ln_vector(v, n):
            for t in range(TILES):
                i = v.bn_stats(stats[:, t, :], X[:, t, :])
            i.then_inc(ln_stats, 1)
            v.wait_ge(ln_stats, n + 1)
            for t in range(TILES):
                i = v.bn_aggr(mv[:, t, :], stats[:, t, :])
            i.then_inc(ln_mv, 1)
            v.wait_ge(ln_rs, n + 1)
            for c in range(NCH):
                q = NCH * n + c
                v.wait_ge(ln_tr, KD * q)
                for r in range(CT):
                    t = CT * c + r
                    i = v.tensor_scalar(xn[:, r, :], X[:, t, :], mv[:, t, 0:1], rstd[:, t:t + 1], ALU.subtract, ALU.mult)
                i.then_inc(ln_xn, 1)
                if c >= 1:
                    ln_split(v, n, c - 1)
            ln_split(v, n, NCH - 1)

        def ln_gpsimd(g, n):
            g.wait_ge(ln_mv, n + 1)
            g.tensor_scalar(veps[:], mv[:, :, 1], EPS, None, ALU.add).then_inc(ln_ve, 1)
            g.wait_ge(ln_ve, n + 1)
            g.tensor_tensor(rstd[:], veps[:], mhalf[:], ALU.pow).then_inc(ln_rs, 1)

        def ln_bank(c, k):
            return ps[:, LN_BANK + KD * (c % 2) + k, :]

        def ln_split(v, n, c):
            q = NCH * n + c
            for k in range(KD):
                v.wait_ge(ln_hi, KD * q + k + 1)
                v.tensor_tensor(XTl[:, k, CH * c:CH * (c + 1)], ln_bank(c, k), XTh[:, k, CH * c:CH * (c + 1)].bitcast(F32),
                                ALU.subtract).then_inc(ln_lo, 1)

        def ln_tensor(pe, n, c):
            q = NCH * n + c
            pe.wait_ge(ln_xn, q + 1)
            pe.wait_ge(ln_lo, KD * max(q - 1, 0))
            for k in range(KD):
                for r in range(CT):
                    i = pe.transpose(ln_bank(c, k)[:, r * P:(r + 1) * P], xn[:, r, k * P:(k + 1) * P], ident[:])
                i.then_inc(ln_tr, 1)

        def ln_scalar(s, n, c):
            q = NCH * n + c
            for k in range(KD):
                s.wait_ge(ln_tr, KD * q + k + 1)
                s.copy(XTh[:, k, CH * c:CH * (c + 1)], ln_bank(c, k)).then_inc(ln_hi, 1)

        def xt(k, c):
            return XTh[:, k, ds(CH * c, CH)], XTl[:, k, ds(CH * c, CH)]

        E = a["b2"].shape[0]
        I = a["w2"].shape[2] * P
        JI = I // P
        UNITS = E * JI
        moe_ctx = ExitStack()
        w1raw = sb("w1raw", [P, 2, KD, 2 * I], F32, moe_ctx)
        w2raw = sb("w2raw", [P, 2, JI, D], F32, moe_ctx)
        w1h = sb("w1h", [P, E, KD, 2 * I], F32R, moe_ctx)
        w1l = sb("w1l", [P, E, KD, 2 * I], F32R, moe_ctx)
        w2h = sb("w2h", [P, E, JI, D], F32R, moe_ctx)
        w2l = sb("w2l", [P, E, JI, D], F32R, moe_ctx)
        b1 = sb("b1", [P, E, 2 * JI], F32, moe_ctx)
        b1s = sb("b1s", [P, E, 2 * JI], F32, moe_ctx)
        b1p = sb("b1p", [P, E, 2 * JI], F32, moe_ctx)
        b2 = sb("b2", [E, D], F32, moe_ctx)
        gwraw = sb("gwraw", [P, KD, E], F32, moe_ctx)
        gwh = sb("gwh", [P, KD, E], F32R, moe_ctx)
        gwl = sb("gwl", [P, KD, E], F32R, moe_ctx)
        gb = sb("gb", [E, 1], F32, moe_ctx)
        gap = sb("gap", [P, TILES, 2], F32, moe_ctx)
        gate = sb("gate", [P, TILES, 2], F32, moe_ctx)
        we = sb("we", [P, TILES, E], F32, moe_ctx)
        weTc = sb("weTc", [E, CH], F32, moe_ctx)
        iota_e = sb("iota_e", [P, E], F32, moe_ctx)
        WR = 4
        web = sb("web", [P, WR, CH], F32, moe_ctx)
        if T != WR * CH:
            raise ValueError("the transposed routing weights take the ring's place")
        weT = web[0:E].rearrange("e w t -> e (w t)")
        lgT = weT
        pick = xn[:, 0, 0:2 * TILES * E].rearrange("p (t m e) -> p t m e", m=2, e=E)
        top, topf, topi = (xn[:, 1 + k // 2, 8 * TILES * (k % 2):8 * TILES * (k % 2 + 1)] for k in range(3))
        top, topf, topi = (x.rearrange("p (t e) -> p t e", e=8) for x in (top, topf, topi.bitcast(U32)))
        sig = sb("sig", [P, 2, CH], F32, moe_ctx)
        gt = sb("gt", [P, 2, CH], F32, moe_ctx)
        lt = sb("lt", [P, 2, CH], F32, moe_ctx)
        y = sb("y", [P, 2, CH], F32, moe_ctx)
        yh = sb("yh", [P, 4, CH], F32R, moe_ctx)
        yl = sb("yl", [P, 4, CH], F32R, moe_ctx)
        moe_ctx.close()
        w1_dram, w2_dram = a["w1"], a["w2"]
        we_scratch = [a["we_scratch0"], a["we_scratch1"]]
        m_w, m_wh, m_wl, m_b, m_bs = [sem("m_w0"), sem("m_w1")], sem("m_wh"), sem("m_wl"), sem("m_b"), sem("m_bs")
        g_lg, g_lgs, g_tr, g_top, g_topi, g_gap, g_sig, g_pk, g_pg, g_we, g_weT, g_weTs, g_st = (
            sem(n) for n in "g_lg g_lgs g_tr g_top g_topi g_gap g_sig g_pk g_pg g_we g_weT g_weTs g_st".split())
        m_wtc, m_g, m_l, m_sig, m_gt, m_lt, m_y, m_yh, m_yl, m_dn, m_x = (
            sem(n) for n in "m_wtc m_g m_l m_sig m_gt m_lt m_y m_yh m_yl m_dn m_x".split())
        m_web = [sem(f"m_web{k}") for k in range(WR)]
        O_BANK, GL_BANK = 2, 4

        def o_tile(r):
            return ps[:, O_BANK + r // 2, (r % 2) * D:(r % 2 + 1) * D]

        def moe_sync(sp, n):
            def weights(e):
                if e >= 2:
                    sp.wait_ge(m_wl, E * n + e - 1)
                sp.dma_start(w1raw[:, e % 2], w1_dram[:, e]).then_inc(m_w[e % 2], 16)
                sp.dma_start(w2raw[:, e % 2], w2_dram[:, e]).then_inc(m_w[e % 2], 16)

            def routing(c, e):
                q = NCH * n + c
                sp.wait_ge(m_y, met(UNITS * q + JI * (e - WR + 1)))
                sp.dma_start(web[:, e % WR, :], we_scratch[n][e, ds(CH * c, CH)].partition_broadcast(P)).then_inc(m_web[e % WR], 16)

            def biases(c):
                q = NCH * n + c
                sp.wait_ge(m_dn, met(UNITS * q))
                sp.dma_start(weTc[:], we_scratch[n][:, ds(CH * c, CH)]).then_inc(m_wtc, 16)

            sp.dma_start(b1[:], a["b1"]).then_inc(m_b, 16)
            sp.dma_start(b2[:], a["b2"]).then_inc(m_b, 16)
            sp.dma_start(gwraw[:], a["gate_w"]).then_inc(m_b, 16)
            sp.dma_start(gb[:], a["gate_b"]).then_inc(m_b, 16)
            sp.dma_start(iota_e[:], a["iota_e"]).then_inc(m_b, 16)
            weights(0)
            weights(1)
            sp.wait_ge(g_weTs, n + 1)
            sp.dma_start(we_scratch[n], weT).then_inc(g_st, 16)
            sp.wait_ge(g_st, 16 * (n + 1))
            for e in range(WR):
                routing(0, e)
            for e in range(2, E):
                weights(e)
                if e >= WR:
                    routing(0, e)
            biases(0)
            with sp.Fori(1, NCH) as c:
                for e in range(E):
                    routing(c, e)
                biases(c)

        def moe_scalar(s, n):
            s.wait_ge(m_b, 80 * (n + 1))
            s.copy(gwh[:], gwraw[:]).then_inc(m_bs, 1)
            s.wait_ge(m_b, 80 * (n + 1))
            s.mul(b1s[:], b1[:], 1.702).then_inc(m_bs, 1)
            def logits(c):
                s.wait_ge(g_lg, NCH * n + c + 1)
                s.activation(lgT[:, CH * c:CH * (c + 1)], ps[0:E, GL_BANK + c % 2, :], ACT.Identity, bias=gb[:]).then_inc(g_lgs, 1)

            for c in range(NCH):
                ln_scalar(s, LNC[n], c)
                if c >= 1:
                    logits(c - 1)
            logits(NCH - 1)

            def weights(e):
                s.wait_ge(m_w[e % 2], 32 * (E // 2 * n + e // 2 + 1))
                s.copy(w1h[:, e], w1raw[:, e % 2])
                s.copy(w2h[:, e], w2raw[:, e % 2]).then_inc(m_wh, 1)

            weights(0)
            weights(1)
            s.wait_ge(g_gap, n + 1)
            s.activation(gate[:], gap[:], ACT.Sigmoid).then_inc(g_sig, 1)
            s.wait_ge(g_weT, n + 1)
            s.copy(weT, ps[0:E, 0:T // CH, :].rearrange("e b t -> e (b t)")).then_inc(g_weTs, 1)

            def sigmoid(q, u):
                U = UNITS * q + u
                e, j = u // JI, u % JI
                s.wait_ge(m_g, U + 1)
                s.wait_ge(m_gt, met(U - 1))
                s.activation(sig[:, u % 2, :], ps[:, GL_BANK + 2 * (u % 2), :], ACT.Sigmoid,
                             bias=b1s[:, e, j:j + 1], scale=1.702).then_inc(m_sig, 1)

            def high(q, u):
                U = UNITS * q + u
                s.wait_ge(m_y, U + 1)
                s.wait_ge(m_dn, met(U - 3))
                s.copy(yh[:, u % 4, :], y[:, u % 2, :]).then_inc(m_yh, 1)

            def chunk(c, first=False):
                q = NCH * n + c
                for u in range(UNITS):
                    sigmoid(q, u)
                    if u >= 1:
                        high(q, u - 1)
                    elif not first:
                        high(q - 1, UNITS - 1)
                    if first and u % 2 == 0 and 2 <= u // 2 + 1 < E:
                        weights(u // 2 + 1)

            chunk(0, first=True)
            with s.Fori(1, NCH) as c:
                chunk(c)
            high(NCH * (n + 1) - 1, UNITS - 1)

        def gate_tensor(pe, n, c):
            if c < NCH:
                pe.wait_ge(m_bs, 3 * (n + 1))
                pe.wait_ge(ln_lo, KD * (NCH * LNC[n] + c + 1))
                pe.wait_ge(g_lgs, NCH * n + max(c - 1, 0))
                for k in range(KD):
                    i = product(pe, ps[0:E, GL_BANK + c % 2, :], (gwh[:, k, :], gwl[:, k, :]), xt(k, c), k == 0, k == KD - 1)
                i.then_inc(g_lg, 1)
            if c >= 1:
                pe.wait_ge(g_lgs, NCH * n + c)
                for t in range(CT * (c - 1), CT * c):
                    i = pe.transpose(ps[:, GL_BANK + 3, t * E:(t + 1) * E], lgT[:, t * P:(t + 1) * P], ident[0:E, 0:E])
                i.then_inc(g_tr, 1)

        def gate_vector(v, n):
            lg = ps[:, GL_BANK + 3, 0:TILES * E].rearrange("p (t e) -> p t e", e=E)
            v.wait_ge(g_tr, NCH * (n + 1))
            for t in range(TILES):
                i = v.max(top[:, t, :], lg[:, t, :])
            i.then_inc(g_top, 1)
            v.wait_ge(g_top, n + 1)
            for t in range(TILES):
                i = v.max_index(topi[:, t, :], top[:, t, :], lg[:, t, :])
            v.tensor_tensor(gap[:, :, 0], top[:, :, 0], top[:, :, 1], ALU.subtract)
            v.tensor_tensor(gap[:, :, 1], top[:, :, 1], top[:, :, 0], ALU.subtract).then_inc(g_gap, 1)
            v.wait_ge(g_gap, n + 1)
            v.tensor_copy(topf, topi).then_inc(g_topi, 1)
            v.wait_ge(g_topi, n + 1)
            for t in range(TILES):
                for m in range(2):
                    i = v.tensor_scalar(pick[:, t, m, :], iota_e[:], topf[:, t, m:m + 1], None, ALU.is_equal)
            i.then_inc(g_pk, 1)
            v.wait_ge(g_sig, n + 1)
            v.wait_ge(g_pk, n + 1)
            for t in range(TILES):
                i = v.tensor_scalar(we[:, t, :], pick[:, t, 0, :], gate[:, t, 0:1], None, ALU.mult)
            i.then_inc(g_pg, 1)
            v.wait_ge(g_pg, n + 1)
            for t in range(TILES):
                i = v.scalar_tensor_tensor(out=we[:, t, :], in0=pick[:, t, 1, :], scalar=gate[:, t, 1:2],
                                           in1=we[:, t, :], op0=ALU.mult, op1=ALU.add)
            i.then_inc(g_we, 1)

        def moe_vector(v, n):
            v.wait_ge(m_bs, 3 * n + 2)
            v.tensor_tensor(gwl[:], gwraw[:], gwh[:].bitcast(F32), ALU.subtract).then_inc(m_bs, 1)
            v.tensor_scalar(b1p[:], b1[:], 1.0, None, ALU.add)
            ln_vector(v, LNC[n])

            def weights(e):
                v.wait_ge(m_wh, E * n + e + 1)
                v.tensor_tensor(w1l[:, e], w1raw[:, e % 2], w1h[:, e].bitcast(F32), ALU.subtract)
                v.tensor_tensor(w2l[:, e], w2raw[:, e % 2], w2h[:, e].bitcast(F32), ALU.subtract).then_inc(m_wl, 1)

            weights(0)
            gate_vector(v, n)
            weights(1)

            def glu(q, u):
                U = UNITS * q + u
                e, j = u // JI, u % JI
                v.wait_ge(m_sig, U + 1)
                v.scalar_tensor_tensor(out=gt[:, u % 2, :], in0=ps[:, GL_BANK + 2 * (u % 2), :],
                                       scalar=b1[:, e, j:j + 1], in1=sig[:, u % 2, :],
                                       op0=ALU.add, op1=ALU.mult).then_inc(m_gt, 1)
                v.wait_ge(m_l, U + 1)
                v.wait_ge(m_gt, U + 1)
                v.wait_ge(m_y, met(U - 1))
                v.scalar_tensor_tensor(out=lt[:, u % 2, :], in0=ps[:, GL_BANK + 2 * (u % 2) + 1, :],
                                       scalar=b1p[:, e, JI + j:JI + j + 1], in1=gt[:, u % 2, :],
                                       op0=ALU.add, op1=ALU.mult).then_inc(m_lt, 1)

            def low(q, u):
                U = UNITS * q + u
                v.wait_ge(m_yh, U + 1)
                v.tensor_tensor(yl[:, u % 4, :], y[:, u % 2, :], yh[:, u % 4, :].bitcast(F32),
                                ALU.subtract).then_inc(m_yl, 1)

            def residual(q, c):
                v.wait_ge(m_dn, UNITS * (q + 1))
                for r in range(CT):
                    xr = X[:, ds(CT * c + r, 1), :].rearrange("p a d -> p (a d)")
                    i = v.scalar_tensor_tensor(out=xr, in0=o_tile(r), scalar=0.5, in1=xr, op0=ALU.mult, op1=ALU.add)
                i.then_inc(m_x, 1)

            def chunk(c, first=False):
                q = NCH * n + c
                for u in range(UNITS):
                    glu(q, u)
                    if u >= 1:
                        low(q, u - 1)
                    elif not first:
                        low(q - 1, UNITS - 1)
                    if u == 1 and not first:
                        residual(q - 1, c - 1)
                    if first and u % 2 == 0 and 2 <= u // 2 + 1 < E:
                        weights(u // 2 + 1)

            chunk(0, first=True)
            with v.Fori(1, NCH) as c:
                chunk(c)
            low(NCH * (n + 1) - 1, UNITS - 1)
            residual(NCH * (n + 1) - 1, NCH - 1)

        def moe_gpsimd(g, n):
            ln_gpsimd(g, LNC[n])

            def chunk(c):
                q = NCH * n + c
                for u in range(UNITS):
                    U = UNITS * q + u
                    if u % JI == 0:
                        g.wait_ge(m_web[u // JI % WR], 16 * (E // WR * q + u // JI // WR + 1))
                    g.wait_ge(m_lt, U + 1)
                    g.wait_ge(m_yl, met(U - 1))
                    g.tensor_tensor(y[:, u % 2, :], lt[:, u % 2, :], web[:, u // JI % WR, :], ALU.mult).then_inc(m_y, 1)
            chunk(0)
            with g.Fori(1, NCH) as c:
                chunk(c)

        def moe_tensor(pe, n):
            for c in range(NCH):
                ln_tensor(pe, LNC[n], c)
                if c >= 1:
                    gate_tensor(pe, n, c - 1)
            gate_tensor(pe, n, NCH - 1)
            gate_tensor(pe, n, NCH)

            def routing_weights():
                pe.wait_ge(g_we, n + 1)
                for t in range(TILES):
                    i = pe.transpose(ps[0:E, t // CT, (t % CT) * P:(t % CT + 1) * P], we[:, t, :], ident[:])
                i.then_inc(g_weT, 1)
                pe.wait_ge(g_weTs, n + 1)

            def up(q, c, u):
                U = UNITS * q + u
                e, j = u // JI, u % JI
                pe.wait_ge(m_lt, met(U - 1))
                if j == 0:
                    pe.wait_ge(m_wl, E * n + e + 1)
                for half, signal in ((0, m_g), (1, m_l)):
                    f = half * I + j * P
                    for k in range(KD):
                        i = product(pe, ps[:, GL_BANK + 2 * (u % 2) + half, :],
                                    (w1h[:, e, k, f:f + P], w1l[:, e, k, f:f + P]), xt(k, c), k == 0, k == KD - 1)
                    i.then_inc(signal, 1)

            def down(q, u):
                U = UNITS * q + u
                e, j = u // JI, u % JI
                pe.wait_ge(m_yl, U + 1)
                if u == 0:
                    pe.wait_ge(m_x, met(q))
                for r in range(CT):
                    i = product(pe, o_tile(r), (yh[:, u % 4, r * P:(r + 1) * P], yl[:, u % 4, r * P:(r + 1) * P]),
                                (w2h[:, e, j, :], w2l[:, e, j, :]), u == 0 and r % 2 == 0, False)
                if u < UNITS - 1:
                    i.then_inc(m_dn, 1)
                else:
                    pe.wait_ge(m_wtc, 16 * (q + 1))
                    for r in range(CT):
                        i = pe.matmul(o_tile(r), weTc[:, r * P:(r + 1) * P], b2[:], start=False, stop=r % 2 == 1)
                    i.then_inc(m_dn, 1)

            def chunk(c, first=False):
                q = NCH * n + c
                for u in range(UNITS):
                    if first and u == 1:
                        pe.wait_ge(g_gap, n + 1)
                    up(q, c, u)
                    if first and u == 1:
                        routing_weights()
                    if u >= 2:
                        down(q, u - 2)
                    elif not first:
                        down(q - 1, UNITS - 2 + u)

            chunk(0, first=True)
            with pe.Fori(1, NCH) as c:
                chunk(c)
            down(NCH * (n + 1) - 1, UNITS - 2)
            down(NCH * (n + 1) - 1, UNITS - 1)

        F = a["W1"].shape[2]
        FB = F // P
        f_ctx = ExitStack()
        fraw = [sb(f"f{w}raw", [P, KD, F], F32, f_ctx) for w in "13"]
        fh = [sb(f"f{w}h", [P, KD, F], F32R, f_ctx) for w in "13"]
        fl = [sb(f"f{w}l", [P, KD, F], F32R, f_ctx) for w in "13"]
        f2raw = sb("f2raw", [P, FB, D], F32, f_ctx)
        f2rh = sb("f2rh", [P, FB, D], F32R, f_ctx)
        f2rl = sb("f2rl", [P, FB, D], F32R, f_ctx)
        f2a = sb("f2a", [P, FB, D], F32, f_ctx)
        f2b = sb("f2b", [P, FB, D], F32, f_ctx)
        f2h = sb("f2h", [P, FB, D], F32R, f_ctx)
        f2l = sb("f2l", [P, FB, D], F32R, f_ctx)
        hadr = sb("hadr", [P, P], F32, f_ctx)
        had = sb("had", [P, P], F32R, f_ctx)
        fsig = sb("fsig", [P, 2, CH], F32, f_ctx)
        fg = sb("fg", [P, 2, CH], F32, f_ctx)
        fy = sb("fy", [P, 2, CH], F32, f_ctx)
        fyh = sb("fyh", [P, 4, CH], F32R, f_ctx)
        fyl = sb("fyl", [P, 4, CH], F32R, f_ctx)
        f_ctx.close()
        f_w2, f_w13, f_h2, f_l2, f_h13, f_l13, f_had, f_hev, f_bf, f_2h, f_2l = (
            sem(n) for n in "f_w2 f_w13 f_h2 f_l2 f_h13 f_l13 f_had f_hev f_bf f_2h f_2l".split())
        f_g, f_l, f_sig, f_gt, f_y, f_yh, f_yl, f_dn, f_x = (
            sem(n) for n in "f_g f_l f_sig f_gt f_y f_yh f_yl f_dn f_x".split())
        HB = FB * D // CH
        BF = FB.bit_length() - 1

        def ffn_sync(sp, n):
            sp.dma_start(fraw[0][:], a["W1"]).then_inc(f_w13, 16)
            sp.dma_start(fraw[1][:], a["W3"]).then_inc(f_w13, 16)
            sp.dma_start(hadr[:], a["hadamard"]).then_inc(f_w2, 16)
            sp.dma_start(f2raw[:], a["W2"]).then_inc(f_w2, 16)

        def ffn_scalar(s, n):
            for c in range(NCH):
                ln_scalar(s, LNF[n], c)
                if c == 1:
                    s.wait_ge(f_w2, 32 * (n + 1))
                    s.copy(had[:], hadr[:])
                    s.copy(f2rh[:], f2raw[:]).then_inc(f_h2, 1)
                if c >= 2:
                    s.wait_ge(f_w13, 32 * (n + 1))
                    s.copy(fh[c - 2][:], fraw[c - 2][:]).then_inc(f_h13, 1)
            for b in range(HB):
                s.wait_ge(f_had, n + 1)
                s.mul(f2a[:, 2 * b:2 * b + 2, :], ps[:, 4 + b, :], float(F) ** -0.5).then_inc(f_hev, 1)

            def sigmoid(q, u):
                U = FB * q + u
                s.wait_ge(f_g, U + 1)
                s.wait_ge(f_gt, met(U - 1))
                s.activation(fsig[:, u % 2, :], ps[:, GL_BANK + 2 * (u % 2), :], ACT.Sigmoid).then_inc(f_sig, 1)

            def high(q, u):
                U = FB * q + u
                s.wait_ge(f_y, U + 1)
                s.wait_ge(f_dn, met(U - 3))
                s.copy(fyh[:, u % 4, :], fy[:, u % 2, :]).then_inc(f_yh, 1)

            def chunk(c, first=False):
                q = NCH * n + c
                for u in range(FB):
                    sigmoid(q, u)
                    if first and u == 0:
                        s.wait_ge(f_bf, BF * (n + 1))
                        s.copy(f2h[:], f2b[:]).then_inc(f_2h, 1)
                    if u >= 1:
                        high(q, u - 1)
                    elif not first:
                        high(q - 1, FB - 1)

            chunk(0, first=True)
            with s.Fori(1, NCH) as c:
                chunk(c)
            high(NCH * (n + 1) - 1, FB - 1)

        def ffn_vector(v, n):
            ln_vector(v, LNF[n])
            for w in range(2):
                v.wait_ge(f_h13, 2 * n + w + 1)
                v.tensor_tensor(fl[w][:], fraw[w][:], fh[w][:].bitcast(F32), ALU.subtract).then_inc(f_l13, 1)
            v.wait_ge(f_hev, HB * (n + 1))
            bufs = [f2a, f2b]
            for k in range(BF):
                src, dst = (t[:].rearrange("p (a two h) d -> p a two (h d)", two=2, h=1 << k)
                            for t in (bufs[k % 2], bufs[(k + 1) % 2]))
                if k >= 1:
                    v.wait_ge(f_bf, met(BF * n + k))
                v.tensor_tensor(dst[:, :, 0], src[:, :, 0], src[:, :, 1], ALU.add)
                v.tensor_tensor(dst[:, :, 1], src[:, :, 0], src[:, :, 1], ALU.subtract).then_inc(f_bf, 1)
            assert BF % 2 == 1
            v.wait_ge(f_2h, n + 1)
            v.tensor_tensor(f2l[:], f2b[:], f2h[:].bitcast(F32), ALU.subtract).then_inc(f_2l, 1)

            def glu(q, u):
                U = FB * q + u
                v.wait_ge(f_sig, U + 1)
                v.tensor_tensor(fg[:, u % 2, :], ps[:, GL_BANK + 2 * (u % 2), :], fsig[:, u % 2, :],
                                ALU.mult).then_inc(f_gt, 1)
                v.wait_ge(f_l, U + 1)
                v.wait_ge(f_gt, U + 1)
                v.wait_ge(f_yl, met(U - 1))
                v.tensor_tensor(fy[:, u % 2, :], ps[:, GL_BANK + 2 * (u % 2) + 1, :], fg[:, u % 2, :],
                                ALU.mult).then_inc(f_y, 1)

            def residual(q, c):
                v.wait_ge(f_dn, FB * (q + 1))
                for r in range(CT):
                    xr = X[:, ds(CT * c + r, 1), :].rearrange("p a d -> p (a d)")
                    i = v.scalar_tensor_tensor(out=xr, in0=o_tile(r), scalar=0.5, in1=xr, op0=ALU.mult, op1=ALU.add)
                i.then_inc(f_x, 1)

            def chunk(c, first=False):
                q = NCH * n + c
                for u in range(FB):
                    glu(q, u)
                    if u == 1 and not first:
                        residual(q - 1, c - 1)

            chunk(0, first=True)
            with v.Fori(1, NCH) as c:
                chunk(c)
            residual(NCH * (n + 1) - 1, NCH - 1)

        def ffn_gpsimd(g, n):
            ln_gpsimd(g, LNF[n])

            g.wait_ge(f_h2, n + 1)
            g.tensor_tensor(f2rl[:], f2raw[:], f2rh[:].bitcast(F32), ALU.subtract).then_inc(f_l2, 1)

            def chunk(c):
                q = NCH * n + c
                for u in range(FB):
                    U = FB * q + u
                    g.wait_ge(f_yh, U + 1)
                    g.tensor_tensor(fyl[:, u % 4, :], fy[:, u % 2, :], fyh[:, u % 4, :].bitcast(F32),
                                    ALU.subtract).then_inc(f_yl, 1)
            chunk(0)
            with g.Fori(1, NCH) as c:
                chunk(c)

        def ffn_tensor(pe, n):
            for c in range(NCH):
                ln_tensor(pe, LNF[n], c)
            pe.wait_ge(f_l2, n + 1)
            for b in range(HB):
                pe.matmul(ps[:, 4 + b, :], had[:], f2rh[:, 2 * b:2 * b + 2, :], start=True, stop=False)
                i = pe.matmul(ps[:, 4 + b, :], had[:], f2rl[:, 2 * b:2 * b + 2, :], start=False, stop=True)
            i.then_inc(f_had, 1)
            pe.wait_ge(ln_lo, KD * NCH * (LNF[n] + 1))
            pe.wait_ge(f_l13, 2 * (n + 1))
            pe.wait_ge(f_hev, HB * (n + 1))

            def up(q, c, u):
                U = FB * q + u
                pe.wait_ge(f_y, met(U - 1))
                for half, signal in ((0, f_g), (1, f_l)):
                    for k in range(KD):
                        i = product(pe, ps[:, GL_BANK + 2 * (u % 2) + half, :],
                                    (fh[half][:, k, u * P:(u + 1) * P], fl[half][:, k, u * P:(u + 1) * P]),
                                    xt(k, c), k == 0, k == KD - 1)
                    i.then_inc(signal, 1)

            def down(q, u):
                U = FB * q + u
                pe.wait_ge(f_yl, U + 1)
                if u == 0:
                    pe.wait_ge(f_2l, n + 1)
                    pe.wait_ge(f_x, met(q))
                for r in range(CT):
                    i = product(pe, o_tile(r), (fyh[:, u % 4, r * P:(r + 1) * P], fyl[:, u % 4, r * P:(r + 1) * P]),
                                (f2h[:, u, :], f2l[:, u, :]), u == 0 and r % 2 == 0, u == FB - 1 and r % 2 == 1)
                i.then_inc(f_dn, 1)

            def chunk(c, first=False):
                q = NCH * n + c
                for u in range(FB):
                    up(q, c, u)
                    if u >= 2:
                        down(q, u - 2)
                    elif not first:
                        down(q - 1, FB - 2 + u)

            chunk(0, first=True)
            with pe.Fori(1, NCH) as c:
                chunk(c)
            down(NCH * (n + 1) - 1, FB - 2)
            down(NCH * (n + 1) - 1, FB - 1)

        NHEAD, HD, RD, LAT = 16, 16, 64, 64
        GH = 4
        NG = NHEAD // GH
        SCALE = float(1.0 / np.sqrt(np.float32(HD + RD)))
        BF16 = mybir.dt.bfloat16
        a_ctx = ExitStack()
        QL = sb("QL", [P, T], F32R, a_ctx)
        CK = sb("CK", [P, T], F32R, a_ctx)
        KB = sb("KB", [P, T], F32R, a_ctx)
        V = sb("V", [P, TILES, D], F32, a_ctx)
        rb = sb("rb", [P, 2, CH], F32, a_ctx)
        rr = sb("rr", [P, 2, CH], F32, a_ctx)
        cs = sb("cs", [P, 2, 2, CH], F32, a_ctx)
        tmpq = sb("tmpq", [P, 2, CH], F32R, a_ctx)
        tmpk = sb("tmpk", [P, 2, 2 * CH], F32R, a_ctx)
        cm_bf = sb("cm_bf", [P, 3, P], BF16, a_ctx)
        rowm = sb("rowm", [P, 1], F32, a_ctx)
        mp = sb("mp", [P, GH * CT, 2], F32, a_ctx)
        mcol = sb("mcol", [P, GH * CT], F32, a_ctx)
        mrow = sb("mrow", [GH * CT, P], F32R, a_ctx)
        whr = sb("whr", [P, 2, CH], F32, a_ctx)
        whh = sb("whh", [P, GH, CH], F32R, a_ctx)
        whl = sb("whl", [P, GH, CH], F32R, a_ctx)
        wor = sb("wor", [P, D], F32, a_ctx)
        woh = sb("woh", [P, D], F32R, a_ctx)
        wol = sb("wol", [P, D], F32R, a_ctx)
        VG = sb("VG", [P, TILES, GH, 2 * HD], F32, a_ctx)
        qA = sb("qA", [P, 2, GH, CH], F32R, a_ctx)
        qB = sb("qB", [P, 2, GH, CH], F32R, a_ctx)
        pre_ctx = ExitStack()
        wp_raw = sb("wp_raw", [P, KD, 4, P], F32, pre_ctx)
        cm_raw = sb("cm_raw", [P, 2, P], F32, pre_ctx)
        wp_h = sb("wp_h", [P, KD, 4, P], F32R, pre_ctx)
        wp_l = sb("wp_l", [P, KD, 4, P], F32R, pre_ctx)
        wv_raw = sb("wv_raw", [P, D], F32, pre_ctx)
        wv_h = sb("wv_h", [P, D], F32R, pre_ctx)
        wv_l = sb("wv_l", [P, D], F32R, pre_ctx)
        tmpl = sb("tmpl", [P, 2, CH], F32R, pre_ctx)
        pre_ctx.close()
        PT = sb("PT", [P, 2, GH, CH], F32, a_ctx)
        Osb = sb("Osb", [P, CH], F32, a_ctx)

        onh = sb("onh", [P, CH], F32R, a_ctx)
        onl = sb("onl", [P, CH], F32R, a_ctx)
        spread = sb("spread", [P, P], F32, a_ctx)
        a_ctx.close()
        KA = [XTh[:, 0, :], XTh[:, 1, :], XTl[:, 0, :], XTl[:, 1, :]]
        (a_c, a_wph, a_wpl, a_ms, a_cs, a_pq, a_pt, a_pd, a_rr, a_rh, a_kb, a_v, a_ve, a_kr) = (
            sem(x) for x in ("a_c a_wph a_wpl a_ms a_cs a_pq a_pt a_pd a_rr a_rh a_kb a_v a_ve a_kr").split())
        a_w = [sem("a_w0"), sem("a_w1")]
        (a_wh, a_wl, a_wo, a_woh, a_wol, a_full, a_free, a_tk, a_tq, a_qhi, a_qb, a_mc, a_mt, a_mr, a_md, a_st, a_exp,
         a_av, a_vg, a_oe, a_den, a_rc, a_on, a_oh, a_ol) = (
            sem(x) for x in ("a_wh a_wl a_wo a_woh a_wol a_full a_free a_tk a_tq a_qhi a_qb a_mc a_mt a_mr a_md a_st a_exp "
                             "a_av a_vg a_oe a_den a_rc a_on a_oh a_ol").split())
        a_csl = [sem("a_cs0"), sem("a_cs1")]
        ST_BANK, AV_BANK, MISC_BANK = 4, 6, 7

        TAIL = 3

        def first_part(c):
            yield "P", c, 0, 0
            yield "P", c, 1, 0
            for h in range(GH):
                yield "H", c, h, 0
                for r in range(CT):
                    yield "M", c, h, r
                    if r == 0 and h + 2 < GH:
                        yield "P", c, h + 2, 0
            yield "R", c, 0, 0

        def second_part(c):
            for j in range(CT * (c + 1)):
                for half in range(2):
                    yield "S", c, j, half
                if c >= 1 and j == 1:
                    yield "F", c - 1, 0, 0
                if c >= 1 and j == 3:
                    yield "G", c - 1, 0, 0
                if c == NCH - 1 and j in range(3, 3 + 2 * GH, 2):
                    yield "W", c, (j - 3) // 2, 0
            yield "L", c, 0, 0

        def steps():
            for h in range(GH):
                yield "K", 0, h, 0
                if h == 0:
                    yield "F", -1, 0, 0
                yield "K", 1, h, 0
                if h == 1:
                    yield "G", -1, 0, 0
                    yield "O", 0, 0, 0
                yield "P", 0, h, 0
                if h >= 1:
                    yield "H", 0, h - 1, 0
                    for r in range(CT):
                        yield "M", 0, h - 1, r
            yield "H", 0, GH - 1, 0
            for r in range(CT):
                yield "M", 0, GH - 1, r
            yield "R", 0, 0, 0
            for c in range(NCH):
                one = list(first_part(c + 1)) if c + 1 < NCH else []
                two = list(second_part(c))
                cost = {"M": (c + 3) // 2, "P": 3, "H": 1, "R": 1}
                every, done, spent = sum(cost[step[0]] for step in one), 0, 0
                over = len(two) - min(TAIL, len(two) // 3)
                for k, step in enumerate(two):
                    yield step
                    while done < len(one) and spent * over < (k + 1) * every:
                        yield one[done]
                        spent += cost[one[done][0]]
                        done += 1
                yield from one[done:]

        STEPS = list(steps())
        FIRST = [step for step in STEPS if step[1] >= 0]
        LAST = [step for step in STEPS if step[0] != "W"]
        FINISH = [("F", -1, 0, 0), ("G", -1, 0, 0)]
        piece, PIECES = {}, 0
        for s_, c_, h_, r_ in STEPS:
            for k in range({"K": 1, "P": 2, "M": (c_ + 2) // 2, "G": 1}.get(s_, 0)):
                piece[s_, c_, h_, r_, k] = PIECES
                PIECES += 1
        if PIECES % 2:
            raise ValueError("a group takes an even number of pieces")
        G_BEFORE = ("G", -1, 0, 0, 0)
        K_FIRST = ("K", 0, 0, 0, 0)

        def number(g, key):
            if isinstance(g, int) and g == NG and key == G_BEFORE:
                return PIECES * NG - 1
            if isinstance(g, int) and g == 0 and piece[key] < piece[G_BEFORE]:
                return piece[key]
            return PIECES * g + piece[key] - 1

        SROUND = [CT * c * (c + 1) // 2 for c in range(NCH + 1)]

        def slot(g, key):
            return 2 * (number(g if isinstance(g, int) else 1, key) % 2)

        def st_start(c, j):
            return max(0, j - CT * c) * P

        def attn_tensor(pe, n):
            k0 = LNA[n]
            for c in range(NCH):
                ln_tensor(pe, k0, c)
            pe.wait_ge(ln_lo, KD * NCH * (k0 + 1))
            pe.wait_ge(a_wpl, 1)

            def latents(c):
                pe.wait_ge(a_pd, met(4 * c))
                for w in range(4):
                    for k in range(KD):
                        i = product(pe, ps[:, w, :], (wp_h[:, k, w, :], wp_l[:, k, w, :]), xt(k, c), k == 0, k == KD - 1)
                    i.then_inc(a_pq, 1)
            with pe.Fori(0, NCH) as c:
                latents(c)
            pe.wait_ge(a_pd, met(4 * NCH))
            for t in range(TILES):
                pe.wait_ge(a_ve, met(t - 3))
                tok = slice(t * P, (t + 1) * P)
                pe.matmul(ps[:, 4 + t % 4, 0:D], CK[:, tok], wv_h[:], start=True, stop=False)
                pe.matmul(ps[:, 4 + t % 4, 0:D], CK[0:LAT, tok], wv_l[0:LAT, :], start=False, stop=True).then_inc(a_v, 1)
            pe.wait_ge(a_ve, TILES)
            pe.wait_ge(a_kb, NCH)
            pe.wait_ge(a_kr, 1)

            def project(out, h, w, lat, cols):
                pe.matmul(out, whh[:, h, w * P:(w + 1) * P], lat[:, cols], start=True, stop=False)
                return pe.matmul(out, whl[0:LAT, h, w * P:(w + 1) * P], lat[0:LAT, cols], start=False, stop=True)

            def group(g, steps):
                def take(key, after=None):
                    pe.wait_ge(a_free, met(number(g, key) - 1 if after is None else number(g, after) + 1))
                    return slot(g, key)

                def products(c, j):
                    pe.wait_ge(a_exp, met(GH * (SROUND[-1] * g + SROUND[c] + j + 1)))
                    if j == 0:
                        pe.wait_ge(a_vg, g + 1)
                        pe.wait_ge(a_oe, met(NCH * g + c))
                    lo = st_start(c, j)
                    for h in range(GH):
                        i = pe.matmul(ps[2 * HD * h:2 * HD * (h + 1), AV_BANK, lo:CH], VG[:, j, h, :], PT[:, j % 2, h, lo:CH],
                                      start=(j == 0), stop=(j == CT * (c + 1) - 1))
                    i.then_inc(a_av, 1)

                for kind, c, h, r in steps:
                    u = NCH * g + c
                    par = c % 2
                    if kind == "K":
                        b = take((kind, c, h, r, 0))
                        pe.wait_ge(a_wl, GH * g + h + 1)
                        for w in range(2):
                            i = project(ps[:, b + w, :], h, 3, CK, slice(CH * (2 * c + w), CH * (2 * c + w + 1)))
                        i.then_inc(a_full, 1)
                    elif kind == "P":
                        b = take((kind, c, h, r, 0))
                        project(ps[:, b, :], h, 0, QL, slice(CH * c, CH * (c + 1)))
                        project(ps[:, b + 1, :], h, 1, QL, slice(CH * c, CH * (c + 1))).then_inc(a_full, 1)
                        b = take((kind, c, h, r, 1))
                        project(ps[:, b, :], h, 2, QL, slice(CH * c, CH * (c + 1))).then_inc(a_full, 1)
                    elif kind == "M":
                        pe.wait_ge(a_qhi, GH * u + h + 1)
                        q = qA[:, par, h, r * P:(r + 1) * P]
                        for k in range((c + 2) // 2):
                            key, rows = (kind, c, h, r, k), ("P", c, h, 0, 1)
                            b = take(key, rows if piece[rows] + 1 > piece[key] - 1 else None)
                            for s in range(2 * k, min(2 * k + 2, c + 1)):
                                wide = CH if s < c else max(2 * P, (r + 1) * P)
                                i = pe.matmul(ps[:, b + s % 2, 0:wide], q, KA[h][:, CH * s:CH * s + wide],
                                              start=True, stop=s < c)
                                if s == c:
                                    i = pe.matmul(ps[:, b + s % 2, r * P:(r + 1) * P], cm_bf[:, 2, :], cm_bf[:, 0, :],
                                                  start=False, stop=True)
                            i.then_inc(a_full, 1)
                    elif kind == "R":
                        pe.wait_ge(a_mc, u + 1)
                        pe.wait_ge(a_mr, met(u))
                        pe.wait_ge(a_on, met(u - 1 if c >= 1 else u))
                        pe.transpose(ps[0:GH * CT, MISC_BANK, 0:P], mcol[:], ident[:]).then_inc(a_mt, 1)
                    elif kind == "S":
                        if h == 0 and r == 0:
                            pe.wait_ge(a_md, 16 * (u + 1))
                            pe.wait_ge(a_qb, GH * (u + 1))
                        j = h
                        lo = st_start(c, j)
                        mm_lo = min(lo, CH - 2 * P)
                        for hh in (2 * r, 2 * r + 1):
                            e = GH * (SROUND[-1] * g + SROUND[c] + j) + hh
                            pe.wait_ge(a_exp, met(e - 1))
                            o = ps[:, ST_BANK + hh % 2, :]
                            pe.matmul(o[:, mm_lo:CH], KA[hh][:, j * P:(j + 1) * P], qA[:, par, hh, mm_lo:CH], start=True, stop=False)
                            i = pe.matmul(o[:, mm_lo:CH], KB[:, j * P:(j + 1) * P], qB[:, par, hh, mm_lo:CH],
                                          start=False, stop=j < CT * c)
                            if j >= CT * c:
                                i = pe.matmul(o[:, lo:lo + P], cm_bf[:, 2, :], cm_bf[:, 1, :], start=False, stop=True)
                            i.then_inc(a_st, 1)
                            if hh == 1 and j >= 1:
                                products(c, j - 1)
                    elif kind == "L":
                        products(c, CT * (c + 1) - 1)
                    elif kind == "F":
                        pe.wait_ge(a_oe, u + 1)
                        pe.matmul(ps[:, MISC_BANK, :], spread[:], Osb[:], start=True, stop=True).then_inc(a_den, 1)
                    elif kind == "G":
                        pe.wait_ge(a_ol, u + 1)
                        pe.wait_ge(a_wol, g + 1 if c >= 0 else g)
                        b = take((kind, c, h, r, 0))
                        for t in range(CT):
                            tok = slice(t * P, (t + 1) * P)
                            i = product(pe, ps[:, b + t // 2, (t % 2) * D:(t % 2 + 1) * D], (onh[:, tok], onl[:, tok]),
                                        (woh[:], wol[:]), t % 2 == 0, t % 2 == 1)
                        i.then_inc(a_full, 1)

            group(0, FIRST)
            with pe.Fori(1, NG - 1) as g:
                group(g, STEPS)
            group(NG - 1, LAST)
            group(NG, FINISH)

        def attn_vector(v, n):
            k0 = LNA[n]
            ln_vector(v, k0)
            v.wait_ge(a_ms, 1)
            v.memset(tmpk[96:97].bitcast(F32), 1.0).then_inc(a_ms, 1)
            v.wait_ge(a_wph, 1)
            v.tensor_tensor(wp_l[:], wp_raw[:], wp_h[:].bitcast(F32), ALU.subtract)
            v.tensor_tensor(wv_l[:], wv_raw[:], wv_h[:].bitcast(F32), ALU.subtract).then_inc(a_wpl, 1)

            def latents(c):
                cols = ds(CH * c, CH)
                for w, dst in ((0, QL), (1, CK)):
                    v.wait_ge(a_pt, 2 * c + w + 1)
                    v.tensor_tensor(dst[:, cols], ps[:, w, :], tmpl[:, w, :].bitcast(F32), ALU.add).then_inc(a_pd, 1)
                v.wait_ge(a_cs, 16 * (c + 1))
                v.wait_ge(a_rr, met(c))
                for w in range(2):
                    v.wait_ge(a_pq, met(4 * c + 3 + w))
                    v.tensor_tensor(rb[:, w, :], ps[:, 2 + w, :], cs[:, 0, w, :], ALU.mult).then_inc(a_pd, 1)
                v.wait_ge(a_rh, c + 1)
                v.tensor_tensor(KB[:, cols], rr[:, 0, :], tmpl[:, 0, :].bitcast(F32), ALU.add).then_inc(a_kb, 1)
            v.wait_ge(a_ms, 2)
            with v.Fori(0, NCH) as c:
                latents(c)

            def head_weights(g, h):
                v.wait_ge(a_wh, GH * g + h + 1)
                v.tensor_tensor(whl[:, h, :], whr[:, h % 2, :], whh[:, h, :].bitcast(F32), ALU.subtract).then_inc(a_wl, 1)

            for h in range(GH):
                head_weights(0, h)

            def group(g, steps):
                def full(key):
                    v.wait_ge(a_full, number(g, key) + 1)
                    return slot(g, key)

                for kind, c, h, r in steps:
                    u = NCH * g + c
                    par = c % 2
                    pj = GH * u + h
                    if kind == "K":
                        b = full((kind, c, h, r, 0))
                        v.wait_ge(a_tk, NCH // 2 * (GH * g + h) + c + 1)
                        v.tensor_tensor(KA[h][RD:P, 2 * CH * c:2 * CH * (c + 1)],
                                        ps[RD:P, b:b + 2, :].rearrange("p b s -> p (b s)"),
                                        tmpk[RD:P, c % 2, :].bitcast(F32), ALU.add).then_inc(a_free, 1)
                    elif kind == "W":
                        head_weights(g + 1, h)
                    elif kind == "O":
                        v.wait_ge(a_woh, g + 1)
                        v.tensor_tensor(wol[:], wor[:], woh[:].bitcast(F32), ALU.subtract).then_inc(a_wol, 1)
                    elif kind == "P":
                        b = full((kind, c, h, r, 0))
                        if h == 0:
                            v.wait_ge(a_csl[par], 16 * (NCH // 2 * g + c // 2 + 1))
                        v.wait_ge(a_rr, met(NCH + pj))
                        v.tensor_tensor(rb[:, 0, :], ps[:, b, :], cs[:, par, 0, :], ALU.mult)
                        v.tensor_tensor(rb[:, 1, :], ps[:, b + 1, :], cs[:, par, 1, :], ALU.mult).then_inc(a_free, 1)
                        b = full((kind, c, h, r, 1))
                        v.wait_ge(a_tq, pj + 1)
                        v.tensor_tensor(qA[RD:P, par, h, :], ps[RD:P, b, :], tmpq[RD:P, h % 2, :].bitcast(F32),
                                        ALU.add).then_inc(a_free, 1)
                    elif kind == "M":
                        for k in range((c + 2) // 2):
                            b = full((kind, c, h, r, k))
                            end = min(2 * CH, (CT * c + r + 1) * P - 2 * CH * k)
                            v.tensor_reduce(mp[:, CT * h + r, k:k + 1],
                                            ps[:, b:b + 2, :].rearrange("p b s -> p (b s)")[:, 0:end], AX_X,
                                            ALU.max).then_inc(a_free, 1)
                    elif kind == "R":
                        v.wait_ge(a_free, number(g, ("M", c, GH - 1, CT - 1, (c + 2) // 2 - 1)) + 1)
                        v.wait_ge(a_mt, met(u))
                        v.tensor_reduce(mcol[:], mp[:, :, 0:(c + 2) // 2], AX_X, ALU.max).then_inc(a_mc, 1)
                    elif kind == "F":
                        v.wait_ge(a_den, u + 1)
                        v.reciprocal(ps[:, MISC_BANK, :], ps[:, MISC_BANK, :]).then_inc(a_rc, 1)
                        v.wait_ge(a_rc, u + 1)
                        v.tensor_tensor(Osb[:], Osb[:], ps[:, MISC_BANK, :], ALU.mult).then_inc(a_on, 1)
                        v.wait_ge(a_oh, u + 1)
                        v.tensor_tensor(onl[:], Osb[:], onh[:].bitcast(F32), ALU.subtract).then_inc(a_ol, 1)
                    elif kind == "G":
                        b = full((kind, c, h, r, 0))
                        for t in range(CT):
                            xr = X[:, CT * (c % NCH) + t, :]
                            i = v.tensor_tensor(xr, ps[:, b + t // 2, (t % 2) * D:(t % 2 + 1) * D], xr, ALU.add)
                        i.then_inc(a_free, 1)

            group(0, FIRST)
            with v.Fori(1, NG - 1) as g:
                group(g, STEPS)
            group(NG - 1, LAST)
            group(NG, FINISH)

        def attn_scalar(s, n):
            k0 = LNA[n]
            for c in range(NCH):
                ln_scalar(s, k0, c)
            s.wait_ge(a_c, 96)
            s.copy(cm_bf[:, 0:2, :], cm_raw[:])
            s.copy(cm_bf[:, 2, :], ident[:])
            s.copy(wp_h[:], wp_raw[:])
            s.copy(wv_h[:], wv_raw[:]).then_inc(a_wph, 1)
            s.wait_ge(a_ms, 2)

            def latents(c):
                for w in range(2):
                    s.wait_ge(a_pq, 4 * c + w + 1)
                    if w == 0:
                        s.wait_ge(a_kb, met(c))
                    else:
                        s.wait_ge(a_pd, met(4 * c))
                    s.mul(tmpl[LAT:P, w, :], ps[LAT:P, w, :], -1.0).then_inc(a_pt, 1)
                s.wait_ge(a_rr, c + 1)
                s.wait_ge(a_pd, 4 * c + 1)
                s.mul(tmpl[LAT:P, 0, :], rr[LAT:P, 0, :], -1.0).then_inc(a_rh, 1)
            with s.Fori(0, NCH) as c:
                latents(c)
            for t in range(TILES):
                s.wait_ge(a_v, t + 1)
                s.copy(V[:, t, :], ps[:, 4 + t % 4, 0:D]).then_inc(a_ve, 1)
            s.wait_ge(a_kb, NCH)
            for h in range(GH):
                i = s.copy(KA[h][0:RD, :], KB[0:RD, :].bitcast(F32))
            i.then_inc(a_kr, 1)

            def head_weights(g, h):
                s.wait_ge(a_w[h % 2], 16 * (GH // 2 * g + h // 2 + 1))
                s.copy(whh[:, h, :], whr[:, h % 2, :]).then_inc(a_wh, 1)

            for h in range(GH):
                head_weights(0, h)

            def group(g, steps):
                if steps is not FINISH:
                    s.wait_ge(a_av, met(SROUND[-1] * g))
                    s.wait_ge(a_ve, TILES)
                    s.copy(VG[:, :, :, 0:HD], V[:, :, ds(GH * HD * g, GH * HD)].rearrange("p t (h d) -> p t h d", d=HD)).then_inc(a_vg, 1)
                for kind, c, h, r in steps:
                    u = NCH * g + c
                    par = c % 2
                    pj = GH * u + h
                    if kind == "K":
                        s.wait_ge(a_full, number(g, (kind, c, h, r, 0)) + 1)
                        s.wait_ge(a_free, met(number(g, ("K", c, h - 1, 0, 0) if h else K_FIRST) + (h > 0)))
                        b = slot(g, (kind, c, h, r, 0))
                        s.activation(tmpk[RD:RD + 32, c % 2, :], ps[RD:RD + 32, b:b + 2, :].rearrange("p b s -> p (b s)"),
                                     ACT.Copy, scale=rowm[RD:RD + 32, :]).then_inc(a_tk, 1)
                    elif kind == "W":
                        if h == 0:
                            s.wait_ge(a_full, number(g, ("P", NCH - 1, GH - 1, 0, 1)) + 1)
                        head_weights(g + 1, h)
                    elif kind == "O":
                        s.wait_ge(a_wo, 16 * (g + 1))
                        s.wait_ge(a_full, met(number(g, G_BEFORE) + 1 if steps is not FIRST else 0))
                        s.copy(woh[:], wor[:]).then_inc(a_woh, 1)
                    elif kind == "P":
                        s.wait_ge(a_full, number(g, (kind, c, h, r, 1)) + 1)
                        last = ("P", c, h - 2, 0, 1) if h >= 2 else ("P", c - 1, h + 2, 0, 1)
                        s.wait_ge(a_free, met(number(g, last) + 1 if h >= 2 or c >= 1 else number(g, K_FIRST)))
                        s.activation(tmpq[96:P, h % 2, :], ps[96:P, slot(g, (kind, c, h, r, 1)), :],
                                     ACT.Copy, scale=rowm[96:P, :]).then_inc(a_tq, 1)
                    elif kind == "H":
                        s.wait_ge(a_rr, NCH + pj + 1)
                        s.copy(qA[0:RD, par, h, :], rr[0:RD, h % 2, :])
                        s.copy(qB[RD:P, par, h, :], rr[RD:P, h % 2, :]).then_inc(a_qhi, 1)
                    elif kind == "R":
                        s.wait_ge(a_mt, u + 1)
                        s.wait_ge(a_md, met(16 * u))
                        s.mul(mrow[:], ps[0:GH * CT, MISC_BANK, 0:P], -1.0).then_inc(a_mr, 1)
                    elif kind == "S":
                        j = h
                        lo = st_start(c, j)
                        for hh in (2 * r, 2 * r + 1):
                            rnd = SROUND[-1] * g + SROUND[c] + j
                            s.wait_ge(a_st, GH * rnd + hh + 1)
                            if hh == 0:
                                s.wait_ge(a_av, met(rnd - 1))
                            s.activation(PT[:, j % 2, hh, lo:CH], ps[:, ST_BANK + hh % 2, lo:CH], ACT.Exp,
                                         scale=SCALE).then_inc(a_exp, 1)
                    elif kind == "L":
                        s.wait_ge(a_av, met(SROUND[-1] * g + SROUND[c + 1]))
                        s.wait_ge(a_ol, met(u))
                        s.copy(Osb[:], ps[:, AV_BANK, :]).then_inc(a_oe, 1)
                    elif kind == "F":
                        s.wait_ge(a_on, u + 1)
                        if c < 0:
                            s.wait_ge(a_full, number(g - 1, ("G", NCH - 2, 0, 0, 0)) + 1)
                        elif c >= 1 or steps is not FIRST:
                            s.wait_ge(a_full, number(g, ("G", c - 1, 0, 0, 0)) + 1)
                        s.copy(onh[:], Osb[:]).then_inc(a_oh, 1)

            group(0, FIRST)
            with s.Fori(1, NG - 1) as g:
                group(g, STEPS)
            group(NG - 1, LAST)
            group(NG, FINISH)

        def attn_gpsimd(p, n):
            k0 = LNA[n]
            p.memset(VG[:], 1.0)
            for t in (tmpl, tmpq, tmpk):
                i = p.memset(t[:].bitcast(F32), 0.0)
            i.then_inc(a_ms, 1)
            ln_gpsimd(p, k0)
            with p.Fori(0, NCH) as c:
                p.wait_ge(a_pd, 4 * (c + 1))
                p.wait_ge(a_kb, met(c))
                p.tensor_tensor(rr[:, 0, :], rb[:, 0, :], rb[:, 1, :], ALU.add).then_inc(a_rr, 1)

            def group(g, steps):
                for kind, c, h, r in steps:
                    u = NCH * g + c
                    par = c % 2
                    pj = GH * u + h
                    if kind == "P":
                        p.wait_ge(a_free, number(g, (kind, c, h, r, 0)) + 1)
                        p.wait_ge(a_kb, NCH)
                        p.wait_ge(a_qb, met(pj - 1))
                        p.tensor_tensor(rr[:, h % 2, :], rb[:, 0, :], rb[:, 1, :], ALU.add).then_inc(a_rr, 1)
                    elif kind == "H":
                        p.wait_ge(a_qhi, pj + 1)
                        p.tensor_tensor(qB[0:RD, par, h, :], rr[0:RD, h % 2, :], qA[0:RD, par, h, :].bitcast(F32),
                                        ALU.subtract).then_inc(a_qb, 1)

            group(0, FIRST)
            with p.Fori(1, NG - 1) as g:
                group(g, STEPS)
            group(NG - 1, LAST)
            group(NG, FINISH)

        def attn_sync(sp, n):
            sp.dma_start(wp_raw[:], a["wp"]).then_inc(a_c, 16)
            sp.dma_start(wv_raw[:], a["wv"]).then_inc(a_c, 16)
            sp.dma_start(cm_raw[:], a["cmask"]).then_inc(a_c, 16)
            sp.dma_start(rowm[:], a["rowm"]).then_inc(a_c, 16)
            sp.dma_start(spread[:], a["spread"]).then_inc(a_c, 32)
            with sp.Fori(0, NCH) as c:
                sp.wait_ge(a_pd, met(4 * c))
                sp.dma_start(cs[:, 0], a["rope"][:, :, ds(CH * c, CH)]).then_inc(a_cs, 16)
            sp.wait_ge(a_pd, met(4 * NCH))

            def head_weights(g, h):
                sp.wait_ge(a_wl, met(GH * g + h - 1))
                sp.dma_start(whr[:, h % 2, :], a["whead"][:, ds(GH * g + h, 1), :]).then_inc(a_w[h % 2], 16)

            for h in range(GH):
                head_weights(0, h)

            def group(g, steps):
                if steps is not FINISH:
                    sp.wait_ge(a_wol, met(g))
                    sp.dma_start(wor[:], a["wog"][ds(g, 1)]).then_inc(a_wo, 16)
                for kind, c, h, r in steps:
                    u = NCH * g + c
                    if kind == "P" and h == 0:
                        if c >= 2:
                            sp.wait_ge(a_rr, met(NCH + GH * (u - 1)))
                        else:
                            sp.wait_ge(a_rr, met(NCH + GH * NCH * g))
                        sp.dma_start(cs[:, c % 2], a["rope"][:, :, CH * c:CH * (c + 1)]).then_inc(a_csl[c % 2], 16)
                    if kind == "W":
                        head_weights(g + 1, h)
                    if kind == "R":
                        sp.wait_ge(a_mr, u + 1)
                        sp.dma_start(qA[96:97, c % 2].rearrange("a h (r t) -> a (h r) t", t=P).bitcast(F32), mrow[:].bitcast(F32)).then_inc(a_md, 16)

            group(0, FIRST)
            with sp.Fori(1, NG - 1) as g:
                group(g, STEPS)
            group(NG - 1, LAST)
            group(NG, FINISH)

        NHI, DI = 16, 128
        TOPK = 32
        NEG = -1e30
        TAKEN = -3e38
        KVI = 2 * P + NHI
        i_ctx = ExitStack()
        wih = sb("wih", [P, NHI + 1, KD, DI], F32R, i_ctx)
        wil = sb("wil", [P, NHI + 1, KD, DI], F32R, i_ctx)
        KIh = sb("KIh", [P, T], F32R, i_ctx)
        KIl = sb("KIl", [P, T], F32R, i_ctx)
        imask = sb("imask", [P, CH], F32, i_ctx)
        iw = sb("iw", [P, TILES, NHI], F32, i_ctx)
        iwa = sb("iwa", [P, TILES, NHI], F32, i_ctx)
        iws = sb("iws", [P, TILES, NHI], F32, i_ctx)
        Isc = sb("Isc", [P, 2, T], F32, i_ctx)
        RL = 3
        rlv = sb("rlv", [P, RL, CH], F32, i_ctx)
        rlp = sb("rlp", [P, RL, CH], F32, i_ctx)
        part_sum = sb("part_sum", [P, CH], F32, i_ctx)
        v8 = sb("v8", [P, 2, 8], F32, i_ctx)
        idx = sb("idx", [P, TILES, TOPK], U32, i_ctx)
        idxf = sb("idxf", [P, TILES, TOPK], F32, i_ctx)
        selt = sb("selt", [P, 4, P // 4], F32, i_ctx)
        raw_ctx = ExitStack()
        wir = sb("wir", [P, NHI + 1, D], F32, raw_ctx)
        wirh = sb("wirh", [P, NHI + 1, D], F32R, raw_ctx)
        wirl = sb("wirl", [P, NHI + 1, D], F32R, raw_ctx)
        ikv_raw = sb("ikv_raw", [P, KD, KVI], F32, raw_ctx)
        ihadr = sb("ihadr", [P, P], F32, raw_ctx)
        ikv_h = sb("ikv_h", [P, KD, KVI], F32R, raw_ctx)
        ikv_l = sb("ikv_l", [P, KD, KVI], F32R, raw_ctx)
        kvs = sb("kvs", [P, 2, 2 * P], F32, raw_ctx)
        ihad = sb("ihad", [P, P], F32R, raw_ctx)
        raw_ctx.close()
        qih = sb("qih", [P, NHI, CH], F32R, i_ctx)
        qil = sb("qil", [P, NHI, CH], F32R, i_ctx)
        i_ctx.close()
        (i_c, i_rh, i_rl, i_t, i_th, i_tl, i_ki, i_kh, i_kl, i_kv, i_kve, i_iw, i_q, i_qh, i_ql, i_L, i_R,
         i_A, i_k, i_sg, i_B, i_xt) = (
            sem(x) for x in ("i_c i_rh i_rl i_t i_th i_tl i_ki i_kh i_kl i_kv i_kve i_iw i_q i_qh i_ql i_L i_R "
                             "i_A i_k i_sg i_B i_xt").split())
        i_kvd = [sem("i_kvd0"), sem("i_kvd1")]
        HSC = float(DI) ** -0.5
        NTB = (NHI + 1 + 1) // 2

        def blocks(t):
            return [(h, b) for b in range(t // CT + 1) for h in range(NHI)]

        LB = [0]
        for t in reversed(range(TILES)):
            LB.append(LB[-1] + len(blocks(t)))

        PH = (1, 3, 5, 7, 9, 11, 13)
        VH = tuple(h for h in range(NHI) if h not in PH)

        def counted(n, h):
            heads = PH if h in PH else VH
            return len(heads) * (n // NHI) + heads.index(h)

        def added(m):
            return m + m // len(VH) + 1

        def width(t, b):
            return CH if b < t // CT else (t % CT + 1) * P

        def index_sync(sp, n):
            sp.dma_start(wir[:], a["wi"]).then_inc(i_c, 16)
            sp.dma_start(ihadr[:], a["hadamard"]).then_inc(i_c, 16)
            sp.dma_start(ikv_raw[:], a["wkvi"]).then_inc(i_c, 16)
            sp.dma_start(imask[:], a["imask"]).then_inc(i_c, 16)
            sp.dma_start(selt[:], a["selt"]).then_inc(i_c, 16)
            for t in range(TILES):
                sp.wait_ge(i_kve, t + 1)
                sp.dma_start(a["kv_scratch"][t * P:(t + 1) * P, :], kvs[:, t % 2, :]).then_inc(i_kvd[t % 2], 16)
            sp.wait_ge(i_kvd[0], met(16 * TILES // 2))
            sp.wait_ge(i_kvd[1], met(16 * TILES // 2))

        def index_tensor(pe, n):
            k0 = LNA[n]
            for c in range(NCH):
                ln_tensor(pe, k0, c)
            pe.wait_ge(i_rl, 1)
            for m in range(NTB):
                pe.wait_ge(i_tl, met(m - 3))
                for hh in range(min(2, NHI + 1 - 2 * m)):
                    for k in range(KD):
                        at = (hh * KD + k) * DI
                        o = ps[:, 4 + m % 4, at:at + DI]
                        first = at == 0
                        last = hh == min(2, NHI + 1 - 2 * m) - 1 and k == KD - 1
                        pe.matmul(o, wirh[:, 2 * m + hh, k * P:(k + 1) * P], ihad[:], start=first, stop=False)
                        i = pe.matmul(o, wirl[:, 2 * m + hh, k * P:(k + 1) * P], ihad[:], start=False, stop=last)
                i.then_inc(i_t, 1)
            pe.wait_ge(ln_lo, KD * NCH * (k0 + 1))
            pe.wait_ge(i_tl, NTB)

            def keys(c):
                pe.wait_ge(i_kl, max(c - 1, 0))
                for k in range(KD):
                    i = product(pe, ps[:, 2 + c % 2, :], (wih[:, NHI, k, :], wil[:, NHI, k, :]), xt(k, c), k == 0, k == KD - 1)
                i.then_inc(i_ki, 1)
            for c in range(NCH):
                keys(c)
            for t in range(TILES):
                pe.wait_ge(i_kve, met(t - 1))
                tok = slice(t * P, (t + 1) * P)
                for k in range(KD):
                    i = product(pe, ps[:, 4 + t % 2, 0:KVI], (XTh[:, k, tok], XTl[:, k, tok]),
                                (ikv_h[:, k, :], ikv_l[:, k, :]), k == 0, k == KD - 1)
                i.then_inc(i_kv, 1)
            pe.wait_ge(i_kl, NCH)
            pe.wait_ge(i_kve, TILES)
            n_l = 0
            for d in range(NCH):
                c = NCH - 1 - d
                for h in range(NHI):
                    pe.wait_ge(i_ql, met(NHI * d + h - 1))
                    for k in range(KD):
                        i = product(pe, ps[:, h % 2, :], (wih[:, h, k, :], wil[:, h, k, :]), xt(k, c), k == 0, k == KD - 1)
                    i.then_inc(i_q, 1)
                for t in reversed(range(CT * c, CT * (c + 1))):
                    tok = slice((t - CT * c) * P, (t - CT * c + 1) * P)
                    for h, b in blocks(t):
                        pe.wait_ge(i_ql, NHI * d + h + 1)
                        pe.wait_ge(i_R, met(n_l - 3))
                        w = max(width(t, b), 2 * P)
                        product(pe, ps[:, 2 + n_l % 4, 0:w], (qih[:, h, tok], qil[:, h, tok]),
                                (KIh[:, CH * b:CH * b + w], KIl[:, CH * b:CH * b + w]), True, True).then_inc(i_L, 1)
                        n_l += 1
            pe.wait_ge(i_k, TOPK_STEPS * TILES + 1)
            for t in range(TILES):
                for j in range(4):
                    i = pe.matmul(ps[TOPK * j:TOPK * (j + 1), 6, TOPK * t:TOPK * (t + 1)], idxf[:, t, :], selt[:, j, :],
                                  start=t == 0, stop=t == TILES - 1)
            i.then_inc(i_xt, 1)

        def index_scalar(s, n):
            k0 = LNA[n]
            for c in range(NCH):
                ln_scalar(s, k0, c)
            s.wait_ge(i_c, 80)
            s.copy(wirh[:], wir[:])
            s.copy(ihad[:], ihadr[:])
            s.copy(ikv_h[:], ikv_raw[:]).then_inc(i_rh, 1)
            for m in range(NTB):
                hs = slice(2 * m, min(2 * m + 2, NHI + 1))
                size = (hs.stop - hs.start) * KD * DI
                s.wait_ge(i_t, m + 1)
                s.mul(wih[:, hs], ps[:, 4 + m % 4, 0:size], HSC).then_inc(i_th, 1)
            for c in range(NCH):
                s.wait_ge(i_ki, c + 1)
                s.copy(KIh[:, ds(CH * c, CH)], ps[:, 2 + c % 2, :]).then_inc(i_kh, 1)
            for t in range(TILES):
                s.wait_ge(i_kv, t + 1)
                if t >= 2:
                    s.wait_ge(i_kvd[t % 2], met(16 * (t // 2)))
                s.copy(iw[:, t, :], ps[:, 4 + t % 2, 2 * P:KVI])
                s.copy(kvs[:, t % 2, :], ps[:, 4 + t % 2, 0:2 * P]).then_inc(i_kve, 1)
            before = None

            def signed(t, h, w, n):
                at = rlp[:, counted(n, h) % RL, 0:w]
                s.wait_ge(i_R, n + 1)
                s.activation(at, at, ACT.Copy, scale=iws[:, t, h:h + 1]).then_inc(i_sg, 1)

            n_l = 0
            for d in range(NCH):
                c = NCH - 1 - d
                for h in range(NHI):
                    s.wait_ge(i_q, NHI * d + h + 1)
                    s.wait_ge(i_L, met(LB[CT * d]))
                    if d == 0 and h == 0:
                        s.wait_ge(i_kvd[0], 16 * (TILES // 2))
                        s.wait_ge(i_kvd[1], 16 * (TILES // 2))
                    s.copy(qih[:, h, :], ps[:, h % 2, :]).then_inc(i_qh, 1)
                if d == 0:
                    s.wait_ge(i_iw, 3)
                for t in reversed(range(CT * c, CT * (c + 1))):
                    for h, b in blocks(t):
                        w = width(t, b)
                        m = counted(n_l, h)
                        s.wait_ge(i_L, n_l + 1)
                        if h in VH:
                            s.wait_ge(i_A, max(added(m - RL), 0))
                        else:
                            s.wait_ge(i_B, max(m - RL + 1, 0))
                        s.activation((rlp if h in PH else rlv)[:, m % RL, 0:w], ps[:, 2 + n_l % 4, 0:w], ACT.Relu,
                                     scale=iwa[:, t, h:h + 1]).then_inc(i_R, 1)
                        if h in VH:
                            if before:
                                signed(*before)
                            before = None
                        else:
                            before = t, h, w, n_l
                        n_l += 1

        def index_vector(v, n):
            k0 = LNA[n]
            ln_vector(v, k0)
            v.wait_ge(i_rh, 1)
            v.tensor_tensor(wirl[:], wir[:], wirh[:].bitcast(F32), ALU.subtract)
            v.tensor_tensor(ikv_l[:], ikv_raw[:], ikv_h[:].bitcast(F32), ALU.subtract).then_inc(i_rl, 1)
            for m in range(NTB):
                hs = slice(2 * m, min(2 * m + 2, NHI + 1))
                size = (hs.stop - hs.start) * KD * DI
                v.wait_ge(i_th, m + 1)
                v.scalar_tensor_tensor(out=wil[:, hs], in0=ps[:, 4 + m % 4, 0:size], scalar=HSC,
                                       in1=wih[:, hs].bitcast(F32), op0=ALU.mult, op1=ALU.subtract).then_inc(i_tl, 1)
            for c in range(NCH):
                v.wait_ge(i_kh, c + 1)
                v.tensor_tensor(KIl[:, ds(CH * c, CH)], ps[:, 2 + c % 2, :], KIh[:, ds(CH * c, CH)].bitcast(F32), ALU.subtract).then_inc(i_kl, 1)
            v.wait_ge(i_kve, TILES)
            v.tensor_scalar(iwa[:], iw[:], -1.0, None, ALU.mult).then_inc(i_iw, 1)
            v.tensor_scalar(iws[:], iw[:], 0.0, 2.0, ALU.is_ge, ALU.mult).then_inc(i_iw, 1)
            v.wait_ge(i_iw, 2)
            v.tensor_tensor(iwa[:], iwa[:], iw[:], ALU.max)
            v.tensor_scalar(iws[:], iws[:], 1.0, None, ALU.subtract).then_inc(i_iw, 1)
            v.wait_ge(i_iw, 3)

            def topk_step(t, k):
                W = (t + 1) * P
                scores = Isc[:, t % 2, 0:W]
                rnd = k // 3
                p = TILES - 1 - t
                v.wait_ge(i_k, TOPK_STEPS * p + k)
                if k == 0:
                    v.wait_ge(i_A, LB[p + 1] // NHI * (len(VH) + 1))
                if k % 3 == 0:
                    i = v.max(v8[:, rnd % 2, :], scores)
                elif k % 3 == 1:
                    i = v.max_index(idx[:, t, 8 * rnd:8 * rnd + 8], v8[:, rnd % 2, :], scores)
                else:
                    i = v.match_replace(scores, v8[:, rnd % 2, :], scores, TAKEN)
                i.then_inc(i_k, 1)

            n_l = 0
            for d in range(NCH):
                c = NCH - 1 - d
                for h in range(NHI):
                    v.wait_ge(i_qh, NHI * d + h + 1)
                    v.tensor_tensor(qil[:, h, :], ps[:, h % 2, :], qih[:, h, :].bitcast(F32), ALU.subtract).then_inc(i_ql, 1)
                for t in reversed(range(CT * c, CT * (c + 1))):
                    p = TILES - 1 - t
                    if p >= 2:
                        v.wait_ge(i_k, TOPK_STEPS * (p - 1))
                    steps_done = 0
                    todo = blocks(t)
                    for at, (h, b) in enumerate(todo):
                        w = width(t, b)
                        acc = Isc[:, t % 2, CH * b:CH * b + w]
                        m = counted(n_l, h)
                        if h in VH:
                            v.wait_ge(i_R, n_l + 1)
                            if h > 0:
                                v.wait_ge(i_A, added(m - 1))
                            if h == 0 and b < c:
                                i = v.tensor_scalar(acc, rlv[:, m % RL, 0:w], iws[:, t, h:h + 1], None, ALU.mult)
                            else:
                                i = v.scalar_tensor_tensor(out=acc, in0=rlv[:, m % RL, 0:w], scalar=iws[:, t, h:h + 1],
                                                           in1=imask[:, CH - w:CH] if h == 0 else acc,
                                                           op0=ALU.mult, op1=ALU.add)
                            i.then_inc(i_A, 1)
                        if h == NHI - 1:
                            v.wait_ge(i_A, added(m))
                            v.wait_ge(i_B, len(PH) * (n_l // NHI + 1))
                            v.tensor_tensor(acc, acc, part_sum[:, 0:w], ALU.add).then_inc(i_A, 1)
                        n_l += 1
                        while p >= 1 and steps_done < (at + 1) * TOPK_STEPS // len(todo):
                            topk_step(t + 1, steps_done)
                            steps_done += 1
            for k in range(TOPK_STEPS):
                topk_step(0, k)
            v.wait_ge(i_k, met(TOPK_STEPS * TILES))
            v.tensor_copy(idxf[:], idx[:]).then_inc(i_k, 1)
            v.wait_ge(i_xt, 1)
            v.tensor_copy(idxT, ps[:, 6, :].rearrange("p (t g) -> p t g", g=TOPK))

        def index_gpsimd(g, n):
            ln_gpsimd(g, LNA[n])
            n_l = 0
            for t in reversed(range(TILES)):
                for h, b in blocks(t):
                    if h in PH[1:]:
                        w, m = width(t, b), counted(n_l, h)
                        at = rlp[:, m % RL, 0:w]
                        g.wait_ge(i_sg, m + 1)
                        if h == PH[1]:
                            g.wait_ge(i_A, (len(VH) + 1) * (n_l // NHI))
                            g.tensor_tensor(part_sum[:, 0:w], rlp[:, (m - 1) % RL, 0:w], at, ALU.add).then_inc(i_B, 2)
                        else:
                            g.wait_ge(i_B, m)
                            g.tensor_tensor(part_sum[:, 0:w], part_sum[:, 0:w], at, ALU.add).then_inc(i_B, 1)
                    n_l += 1

        NHQ, HQ = 16, 128
        GT = 4
        GR = GT * NHQ
        BG = 8
        NB = CH // (GT * BG)
        TB = P // (GT * BG)
        HT = CH // 2
        HN = NHQ // 2
        SSC = float(HQ) ** -0.5
        s_ctx = ExitStack()
        swqh = sb("swqh", [P, NHQ, KD, HQ], F32R, s_ctx)
        swql = sb("swql", [P, NHQ, KD, HQ], F32R, s_ctx)
        swo = sb("swo", [P, NHQ, D], F32, s_ctx)
        smk = sb("smk", [8, P + 2 * CH], BF16, s_ctx)
        sidx = sb("sidx", [P, 2, P // GT], U32, s_ctx)
        RB = 4
        KV = sb("KV", [P, RB * BG, 2 * P], F32, s_ctx)
        KT = sb("KT", [P, BG, P], F32, s_ctx)
        smx = sb("smx", [P, 2, BG // 2], F32, s_ctx)
        snm = sb("snm", [P, 2, BG // 2], F32, s_ctx)
        ssum = sb("ssum", [P, 2, BG // 2], F32, s_ctx)
        srs = sb("srs", [P, 2, BG // 2], F32, s_ctx)
        sP = sb("sP", [P, 2, BG // 2, P], F32, s_ctx)
        sPT = sb("sPT", [P, BG // 2, P], F32, s_ctx)
        raw2_ctx = ExitStack()
        swr = sb("swr", [P, 2, NHQ // 2 * D], F32, raw2_ctx)
        smk_raw = sb("smk_raw", [8, P + 2 * CH], F32, raw2_ctx)
        raw2_ctx.close()
        qT = sb("qT", [P, 2, HT, NHQ], F32, s_ctx)
        oT = sb("oT", [P, 2, P, NHQ], F32, s_ctx)
        s_ctx.close()
        s_w = [sem("s_w0"), sem("s_w1")]
        s_g = [sem(f"s_g{k}") for k in range(RB)]
        (s_c, s_wh, s_wl, s_q, s_qe, s_ix, s_kt, s_kte, s_s, s_nm, s_ex, s_rs, s_p, s_pt, s_pte, s_o, s_oe,
         s_y, s_x) = (
            sem(x) for x in ("s_c s_wh s_wl s_q s_qe s_ix s_kt s_kte s_s s_nm s_ex s_rs s_p s_pt s_pte s_o s_oe "
                             "s_y s_x").split())
        NW = 2

        def w_piece(m):
            return slice(NHQ // 2 * m, NHQ // 2 * (m + 1))

        def select_sync(sp, n):
            sp.dma_start(smk_raw[:], a["smask"]).then_inc(s_c, 16)
            for m in range(NW):
                sp.dma_start(swr[:, m, :], a["swq"][:, m]).then_inc(s_w[m], 16)
            sp.wait_ge(s_w[0], 16)
            sp.dma_start(swo[:], a["swo"]).then_inc(s_w[0], 16)

        def batches():
            for b in range(NB):
                yield "T", b
                yield "W", b - 1
                yield "P", b
                yield "Y", b - 1
                yield "Q", b
                yield "O", b - 1

        SMID = list(batches())
        SFIRST = [(kind, b) for kind, b in SMID if b >= (TB if kind == "Y" else 0)]
        SLAST = [(kind, b) for kind, b in SMID if kind != "P" or b < HN]
        SEND = [("W", NB - 1), ("O", NB - 1)] + [("Y", j) for j in range(NB - 1, NB + TB)]
        HY = NHQ // TB

        def select_tensor(pe, n):
            pe.wait_ge(s_wl, NW)

            def queries(pair, start, bank):
                for m in range(2):
                    h = 2 * (pair % HN) + m
                    for k in range(KD):
                        i = product(pe, ps[:, bank, HT * m:HT * (m + 1)], (swqh[:, h, k, :], swql[:, h, k, :]),
                                    (XTh[:, k, ds(start, HT)], XTl[:, k, ds(start, HT)]),
                                    m == 0 and k == 0, m == 1 and k == KD - 1)
                i.then_inc(s_q, 1)

            for pair in range(HN):
                pe.wait_ge(s_qe, max(pair - 1, 0))
                queries(pair, 0, 6 + pair % 2)
            pe.wait_ge(s_w[0], 32)

            def chunk(c, steps):
                for kind, b in steps:
                    B = NB * c + b
                    if kind == "T":
                        pe.wait_ge(s_g[b % RB], 16 * BG * (NB // RB * c + b // RB + 1))
                        pe.wait_ge(s_kte, met(2 * B))
                        for g in range(BG):
                            i = pe.transpose(ps[:, g // 4, (g % 4) * P:(g % 4 + 1) * P], KV[:, BG * (b % RB) + g, 0:P], ident[:])
                            if g % 4 == 3:
                                i.then_inc(s_kt, 1)
                    elif kind == "P":
                        pe.wait_ge(s_qe, HN + B)
                        queries(b, CH * c + HT * (b // HN + 1), 6)
                    elif kind == "Q":
                        pe.wait_ge(s_kte, 2 * B + 2)
                        pe.wait_ge(s_qe, HN * (2 * c + b // HN + 1))
                        pe.wait_ge(s_ex, met(B - 1))
                        rhs = smk[:, P:P + CH] if isinstance(c, int) and c == 0 and b == 0 else smk[:, P + CH:P + 2 * CH]
                        for g in range(BG):
                            pe.matmul(ps[GR * (g % 2):GR * (g % 2 + 1), 2 + b % 2, g // 2 * P:(g // 2 + 1) * P],
                                          qT[:, b // HN, (b % HN * BG + g) * GT:(b % HN * BG + g + 1) * GT, :].rearrange("p t h -> p (t h)"),
                                          KT[:, g, :], start=g < 2, stop=False)
                        pe.matmul(ps[:, 2 + b % 2, :], smk[:, 0:P], rhs, start=False, stop=True).then_inc(s_s, 1)
                    elif kind == "W":
                        pe.wait_ge(s_p, B + 1)
                        pe.wait_ge(s_pte, B)
                        for m in range(BG // 2):
                            i = pe.transpose(ps[:, 4, m * P:(m + 1) * P], sP[:, b % 2, m, :], ident[:])
                        i.then_inc(s_pt, 1)
                    elif kind == "O":
                        pe.wait_ge(s_pte, B + 1)
                        pe.wait_ge(s_oe, B)
                        for g in range(BG):
                            i = pe.matmul(ps[:, 5, g * GR:(g + 1) * GR], KV[:, BG * (b % RB) + g, P:2 * P],
                                          sPT[:, g // 2, GR * (g % 2):GR * (g % 2 + 1)], start=True, stop=True)
                        i.then_inc(s_o, 1)
                    else:
                        tile, part = b // TB - 1, b % TB
                        if part == 0:
                            pe.wait_ge(s_oe, NB * c + TB * (tile + 1))
                            pe.wait_ge(s_x, met(CT * c + tile))
                        for h in range(HY * part, HY * (part + 1)):
                            i = pe.matmul(ps[:, 7, 0:D], oT[:, tile % 2, :, h], swo[:, h, :], start=h == 0, stop=h == NHQ - 1)
                        if part == TB - 1:
                            i.then_inc(s_y, 1)
            chunk(0, SFIRST)
            with pe.Fori(1, NCH - 1) as c:
                chunk(c, SMID)
            chunk(NCH - 1, SLAST)
            chunk(NCH - 1, SEND)

        def select_scalar(s, n):
            s.wait_ge(s_c, 16)
            s.copy(smk[:], smk_raw[:])
            for m in range(NW):
                s.wait_ge(s_w[m], 16)
                s.copy(swqh[:, w_piece(m)], swr[:, m, :]).then_inc(s_wh, 1)
            s.wait_ge(s_wl, NW)

            def queries(half, pair, bank):
                h = 2 * (pair % HN)
                s.copy(qT[:, half, :, h:h + 2], ps[:, bank, :].rearrange("p (h t) -> p t h", h=2)).then_inc(s_qe, 1)

            for pair in range(HN):
                s.wait_ge(s_q, pair + 1)
                queries(0, pair, 6 + pair % 2)

            def chunk(c, steps):
                for kind, b in steps:
                    B = NB * c + b
                    if kind == "T":
                        for k in range(2):
                            s.wait_ge(s_kt, 2 * B + k + 1)
                            s.wait_ge(s_s, B)
                            s.copy(KT[:, 4 * k:4 * k + 4, :], ps[:, k, :]).then_inc(s_kte, 1)
                    elif kind == "P":
                        s.wait_ge(s_q, HN + B + 1)
                        s.wait_ge(s_s, met(NB * c + HN * (b // HN)))
                        queries((b // HN + 1) % 2, b, 6)
                    elif kind == "Q":
                        s.wait_ge(s_nm, 2 * B + 2)
                        s.wait_ge(s_pt, met(B - 1))
                        for m in range(BG // 2):
                            i = s.activation(sP[:, b % 2, m, :], ps[:, 2 + b % 2, m * P:(m + 1) * P], ACT.Exp,
                                             bias=snm[:, b % 2, m:m + 1], scale=SSC, accum_out=ssum[:, b % 2, m:m + 1])
                        i.then_inc(s_ex, 1)
                    elif kind == "O":
                        s.wait_ge(s_o, B + 1)
                        s.wait_ge(s_y, met(CT * c + b // TB - 1))
                        s.copy(oT[:, b // TB % 2, (b % TB) * GT * BG:(b % TB + 1) * GT * BG, :], ps[:, 5, :]).then_inc(s_oe, 1)
            chunk(0, SFIRST)
            with s.Fori(1, NCH - 1) as c:
                chunk(c, SMID)
            chunk(NCH - 1, SLAST)
            chunk(NCH - 1, SEND)

        def select_vector(v, n):
            def indices(c, r):
                v.wait_ge(s_kt, met(2 * (NB * c + TB * (r - 1))))
                v.tensor_copy(sidx[:, r % 2, :], idxT[:, ds(CT * c + r, 1), :].rearrange("p a g -> p (a g)")).then_inc(s_ix, 1)

            indices(0, 0)
            for m in range(NW):
                v.wait_ge(s_wh, m + 1)
                v.tensor_tensor(swql[:, w_piece(m)], swr[:, m, :], swqh[:, w_piece(m)].bitcast(F32), ALU.subtract).then_inc(s_wl, 1)

            def chunk(c, steps):
                for kind, b in steps:
                    B = NB * c + b
                    if kind == "T" and b % TB == 0 and not (isinstance(c, int) and c == NCH - 1 and b // TB + 1 == CT):
                        indices(c, b // TB + 1)
                    if kind == "Q":
                        v.wait_ge(s_s, B + 1)
                        v.tensor_reduce(smx[:, b % 2, :], ps[:, 2 + b % 2, :].rearrange("p (m k) -> p m k", k=P), AX_X,
                                        ALU.max).then_inc(s_nm, 1)
                        v.wait_ge(s_nm, 2 * B + 1)
                        v.tensor_scalar(snm[:, b % 2, :], smx[:, b % 2, :], -SSC, None, ALU.mult).then_inc(s_nm, 1)
                        v.wait_ge(s_ex, B + 1)
                        v.reciprocal(srs[:, b % 2, :], ssum[:, b % 2, :]).then_inc(s_rs, 1)
                        v.wait_ge(s_rs, B + 1)
                        for m in range(BG // 2):
                            i = v.tensor_scalar(sP[:, b % 2, m, :], sP[:, b % 2, m, :], srs[:, b % 2, m:m + 1], None, ALU.mult)
                        i.then_inc(s_p, 1)
                    elif kind == "W":
                        v.wait_ge(s_pt, B + 1)
                        v.wait_ge(s_o, B)
                        v.tensor_copy(sPT[:], ps[:, 4, :].rearrange("p (m k) -> p m k", k=P)).then_inc(s_pte, 1)
                    elif kind == "Y" and b % TB == TB - 1:
                        tile = b // TB - 1
                        v.wait_ge(s_y, CT * c + tile + 1)
                        xr = X[:, ds(CT * c + tile, 1), :].rearrange("p a d -> p (a d)")
                        v.tensor_tensor(xr, ps[:, 7, 0:D], xr, ALU.add).then_inc(s_x, 1)
            chunk(0, SFIRST)
            with v.Fori(1, NCH - 1) as c:
                chunk(c, SMID)
            chunk(NCH - 1, SLAST)
            chunk(NCH - 1, SEND)

        def select_gpsimd(g, n):
            def chunk(c):
                for b in range(NB):
                    B = NB * c + b
                    if b % TB == 0:
                        g.wait_ge(s_ix, CT * c + b // TB + 1)
                    g.wait_ge(s_o, met(B - RB + 1))
                    g.nop(nofuse=True)
                    for k in range(BG):
                        at = (b % TB) * BG + k
                        g.indirect_dma_start(KV[:, BG * (b % RB) + k, :], None, a["kv_scratch"],
                                             bass.IndirectOffsetOnAxis(sidx[:, b // TB % 2, at:at + 1], 0)).then_inc(s_g[b % RB], 16)
            chunk(0)
            with g.Fori(1, NCH) as c:
                chunk(c)

        plan, norms = [], 0
        for k, name in enumerate(stages):
            plan.append((name[:-1], int(name[-1]), k))
            if name[:-1] != "select":
                {"moe": LNC, "ffn": LNF}.get(name[:-1], LNA)[int(name[-1])] = norms
                norms += 1

        def run(eng, which):
            table = {
                "moe": {"sync": moe_sync, "scalar": moe_scalar, "vector": moe_vector, "gpsimd": moe_gpsimd, "tensor": moe_tensor},
                "ffn": {"sync": ffn_sync, "scalar": ffn_scalar, "vector": ffn_vector, "gpsimd": ffn_gpsimd, "tensor": ffn_tensor},
                "attn": {"sync": attn_sync, "scalar": attn_scalar, "vector": attn_vector, "gpsimd": attn_gpsimd, "tensor": attn_tensor},
                "index": {"sync": index_sync, "scalar": index_scalar, "vector": index_vector, "gpsimd": index_gpsimd, "tensor": index_tensor},
                "select": {"sync": select_sync, "scalar": select_scalar, "vector": select_vector, "gpsimd": select_gpsimd, "tensor": select_tensor},
            }
            for kind, n, k in plan:
                if k > 0:
                    eng.wait_ge(stage_done, 5 * k)
                table[kind][which](eng, n)
                eng.drain().then_inc(stage_done, 1)

        block = ctx.enter_context(nc.Block())

        @block.sync
        def _(sp):
            sp.dma_start(X[:], x_dram).then_inc(x_in, 16)
            sp.dma_start(ident[:], a["ident"]).then_inc(x_in, 16)
            run(sp, "sync")
            sp.wait_ge(stage_done, 5 * len(stages))
            sp.dma_start(out_dram, X[:]).then_inc(x_out, 16)
            sp.wait_ge(x_out, 16)

        @block.scalar
        def _(s):
            run(s, "scalar")

        @block.vector
        def _(v):
            v.memset(mhalf[:], -0.5)
            v.wait_ge(x_in, 32)
            run(v, "vector")

        @block.gpsimd
        def _(g):
            run(g, "gpsimd")

        @block.tensor
        def _(pe):
            pe.wait_ge(x_in, 32)
            run(pe, "tensor")


def lay_out(i):
    P_ = 128
    c = np.ascontiguousarray
    a = {k: np.asarray(v) for k, v in i.items()}
    E, F2, D = a["L0_ffn_w1"].shape
    I = F2 // 2
    g = {}
    g["x"] = c(a["L0_attn_x"][0])
    w1 = np.concatenate([a["L0_ffn_w1"][:, 0::2], a["L0_ffn_w1"][:, 1::2]], axis=1)
    g["w1"] = c(w1.reshape(E, F2, D // P_, P_).transpose(3, 0, 2, 1))
    g["w2"] = c(a["L0_ffn_w2"].reshape(E, D, I // P_, P_).transpose(3, 0, 2, 1))
    b1 = np.concatenate([a["L0_ffn_b1"][:, 0::2], a["L0_ffn_b1"][:, 1::2]], axis=1)
    g["b1"] = c(b1.reshape(E, F2 // P_, P_).transpose(2, 0, 1))
    g["b2"] = c(a["L0_ffn_b2"])
    g["gate_w"] = c(a["L0_ffn_gate_w"].reshape(E, D // P_, P_).transpose(2, 1, 0))
    g["gate_b"] = c(a["L0_ffn_gate_b"].reshape(E, 1))
    for w in ("W1", "W3"):
        t = a[f"L1_ffn_{w}"]
        g[w] = c(t.T.reshape(D // P_, P_, t.shape[0]).transpose(1, 0, 2))
    t = a["L1_ffn_W2"]
    g["W2"] = c(t.T.reshape(t.shape[1] // P_, P_, D).transpose(1, 0, 2))
    T = g["x"].shape[0]
    NHEAD, HD, RD, LAT = 16, 16, 64, 64
    wqd, wkvd, wkr = a["L0_attn_Wqd"], a["L0_attn_Wkvd"], a["L0_attn_Wkr"]
    swap = np.r_[RD // 2:RD, 0:RD // 2]
    wp = np.stack([np.tile(w, (1, 2)) for w in (wqd, wkvd, wkr, wkr[:, swap])], axis=1)
    g["wp"] = c(wp.reshape(D // P_, P_, 4, P_).transpose(1, 0, 2, 3))
    g["wv"] = c(np.tile(a["L0_attn_Wvu"], (2, 1)))
    wqr = a["L0_attn_Wqr"].reshape(LAT, NHEAD, RD)
    wqu, wku = (a[f"L0_attn_{n}"].reshape(LAT, NHEAD, HD) for n in ("Wqu", "Wku"))
    wh = np.zeros((LAT, NHEAD, 4, P_), np.float32)
    wh[:, :, 0] = np.tile(wqr, (1, 1, 2))
    wh[:, :, 1] = np.tile(wqr[:, :, swap], (1, 1, 2))
    for k, w in ((2, wqu), (3, wku)):
        for at in (RD, RD + HD, RD + 3 * HD):
            wh[:, :, k, at:at + HD] = w
    g["whead"] = c(np.tile(wh.reshape(LAT, NHEAD, 4 * P_), (2, 1, 1)))
    wog = np.zeros((NHEAD // 4, 4, 2 * HD, D), np.float32)
    wog[:, :, 0:HD] = a["L0_attn_Wo"].reshape(NHEAD // 4, 4, HD, D)
    g["wog"] = c(wog.reshape(NHEAD // 4, P_, D))
    freqs = 1.0 / 10000.0 ** (np.arange(0, RD, 2, dtype=np.float32) / RD)
    ang = np.outer(np.arange(T, dtype=np.float32), freqs).T
    cos, sin = np.cos(ang), np.sin(ang)
    g["rope"] = c(np.stack([np.tile(cos, (4, 1)), np.tile(np.concatenate([-sin, sin]), (2, 1))], axis=1).astype(np.float32))
    upper = np.triu(np.full((P_, P_), -1e30, np.float32), 1)
    g["cmask"] = c(np.stack([upper, upper.T], axis=1))
    rowm = np.zeros((P_, 1), np.float32)
    rowm[RD + HD:RD + 2 * HD] = rowm[RD + 3 * HD:] = -1.0
    g["rowm"] = rowm
    k = np.arange(P_)
    g["spread"] = c((k[:, None] == (k[None, :] // (2 * HD)) * 2 * HD + HD).astype(np.float32))
    h = np.ones((1, 1), np.float32)
    while h.shape[0] < P_:
        h = np.block([[h, h], [h, -h]])
    g["hadamard"] = c(h)
    wi = np.concatenate([a["L1_attn_wq_idx"], a["L1_attn_wk_idx"]], axis=1)
    g["wi"] = c(wi.T.reshape(-1, P_, D).transpose(1, 0, 2))
    wkvi = np.concatenate([a["L1_attn_wk"], a["L1_attn_wv"], a["L1_attn_w_iw"]], axis=1)
    g["wkvi"] = c(wkvi.reshape(D // P_, P_, -1).transpose(1, 0, 2))
    g["imask"] = c(np.concatenate([np.zeros((P_, 3 * P_), np.float32), upper], axis=1))
    t = np.arange(P_)
    g["selt"] = c((t[:, None, None] == 4 * np.arange(P_ // 4)[None, None, :] + np.arange(4)[None, :, None]).astype(np.float32))
    wq = a["L1_attn_wq"].reshape(D // P_, P_, 16, P_).transpose(1, 2, 0, 3)
    g["swq"] = c(wq.reshape(P_, 2, -1))
    wo = a["L1_attn_wo"].reshape(16, P_, D).transpose(1, 0, 2)
    g["swo"] = c(wo)
    row = np.arange(8)
    m = np.zeros((8, P_ + 2 * 512), np.float32)
    m[:, 0:P_] = row[:, None] == np.arange(P_)[None, :] // 16
    pair, tok, rank = np.meshgrid(np.arange(4), np.arange(4), np.arange(32), indexing="ij")
    for r_ in row:
        own = tok == r_ % 4
        m[r_, P_:P_ + 512] = np.where(own & (rank <= 8 * pair + r_), 0, -1e30).reshape(-1)
        m[r_, P_ + 512:] = np.where(own, 0, -1e30).reshape(-1)
    g["smask"] = m
    g["ident"] = np.eye(P_, dtype=np.float32)
    g["iota_e"] = np.tile(np.arange(E, dtype=np.float32), (P_, 1))
    return g


def scratch(laid):
    T, E = laid["x"].shape[0], laid["b2"].shape[0]
    return {"we_scratch0": ((E, T), F32), "we_scratch1": ((E, T), F32), "kv_scratch": ((T, 256), F32)}


def kernel(**inputs):
    import concourse.bacc as bacc
    from concourse.bass_utils import run_bass_kernel_spmd

    nc = bacc.Bacc("TRN2", target_bir_lowering=False, num_devices=1)
    laid = lay_out(inputs)
    T, D = laid["x"].shape
    args = {n: nc.dram_tensor(f"in_{n}", v.shape, mybir.dt.from_np(v.dtype), kind="ExternalInput").ap()
            for n, v in laid.items()}
    for n, (shape, dt) in scratch(laid).items():
        args[n] = nc.dram_tensor(n, shape, dt, kind="Internal").ap()
    out = nc.dram_tensor("out", (T, D), F32, kind="ExternalOutput").ap()
    build(nc, args, out)
    r = run_bass_kernel_spmd(nc, [{f"in_{n}": v for n, v in laid.items()}], core_ids=[0])
    return r.results[0]["out"].reshape(1, T, D)
```
